# Optimizing a Trainium2 kernel written in Bass

```python
import numpy as np
import jax
import jax.numpy as jnp

def _softmax(x, axis=-1):
    return jax.nn.softmax(x, axis=axis)

def _gelu(x):
    return jax.nn.gelu(x, approximate=True)

def _silu(x):
    return jax.nn.silu(x)

def _sigmoid(x):
    return jax.nn.sigmoid(x)

def _layernorm(x, axis=-1, eps=1e-05):
    m = jnp.mean(x, axis=axis, keepdims=True)
    v = jnp.var(x, axis=axis, keepdims=True)
    return (x - m) / jnp.sqrt(v + eps)

def _scatter_add(tgt, idx, src, axis=0):
    return tgt.at[idx].add(src)

def _segment_sum(src, seg, n):
    return jax.ops.segment_sum(src, seg, n)
kernel_name = 'mk_xattn_seq_d4_seqx_r8_4fb54e'

def setup_inputs(seed: int=0):
    np.random.seed(seed)
    _w = jnp.asarray

    def _rec_inputs():
        import jax
        import jax.numpy as jnp
        _rk = jax.random.key(seed)
        x = -0.0003929 + 0.9999 * jax.random.normal(jax.random.fold_in(_rk, 1), (16, 128, 256), jnp.float32)
        _lenS = 128 - jax.random.randint(jax.random.fold_in(_rk, 7), (16,), 0, max(1, 128 // 4) + 1, jnp.int32)
        _lenS2 = 128 - jax.random.randint(jax.random.fold_in(_rk, 8), (16,), 0, max(1, 128 // 4) + 1, jnp.int32)
        _ctx_2048P = jax.random.normal(jax.random.fold_in(_rk, 11), (16, 16, 256), jnp.float32)
        _ctx_2048c = jax.random.dirichlet(jax.random.fold_in(_rk, 511), 0.3 * jnp.ones((16,), jnp.float32), (16, 128))
        _ctx_2048t = jnp.einsum('bsk,bkd->bsd', _ctx_2048c, _ctx_2048P)
        _ctx_2048t = _ctx_2048t * jax.lax.rsqrt(jnp.mean(jnp.square(_ctx_2048t)) + 1e-12) * 0.953939
        ctx_2048 = 2.81802e-05 + 1.00001 * (_ctx_2048t + 0.3 * jax.random.normal(jax.random.fold_in(_rk, 611), (16, 128, 256), jnp.float32))
        _validS = jnp.arange(128)[None, :] < _lenS[:, None]
        _validS2 = jnp.arange(128)[None, :] < _lenS2[:, None]
        _causal = jnp.tril(jnp.ones((128, 128), dtype=bool))
        mask_BxS2_ik0 = jnp.where(jnp.broadcast_to(_validS2[:, :], (16, 128)), 0, 1).astype(jnp.int32)
        mask_1x1xSxS2_fc1 = jnp.where(jnp.broadcast_to(_validS2[0:1, None, None, :], (1, 1, 128, 128)), 1.0, 0.0).astype(jnp.float32)
        mask_Bx1xSxS2_ff1 = jnp.where(jnp.ones((16, 1, 128, 128), dtype=bool), 1.0, 0.0).astype(jnp.float32)
        return (x, ctx_2048, mask_BxS2_ik0, mask_1x1xSxS2_fc1, mask_Bx1xSxS2_ff1)
    x, ctx_2048, mask_BxS2_ik0, mask_1x1xSxS2_fc1, mask_Bx1xSxS2_ff1 = _rec_inputs()

    def _L0_xattn_setup():
        import jax, jax.numpy as jnp
        import numpy as np
        B, C1, C2, N = (8, 128, 128, 256)
        D = C2 // 8
        key = jax.random.key(seed)
        ks = jax.random.split(key, 8)
        s1 = 1.0 / np.sqrt(C1)
        s2 = 1.0 / np.sqrt(C2)
        return {'x1': jax.random.normal(ks[0], (B, C1, N), jnp.float32), 'x2': jax.random.normal(ks[1], (B, C2, N), jnp.float32), 'Wq': jax.random.uniform(ks[2], (D, C1), jnp.float32, -s1, s1), 'bq': jax.random.uniform(ks[3], (D,), jnp.float32, -s1, s1), 'Wk': jax.random.uniform(ks[4], (D, C2), jnp.float32, -s2, s2), 'bk': jax.random.uniform(ks[5], (D,), jnp.float32, -s2, s2), 'Wv': jax.random.uniform(ks[6], (C1, C2), jnp.float32, -s2, s2), 'bv': jax.random.uniform(ks[7], (C1,), jnp.float32, -s2, s2)}
    _L0_xattn_all = _L0_xattn_setup()
    _L0_xattn_in = {k: v for k, v in _L0_xattn_all.items() if k in ('Wq', 'bq', 'Wk', 'bk', 'Wv', 'bv')}
    del _L0_xattn_all

    def _L1_xattn_setup():
        import jax, jax.numpy as jnp
        import numpy as np
        B, P, K, H, NH = (4, 256, 32, 256, 16)
        DH = H // NH
        EPS = 1e-06

        def rmsnorm(x, w):
            var = jnp.mean(jnp.square(x), axis=-1, keepdims=True)
            return x * jax.lax.rsqrt(var + EPS) * w
        key = jax.random.key(seed)
        ks = jax.random.split(key, 12)
        s = 0.02
        return {'x': jax.random.normal(ks[0], (B, P, H), jnp.float32), 'latents': jax.random.normal(ks[1], (B, K, H), jnp.float32), 'attention_mask': jax.random.randint(ks[2], (B, P), 0, 2, jnp.int32), 'q_w': s * jax.random.normal(ks[3], (H, H), jnp.float32), 'q_b': jnp.zeros((H,), jnp.float32), 'kv_w': s * jax.random.normal(ks[4], (H, 2 * H), jnp.float32), 'kv_b': jnp.zeros((2 * H,), jnp.float32), 'out_w': s * jax.random.normal(ks[5], (H, H), jnp.float32), 'out_b': jnp.zeros((H,), jnp.float32), 'postnorm_w': jnp.ones((H,), jnp.float32), 'mlp_w1': s * jax.random.normal(ks[6], (H, 4 * H), jnp.float32), 'mlp_b1': jnp.zeros((4 * H,), jnp.float32), 'mlp_w2': s * jax.random.normal(ks[7], (4 * H, H), jnp.float32), 'mlp_b2': jnp.zeros((H,), jnp.float32)}
    _L1_xattn_all = _L1_xattn_setup()
    _L1_xattn_in = {k: v for k, v in _L1_xattn_all.items() if k in ('q_w', 'q_b', 'kv_w', 'kv_b', 'out_w', 'out_b', 'postnorm_w', 'mlp_w1', 'mlp_b1', 'mlp_w2', 'mlp_b2')}
    del _L1_xattn_all

    def _L2_xattn_setup():
        import jax, jax.numpy as jnp
        import numpy as np
        B, Q, S1, S2 = (4, 32, 256, 256)
        D, H, K, F = (256, 16, 128, 1024)
        LN_EPS = 1e-05

        def _layer_norm(x, scale, offset):
            mu = jnp.mean(x, axis=-1, keepdims=True)
            var = jnp.var(x, axis=-1, keepdims=True)
            return (x - mu) * jax.lax.rsqrt(var + LN_EPS) * scale + offset

        def _cross_attention(q_in, kv_in, wq, bq, wk, bk, wv, bv, wo, bo, bias_k, bias_v):
            b, q_len, _ = q_in.shape
            t = kv_in.shape[1]
            qh = (q_in @ wq + bq).reshape(b, q_len, H, K)
            kh = (kv_in @ wk + bk).reshape(b, t, H, K)
            vh = (kv_in @ wv + bv).reshape(b, t, H, K)
            kh = jnp.concatenate([kh, jnp.broadcast_to(bias_k, (b, 1, H, K))], axis=1)
            vh = jnp.concatenate([vh, jnp.broadcast_to(bias_v, (b, 1, H, K))], axis=1)
            scale = jnp.sqrt(jnp.asarray(K, q_in.dtype))
            logits = jnp.einsum('bqhk,bthk->bhqt', qh, kh) / scale
            weights = jax.nn.softmax(logits, axis=-1)
            ctx = jnp.einsum('bhqt,bthk->bqhk', weights, vh).reshape(b, q_len, H * K)
            return ctx @ wo + bo

        def _forward(x, xf_1, xf_2, ln1_scale, ln1_offset, wq1, bq1, wk1, bk1, wv1, bv1, wo1, bo1, bias_k1, bias_v1, ln2_scale, ln2_offset, wq2, bq2, wk2, bk2, wv2, bv2, wo2, bo2, bias_k2, bias_v2, ln_mlp_scale, ln_mlp_offset, w_fc1, b_fc1, w_fc2, b_fc2):
            res = x
            h = _layer_norm(x, ln1_scale, ln1_offset)
            x = res + _cross_attention(h, xf_1, wq1, bq1, wk1, bk1, wv1, bv1, wo1, bo1, bias_k1, bias_v1)
            res = x
            h = _layer_norm(x, ln2_scale, ln2_offset)
            x = res + _cross_attention(h, xf_2, wq2, bq2, wk2, bk2, wv2, bv2, wo2, bo2, bias_k2, bias_v2)
            h = _layer_norm(x, ln_mlp_scale, ln_mlp_offset)
            h = jax.nn.gelu(h @ w_fc1 + b_fc1, approximate=False) @ w_fc2 + b_fc2
            return x + h
        key = jax.random.key(seed)
        ks = iter(jax.random.split(key, 64))

        def rn(shape, s=0.02):
            return jax.random.normal(next(ks), shape, jnp.float32) * s
        inp = {'x': rn((B, Q, D), 1.0), 'xf_1': rn((B, S1, D), 1.0), 'xf_2': rn((B, S2, D), 1.0)}
        for i in (1, 2):
            inp[f'ln{i}_scale'] = jnp.ones((D,), jnp.float32)
            inp[f'ln{i}_offset'] = jnp.zeros((D,), jnp.float32)
            inp[f'wq{i}'] = rn((D, H * K))
            inp[f'bq{i}'] = jnp.zeros((H * K,), jnp.float32)
            inp[f'wk{i}'] = rn((D, H * K))
            inp[f'bk{i}'] = jnp.zeros((H * K,), jnp.float32)
            inp[f'wv{i}'] = rn((D, H * K))
            inp[f'bv{i}'] = jnp.zeros((H * K,), jnp.float32)
            inp[f'wo{i}'] = rn((H * K, D))
            inp[f'bo{i}'] = jnp.zeros((D,), jnp.float32)
            inp[f'bias_k{i}'] = rn((1, 1, H, K))
            inp[f'bias_v{i}'] = rn((1, 1, H, K))
        inp['ln_mlp_scale'] = jnp.ones((D,), jnp.float32)
        inp['ln_mlp_offset'] = jnp.zeros((D,), jnp.float32)
        inp['w_fc1'] = rn((D, F))
        inp['b_fc1'] = jnp.zeros((F,), jnp.float32)
        inp['w_fc2'] = rn((F, D))
        inp['b_fc2'] = jnp.zeros((D,), jnp.float32)
        return inp
    _L2_xattn_all = _L2_xattn_setup()
    _L2_xattn_in = {k: v for k, v in _L2_xattn_all.items() if k in ('ln1_scale', 'ln1_offset', 'wq1', 'bq1', 'wk1', 'bk1', 'wv1', 'bv1', 'wo1', 'bo1', 'bias_k1', 'bias_v1', 'ln2_scale', 'ln2_offset', 'wq2', 'bq2', 'wk2', 'bk2', 'wv2', 'bv2', 'wo2', 'bo2', 'bias_k2', 'bias_v2', 'ln_mlp_scale', 'ln_mlp_offset', 'w_fc1', 'b_fc1', 'w_fc2', 'b_fc2')}
    del _L2_xattn_all

    def _L3_xattn_setup():
        import jax, jax.numpy as jnp
        import numpy as np
        H = 256
        NH = 16
        HD = H // NH
        EPS = 1e-05

        def gelu(x):
            return 0.5 * x * (1.0 + jnp.tanh(0.7978845608028654 * x * (1.0 + 0.044715 * x * x)))

        def layernorm(x, scale, bias):
            m = jnp.mean(x, axis=-1, keepdims=True)
            v = jnp.mean(jnp.square(x - m), axis=-1, keepdims=True)
            return (x - m) * jax.lax.rsqrt(v + EPS) * scale + bias

        def split_heads(x):
            b, s, _ = x.shape
            return x.reshape(b, s, NH, HD).transpose(0, 2, 1, 3)

        def merge_heads(x):
            b, nh, s, hd = x.shape
            return x.transpose(0, 2, 1, 3).reshape(b, s, nh * hd)

        def attention(q, k, v, mask):
            scores = jnp.einsum('bhqd,bhkd->bhqk', q, k) / jnp.sqrt(jnp.float32(HD))
            scores = scores * mask - 10000.0 * (1.0 - mask)
            probs = jax.nn.softmax(scores, axis=-1)
            return jnp.einsum('bhqk,bhkd->bhqd', probs, v)
        key = jax.random.key(seed)
        ks = jax.random.split(key, 16)
        b, s, t = (2, 128, 128)
        w = lambda k, i, o: jax.random.normal(k, (i, o), jnp.float32) * 0.02
        inp = {'hidden_states': jax.random.normal(ks[0], (b, s, H), jnp.float32), 'encoder_states': jax.random.normal(ks[1], (b, t, H), jnp.float32), 'ltor_mask': jnp.tril(jnp.ones((1, 1, s, s), jnp.float32)), 'cross_mask': jnp.ones((b, 1, s, t), jnp.float32), 'ln1_s': jnp.ones((H,), jnp.float32), 'ln1_b': jnp.zeros((H,), jnp.float32), 'w_qkv': w(ks[2], H, 3 * H), 'b_qkv': jnp.zeros((3 * H,), jnp.float32), 'w_ao': w(ks[3], H, H), 'b_ao': jnp.zeros((H,), jnp.float32), 'ln2_s': jnp.ones((H,), jnp.float32), 'ln2_b': jnp.zeros((H,), jnp.float32), 'w_q': w(ks[4], H, H), 'b_q': jnp.zeros((H,), jnp.float32), 'w_kv': w(ks[5], H, 2 * H), 'b_kv': jnp.zeros((2 * H,), jnp.float32), 'w_co': w(ks[6], H, H), 'b_co': jnp.zeros((H,), jnp.float32), 'ln3_s': jnp.ones((H,), jnp.float32), 'ln3_b': jnp.zeros((H,), jnp.float32), 'w1': w(ks[7], H, 4 * H), 'b1': jnp.zeros((4 * H,), jnp.float32), 'w2': w(ks[8], 4 * H, H), 'b2': jnp.zeros((H,), jnp.float32)}
        return inp
    _L3_xattn_all = _L3_xattn_setup()
    _L3_xattn_in = {k: v for k, v in _L3_xattn_all.items() if k in ('ln1_s', 'ln1_b', 'w_qkv', 'b_qkv', 'w_ao', 'b_ao', 'ln2_s', 'ln2_b', 'w_q', 'b_q', 'w_kv', 'b_kv', 'w_co', 'b_co', 'ln3_s', 'ln3_b', 'w1', 'b1', 'w2', 'b2')}
    del _L3_xattn_all
    return {'x': x, 'ctx_2048': ctx_2048, 'mask_BxS2_ik0': mask_BxS2_ik0, 'mask_1x1xSxS2_fc1': mask_1x1xSxS2_fc1, 'mask_Bx1xSxS2_ff1': mask_Bx1xSxS2_ff1, 'L0_xattn_Wq': _L0_xattn_in['Wq'], 'L0_xattn_bq': _L0_xattn_in['bq'], 'L0_xattn_Wk': _L0_xattn_in['Wk'], 'L0_xattn_bk': _L0_xattn_in['bk'], 'L0_xattn_Wv': _L0_xattn_in['Wv'], 'L0_xattn_bv': _L0_xattn_in['bv'], 'L1_xattn_q_w': _L1_xattn_in['q_w'], 'L1_xattn_q_b': _L1_xattn_in['q_b'], 'L1_xattn_kv_w': _L1_xattn_in['kv_w'], 'L1_xattn_kv_b': _L1_xattn_in['kv_b'], 'L1_xattn_out_w': _L1_xattn_in['out_w'], 'L1_xattn_out_b': _L1_xattn_in['out_b'], 'L1_xattn_postnorm_w': _L1_xattn_in['postnorm_w'], 'L1_xattn_mlp_w1': _L1_xattn_in['mlp_w1'], 'L1_xattn_mlp_b1': _L1_xattn_in['mlp_b1'], 'L1_xattn_mlp_w2': _L1_xattn_in['mlp_w2'], 'L1_xattn_mlp_b2': _L1_xattn_in['mlp_b2'], 'L2_xattn_ln1_scale': _L2_xattn_in['ln1_scale'], 'L2_xattn_ln1_offset': _L2_xattn_in['ln1_offset'], 'L2_xattn_wq1': _L2_xattn_in['wq1'], 'L2_xattn_bq1': _L2_xattn_in['bq1'], 'L2_xattn_wk1': _L2_xattn_in['wk1'], 'L2_xattn_bk1': _L2_xattn_in['bk1'], 'L2_xattn_wv1': _L2_xattn_in['wv1'], 'L2_xattn_bv1': _L2_xattn_in['bv1'], 'L2_xattn_wo1': _L2_xattn_in['wo1'], 'L2_xattn_bo1': _L2_xattn_in['bo1'], 'L2_xattn_bias_k1': _L2_xattn_in['bias_k1'], 'L2_xattn_bias_v1': _L2_xattn_in['bias_v1'], 'L2_xattn_ln2_scale': _L2_xattn_in['ln2_scale'], 'L2_xattn_ln2_offset': _L2_xattn_in['ln2_offset'], 'L2_xattn_wq2': _L2_xattn_in['wq2'], 'L2_xattn_bq2': _L2_xattn_in['bq2'], 'L2_xattn_wk2': _L2_xattn_in['wk2'], 'L2_xattn_bk2': _L2_xattn_in['bk2'], 'L2_xattn_wv2': _L2_xattn_in['wv2'], 'L2_xattn_bv2': _L2_xattn_in['bv2'], 'L2_xattn_wo2': _L2_xattn_in['wo2'], 'L2_xattn_bo2': _L2_xattn_in['bo2'], 'L2_xattn_bias_k2': _L2_xattn_in['bias_k2'], 'L2_xattn_bias_v2': _L2_xattn_in['bias_v2'], 'L2_xattn_ln_mlp_scale': _L2_xattn_in['ln_mlp_scale'], 'L2_xattn_ln_mlp_offset': _L2_xattn_in['ln_mlp_offset'], 'L2_xattn_w_fc1': _L2_xattn_in['w_fc1'], 'L2_xattn_b_fc1': _L2_xattn_in['b_fc1'], 'L2_xattn_w_fc2': _L2_xattn_in['w_fc2'], 'L2_xattn_b_fc2': _L2_xattn_in['b_fc2'], 'L3_xattn_ln1_s': _L3_xattn_in['ln1_s'], 'L3_xattn_ln1_b': _L3_xattn_in['ln1_b'], 'L3_xattn_w_qkv': _L3_xattn_in['w_qkv'], 'L3_xattn_b_qkv': _L3_xattn_in['b_qkv'], 'L3_xattn_w_ao': _L3_xattn_in['w_ao'], 'L3_xattn_b_ao': _L3_xattn_in['b_ao'], 'L3_xattn_ln2_s': _L3_xattn_in['ln2_s'], 'L3_xattn_ln2_b': _L3_xattn_in['ln2_b'], 'L3_xattn_w_q': _L3_xattn_in['w_q'], 'L3_xattn_b_q': _L3_xattn_in['b_q'], 'L3_xattn_w_kv': _L3_xattn_in['w_kv'], 'L3_xattn_b_kv': _L3_xattn_in['b_kv'], 'L3_xattn_w_co': _L3_xattn_in['w_co'], 'L3_xattn_b_co': _L3_xattn_in['b_co'], 'L3_xattn_ln3_s': _L3_xattn_in['ln3_s'], 'L3_xattn_ln3_b': _L3_xattn_in['ln3_b'], 'L3_xattn_w1': _L3_xattn_in['w1'], 'L3_xattn_b1': _L3_xattn_in['b1'], 'L3_xattn_w2': _L3_xattn_in['w2'], 'L3_xattn_b2': _L3_xattn_in['b2']}

def reference(x, ctx_2048, mask_BxS2_ik0, mask_1x1xSxS2_fc1, mask_Bx1xSxS2_ff1, L0_xattn_Wq, L0_xattn_bq, L0_xattn_Wk, L0_xattn_bk, L0_xattn_Wv, L0_xattn_bv, L1_xattn_q_w, L1_xattn_q_b, L1_xattn_kv_w, L1_xattn_kv_b, L1_xattn_out_w, L1_xattn_out_b, L1_xattn_postnorm_w, L1_xattn_mlp_w1, L1_xattn_mlp_b1, L1_xattn_mlp_w2, L1_xattn_mlp_b2, L2_xattn_ln1_scale, L2_xattn_ln1_offset, L2_xattn_wq1, L2_xattn_bq1, L2_xattn_wk1, L2_xattn_bk1, L2_xattn_wv1, L2_xattn_bv1, L2_xattn_wo1, L2_xattn_bo1, L2_xattn_bias_k1, L2_xattn_bias_v1, L2_xattn_ln2_scale, L2_xattn_ln2_offset, L2_xattn_wq2, L2_xattn_bq2, L2_xattn_wk2, L2_xattn_bk2, L2_xattn_wv2, L2_xattn_bv2, L2_xattn_wo2, L2_xattn_bo2, L2_xattn_bias_k2, L2_xattn_bias_v2, L2_xattn_ln_mlp_scale, L2_xattn_ln_mlp_offset, L2_xattn_w_fc1, L2_xattn_b_fc1, L2_xattn_w_fc2, L2_xattn_b_fc2, L3_xattn_ln1_s, L3_xattn_ln1_b, L3_xattn_w_qkv, L3_xattn_b_qkv, L3_xattn_w_ao, L3_xattn_b_ao, L3_xattn_ln2_s, L3_xattn_ln2_b, L3_xattn_w_q, L3_xattn_b_q, L3_xattn_w_kv, L3_xattn_b_kv, L3_xattn_w_co, L3_xattn_b_co, L3_xattn_ln3_s, L3_xattn_ln3_b, L3_xattn_w1, L3_xattn_b1, L3_xattn_w2, L3_xattn_b2):
    import jax
    import jax.numpy as jnp

    def _L0_xattn_ref(x1, x2, Wq, bq, Wk, bk, Wv, bv):
        import jax, jax.numpy as jnp
        import numpy as np
        B, C1, C2, N = (8, 128, 128, 256)
        D = C2 // 8
        q = jnp.einsum('bcn,dc->bnd', x1, Wq) + bq
        k = jnp.einsum('bcn,dc->bdn', x2, Wk) + bk[:, None]
        v = jnp.einsum('bcn,dc->bdn', x2, Wv) + bv[:, None]
        attn = jax.nn.softmax(jnp.einsum('bnd,bdm->bnm', q, k), axis=2)
        attn_out = jnp.einsum('bcm,bnm->bcn', v, attn)
        return attn_out + x1

    def _L1_xattn_ref(x, latents, attention_mask, q_w, q_b, kv_w, kv_b, out_w, out_b, postnorm_w, mlp_w1, mlp_b1, mlp_w2, mlp_b2):
        import jax, jax.numpy as jnp
        import numpy as np
        B, P, K, H, NH = (4, 256, 32, 256, 16)
        DH = H // NH
        EPS = 1e-06

        def rmsnorm(x, w):
            var = jnp.mean(jnp.square(x), axis=-1, keepdims=True)
            return x * jax.lax.rsqrt(var + EPS) * w
        b, p, _ = x.shape
        k_len = latents.shape[1]
        residual = latents
        h = jnp.concatenate([x, latents], axis=1)
        q = (latents @ q_w + q_b).reshape(b, k_len, NH, DH)
        kv = (h @ kv_w + kv_b).reshape(b, p + k_len, NH, DH, 2)
        kmat, v = (kv[..., 0], kv[..., 1])
        attn = jnp.einsum('bkhd,bnhd->bhkn', q, kmat) / DH
        full_mask = jnp.concatenate([attention_mask.astype(bool), jnp.ones((b, k_len), bool)], axis=-1)
        attn = jnp.where(full_mask[:, None, None, :], attn, -jnp.inf)
        attn = jax.nn.softmax(attn.astype(jnp.float32), axis=-1).astype(q.dtype)
        attn_out = jnp.einsum('bhkn,bnhd->bkhd', attn, v).reshape(b, k_len, H)
        attn_out = attn_out @ out_w + out_b + residual
        out = rmsnorm(attn_out, postnorm_w)
        out = jax.nn.gelu(out @ mlp_w1 + mlp_b1) @ mlp_w2 + mlp_b2
        return out + residual

    def _L2_xattn_ref(x, xf_1, xf_2, ln1_scale, ln1_offset, wq1, bq1, wk1, bk1, wv1, bv1, wo1, bo1, bias_k1, bias_v1, ln2_scale, ln2_offset, wq2, bq2, wk2, bk2, wv2, bv2, wo2, bo2, bias_k2, bias_v2, ln_mlp_scale, ln_mlp_offset, w_fc1, b_fc1, w_fc2, b_fc2):
        import jax, jax.numpy as jnp
        import numpy as np
        B, Q, S1, S2 = (4, 32, 256, 256)
        D, H, K, F = (256, 16, 128, 1024)
        LN_EPS = 1e-05

        def _layer_norm(x, scale, offset):
            mu = jnp.mean(x, axis=-1, keepdims=True)
            var = jnp.var(x, axis=-1, keepdims=True)
            return (x - mu) * jax.lax.rsqrt(var + LN_EPS) * scale + offset

        def _cross_attention(q_in, kv_in, wq, bq, wk, bk, wv, bv, wo, bo, bias_k, bias_v):
            b, q_len, _ = q_in.shape
            t = kv_in.shape[1]
            qh = (q_in @ wq + bq).reshape(b, q_len, H, K)
            kh = (kv_in @ wk + bk).reshape(b, t, H, K)
            vh = (kv_in @ wv + bv).reshape(b, t, H, K)
            kh = jnp.concatenate([kh, jnp.broadcast_to(bias_k, (b, 1, H, K))], axis=1)
            vh = jnp.concatenate([vh, jnp.broadcast_to(bias_v, (b, 1, H, K))], axis=1)
            scale = jnp.sqrt(jnp.asarray(K, q_in.dtype))
            logits = jnp.einsum('bqhk,bthk->bhqt', qh, kh) / scale
            weights = jax.nn.softmax(logits, axis=-1)
            ctx = jnp.einsum('bhqt,bthk->bqhk', weights, vh).reshape(b, q_len, H * K)
            return ctx @ wo + bo

        def _forward(x, xf_1, xf_2, ln1_scale, ln1_offset, wq1, bq1, wk1, bk1, wv1, bv1, wo1, bo1, bias_k1, bias_v1, ln2_scale, ln2_offset, wq2, bq2, wk2, bk2, wv2, bv2, wo2, bo2, bias_k2, bias_v2, ln_mlp_scale, ln_mlp_offset, w_fc1, b_fc1, w_fc2, b_fc2):
            res = x
            h = _layer_norm(x, ln1_scale, ln1_offset)
            x = res + _cross_attention(h, xf_1, wq1, bq1, wk1, bk1, wv1, bv1, wo1, bo1, bias_k1, bias_v1)
            res = x
            h = _layer_norm(x, ln2_scale, ln2_offset)
            x = res + _cross_attention(h, xf_2, wq2, bq2, wk2, bk2, wv2, bv2, wo2, bo2, bias_k2, bias_v2)
            h = _layer_norm(x, ln_mlp_scale, ln_mlp_offset)
            h = jax.nn.gelu(h @ w_fc1 + b_fc1, approximate=False) @ w_fc2 + b_fc2
            return x + h
        return _forward(x, xf_1, xf_2, ln1_scale, ln1_offset, wq1, bq1, wk1, bk1, wv1, bv1, wo1, bo1, bias_k1, bias_v1, ln2_scale, ln2_offset, wq2, bq2, wk2, bk2, wv2, bv2, wo2, bo2, bias_k2, bias_v2, ln_mlp_scale, ln_mlp_offset, w_fc1, b_fc1, w_fc2, b_fc2)

    def _L3_xattn_ref(hidden_states, encoder_states, ltor_mask, cross_mask, ln1_s, ln1_b, w_qkv, b_qkv, w_ao, b_ao, ln2_s, ln2_b, w_q, b_q, w_kv, b_kv, w_co, b_co, ln3_s, ln3_b, w1, b1, w2, b2):
        import jax, jax.numpy as jnp
        import numpy as np
        H = 256
        NH = 16
        HD = H // NH
        EPS = 1e-05

        def gelu(x):
            return 0.5 * x * (1.0 + jnp.tanh(0.7978845608028654 * x * (1.0 + 0.044715 * x * x)))

        def layernorm(x, scale, bias):
            m = jnp.mean(x, axis=-1, keepdims=True)
            v = jnp.mean(jnp.square(x - m), axis=-1, keepdims=True)
            return (x - m) * jax.lax.rsqrt(v + EPS) * scale + bias

        def split_heads(x):
            b, s, _ = x.shape
            return x.reshape(b, s, NH, HD).transpose(0, 2, 1, 3)

        def merge_heads(x):
            b, nh, s, hd = x.shape
            return x.transpose(0, 2, 1, 3).reshape(b, s, nh * hd)

        def attention(q, k, v, mask):
            scores = jnp.einsum('bhqd,bhkd->bhqk', q, k) / jnp.sqrt(jnp.float32(HD))
            scores = scores * mask - 10000.0 * (1.0 - mask)
            probs = jax.nn.softmax(scores, axis=-1)
            return jnp.einsum('bhqk,bhkd->bhqd', probs, v)
        ln_out = layernorm(hidden_states, ln1_s, ln1_b)
        qkv = ln_out @ w_qkv + b_qkv
        q, k, v = jnp.split(qkv, 3, axis=-1)
        ctx = merge_heads(attention(split_heads(q), split_heads(k), split_heads(v), ltor_mask))
        attn_out = ctx @ w_ao + b_ao
        x = hidden_states + attn_out
        ln_out = layernorm(x, ln2_s, ln2_b)
        q = ln_out @ w_q + b_q
        kv = encoder_states @ w_kv + b_kv
        k, v = jnp.split(kv, 2, axis=-1)
        ctx = merge_heads(attention(split_heads(q), split_heads(k), split_heads(v), cross_mask))
        cross_out = ctx @ w_co + b_co
        x = x + cross_out
        ln_out = layernorm(x, ln3_s, ln3_b)
        mlp_out = gelu(ln_out @ w1 + b1) @ w2 + b2
        return x + mlp_out
    x = _L0_xattn_ref(x, ctx_2048, L0_xattn_Wq, L0_xattn_bq, L0_xattn_Wk, L0_xattn_bk, L0_xattn_Wv, L0_xattn_bv)
    x = _L1_xattn_ref(ctx_2048, x, mask_BxS2_ik0, L1_xattn_q_w, L1_xattn_q_b, L1_xattn_kv_w, L1_xattn_kv_b, L1_xattn_out_w, L1_xattn_out_b, L1_xattn_postnorm_w, L1_xattn_mlp_w1, L1_xattn_mlp_b1, L1_xattn_mlp_w2, L1_xattn_mlp_b2)
    x = _L2_xattn_ref(x, ctx_2048, ctx_2048, L2_xattn_ln1_scale, L2_xattn_ln1_offset, L2_xattn_wq1, L2_xattn_bq1, L2_xattn_wk1, L2_xattn_bk1, L2_xattn_wv1, L2_xattn_bv1, L2_xattn_wo1, L2_xattn_bo1, L2_xattn_bias_k1, L2_xattn_bias_v1, L2_xattn_ln2_scale, L2_xattn_ln2_offset, L2_xattn_wq2, L2_xattn_bq2, L2_xattn_wk2, L2_xattn_bk2, L2_xattn_wv2, L2_xattn_bv2, L2_xattn_wo2, L2_xattn_bo2, L2_xattn_bias_k2, L2_xattn_bias_v2, L2_xattn_ln_mlp_scale, L2_xattn_ln_mlp_offset, L2_xattn_w_fc1, L2_xattn_b_fc1, L2_xattn_w_fc2, L2_xattn_b_fc2)
    x = _L3_xattn_ref(x, ctx_2048, mask_1x1xSxS2_fc1, mask_Bx1xSxS2_ff1, L3_xattn_ln1_s, L3_xattn_ln1_b, L3_xattn_w_qkv, L3_xattn_b_qkv, L3_xattn_w_ao, L3_xattn_b_ao, L3_xattn_ln2_s, L3_xattn_ln2_b, L3_xattn_w_q, L3_xattn_b_q, L3_xattn_w_kv, L3_xattn_b_kv, L3_xattn_w_co, L3_xattn_b_co, L3_xattn_ln3_s, L3_xattn_ln3_b, L3_xattn_w1, L3_xattn_b1, L3_xattn_w2, L3_xattn_b2)
    return x

_drawn_inputs = setup_inputs


def setup_inputs(seed=0):
    import zlib

    import numpy as np

    out = dict(_drawn_inputs(seed))
    spreads = {'L1_xattn_q_b': (0.0, 0.8),
     'L1_xattn_kv_b': (0.0, 0.8),
     'L1_xattn_out_b': (0.0, 0.8),
     'L1_xattn_postnorm_w': (1.0, 0.6),
     'L1_xattn_mlp_b1': (0.0, 0.1),
     'L1_xattn_mlp_b2': (0.0, 0.1),
     'L2_xattn_ln1_scale': (1.0, 0.6),
     'L2_xattn_ln1_offset': (0.0, 0.8),
     'L2_xattn_bq1': (0.0, 0.8),
     'L2_xattn_bk1': (0.0, 2.0),
     'L2_xattn_bv1': (0.0, 0.1),
     'L2_xattn_bo1': (0.0, 0.1),
     'L2_xattn_ln2_scale': (1.0, 0.6),
     'L2_xattn_ln2_offset': (0.0, 0.8),
     'L2_xattn_bq2': (0.0, 0.8),
     'L2_xattn_bk2': (0.0, 2.0),
     'L2_xattn_bv2': (0.0, 0.1),
     'L2_xattn_bo2': (0.0, 0.1),
     'L2_xattn_ln_mlp_scale': (1.0, 0.6),
     'L2_xattn_ln_mlp_offset': (0.0, 0.8),
     'L2_xattn_b_fc1': (0.0, 0.1),
     'L2_xattn_b_fc2': (0.0, 0.1),
     'L3_xattn_ln1_s': (1.0, 0.6),
     'L3_xattn_ln1_b': (0.0, 0.8),
     'L3_xattn_b_qkv': (0.0, 0.283),
     'L3_xattn_b_ao': (0.0, 0.1),
     'L3_xattn_ln2_s': (1.0, 0.6),
     'L3_xattn_ln2_b': (0.0, 2.0),
     'L3_xattn_b_q': (0.0, 2.0),
     'L3_xattn_b_kv': (0.0, 0.289),
     'L3_xattn_b_co': (0.0, 0.1),
     'L3_xattn_ln3_s': (1.0, 0.6),
     'L3_xattn_ln3_b': (0.0, 0.744),
     'L3_xattn_b1': (0.0, 0.1),
     'L3_xattn_b2': (0.0, 0.1)}
    factors = {'L0_xattn_bq': 2.914,
     'L0_xattn_bk': 64.0,
     'L1_xattn_q_w': 8.0,
     'L1_xattn_kv_w': 8.0,
     'L1_xattn_out_w': 8.0,
     'L2_xattn_wq1': 8.0,
     'L2_xattn_wk1': 8.0,
     'L2_xattn_bias_k1': 64.0,
     'L2_xattn_bias_v1': 64.0,
     'L2_xattn_wq2': 8.0,
     'L2_xattn_wk2': 8.0,
     'L2_xattn_bias_k2': 64.0,
     'L2_xattn_bias_v2': 64.0,
     'L3_xattn_w_q': 8.0}
    for name, (base, spread) in spreads.items():
        noise = np.random.default_rng([zlib.crc32(name.encode()), seed]).standard_normal(out[name].shape)
        drawn = base * np.exp(spread * noise) if base else spread * noise
        out[name] = jnp.asarray(drawn.astype(out[name].dtype))
    for name, factor in factors.items():
        out[name] = (out[name] * factor).astype(out[name].dtype)
    return out
```

```python
from contextlib import ExitStack

import concourse.bass as bass
from concourse import mybir

F32 = mybir.dt.float32
F32R = mybir.dt.float32r
I32 = mybir.dt.int32
ALU = mybir.AluOpType
ACT = mybir.ActivationFunctionType
AX = mybir.AxisListType

P = 128
B, S, D = 16, 128, 256
DC = D // P
GB = 4
G = B // GB
T = GB * S
D0 = 16
NH, DH = 16, 16
HPT = P // DH
QH = 4
H2, K2 = 16, 128
HG = 4
F = 1024
FC = F // P
NEG = -1.0e30


COLUMNS = {"L1_xattn_q_b": 2, "L1_kv_b_k": 2, "L1_kv_b_v": 2, "L1_xattn_postnorm_w": 2, "L1_xattn_mlp_b1": 8}
for _i in "12":
    COLUMNS.update({f"L2_xattn_ln{_i}_scale": 2, f"L2_xattn_ln{_i}_offset": 2, f"L2_xattn_bq{_i}": 16,
                    f"L2_xattn_bk{_i}": 16, f"L2_xattn_bv{_i}": 16, f"L2_xattn_bias_k{_i}": 16,
                    f"L2_xattn_bias_v{_i}": 16})
COLUMNS.update({"L2_xattn_ln_mlp_scale": 2, "L2_xattn_ln_mlp_offset": 2, "L2_xattn_b_fc1": 8})
COLUMNS.update({f"L3_xattn_ln{_i}_{_s}": 2 for _i in "123" for _s in "sb"})
COLUMNS.update({"L3_xattn_b_qkv": 6, "L3_xattn_b_q": 2, "L3_xattn_b_kv": 4, "L3_xattn_b1": 8})


class Op:

    def __init__(self, stage, emit, waits, dma):
        self.stage, self.emit, self.waits, self.dma = stage, emit, waits, dma
        self.signals, self.value = dma, None


class Queue:

    def __init__(self):
        self.ops = []

    def do(self, stage, emit, waits=(), dma=False):
        op = Op(stage, emit, [w for w in waits if w is not None], dma)
        for w in op.waits:
            w.signals = True
        self.ops.append(op)
        return op


class Slot:

    def __init__(self, t):
        self.t, self.taken, self._free = t, False, []

    @property
    def free(self):
        return self._free

    @free.setter
    def free(self, ops):
        self._free, self.taken = ops, False


class Ring:

    def __init__(self, slots):
        self.slots, self.n = [s if isinstance(s, Slot) else Slot(s) for s in slots], 0

    def take(self):
        slot = self.slots[self.n % len(self.slots)]
        self.n += 1
        assert not slot.taken, "the ring is too short"
        slot.taken = True
        return slot


class Program:
    def __init__(self, nc, ctx):
        self.nc, self.ctx = nc, ctx
        self.pe, self.act, self.dve, self.pool, self.sp = (Queue() for _ in range(5))
        self.queues = {"pe": self.pe, "act": self.act, "dve": self.dve, "pool": self.pool, "sp": self.sp}

    def emit(self):
        sems, counts = {}, {}
        for name, q in self.queues.items():
            for op in q.ops:
                if op.signals:
                    key = (name, op.stage)
                    if key not in sems:
                        sems[key] = self.ctx.enter_context(self.nc.semaphore(f"{name}_{op.stage}"))
                    counts[key] = counts.get(key, 0) + (16 if op.dma else 1)
                    op.sem, op.value = sems[key], counts[key]
        block = self.ctx.enter_context(self.nc.Block())

        def program(q):
            def body(eng):
                seen = {}
                for op in q.ops:
                    need = {}
                    for w in op.waits:
                        if need.get(w.sem.name, (None, 0))[1] < w.value:
                            need[w.sem.name] = (w.sem, w.value)
                    for k, (s, v) in need.items():
                        if seen.get(k, 0) < v:
                            eng.wait_ge(s, v)
                            seen[k] = v
                    ins = op.emit(eng)
                    if op.signals:
                        ins.then_inc(op.sem, 16 if op.dma else 1)
            return body

        block.sync(program(self.sp))
        block.gpsimd(program(self.pool))
        block.scalar(program(self.act))
        block.vector(program(self.dve))
        block.tensor(program(self.pe))


def matmul_split(eng, out, st, mv, start, stop, check=True):
    passes = [(st[0], mv[0]), (st[0], mv[1]), (st[1], mv[0])]
    for i, (a, b) in enumerate(passes):
        ins = eng.matmul(out, a, b, start=start and i == 0, stop=stop and i == 2, skip_group_check=not check)
    return ins


def f32(ap):
    return ap.bitcast(F32)


class Kernel:
    def __init__(self, nc, ctx, a, out, stop_after=None):
        self.nc, self.a, self.out = nc, a, out
        self.p = Program(nc, ctx)
        self.ctx = ctx
        self.fence = []
        self.weight_tiles = {}
        self.phase = ""
        self.stop_after = stop_after

    def sb(self, name, shape, dt=F32, scope=None):
        return (scope or self.ctx).enter_context(self.nc.sbuf_tensor(self.phase + name, shape, dt))

    def ring(self, name, n, shape, dt=F32, scope=None):
        r = Ring([self.sb(f"{name}{i}", shape, dt, scope) for i in range(n)])
        for s in r.slots:
            s.free = list(self.fence)
        return r

    def split_ring(self, name, n, shape, scope):
        return self.ring(name, n, [P, 2] + shape, F32R, scope)

    def close_phase(self):
        self.fence = [q.do("phase_end", lambda e: e.nop()) for q in ()]
        p = self.p
        self.fence = [q.ops[-1] for q in (p.pe, p.act, p.dve, p.pool, p.sp) if q.ops]

    def load(self, stage, dst, src, waits=(), q=None):
        return (q or self.p.sp).do(stage, lambda e: e.dma_start(dst, src), waits, dma=True)

    def cols(self, name):
        at = 0
        for n, c in COLUMNS.items():
            if n == name:
                return self.columns[:, at:at + c]
            at += c
        raise KeyError(name)

    def load_bcast(self, stage, name, src, scope):
        t = self.sb(name, [P, src.shape[0]], F32, scope)
        return t, self.load(stage, t[:], src.partition_broadcast(P), self.fence)

    def split_on(self, q, stage, hi, lo, src, waits):
        if q is self.p.pool:
            h = q.do(stage + "_hi", lambda e: e.tensor_scalar(hi, src, 1.0, 1.0, ALU.mult, ALU.mult), waits)
        else:
            h = q.do(stage + "_hi", lambda e: e.tensor_copy(hi, src), waits)
        return q.do(stage + "_lo", lambda e: e.tensor_tensor(lo, src, f32(hi), ALU.subtract), [h])

    def split_psum(self, stage, hi, lo, src, waits, lo_waits=()):
        h = self.p.act.do(stage + "_hi", lambda e: e.activation(hi, src, ACT.Copy), waits)
        return self.p.dve.do(stage + "_lo", lambda e: e.tensor_tensor(lo, src, f32(hi), ALU.subtract),
                             [h, *lo_waits])

    def split_psum_bias(self, stage, hi, lo, src, bias, waits):
        h = self.p.act.do(stage + "_hi", lambda e: e.activation(hi, src, ACT.Identity, bias=bias), waits)
        return self.p.dve.do(stage + "_lo", lambda e: e.scalar_tensor_tensor(
            out=lo, in0=src, scalar=bias, in1=f32(hi), op0=ALU.add, op1=ALU.subtract), [h])

    def load_weight(self, name, src, scope, q, view=None):
        k, n = src.shape
        c = k // P
        t = self.weight_tiles.pop(name, None) or self.sb(name, [P, 2, c, n], F32R, scope)
        done, cs = None, max(1, self.stage_cols // n)
        for c0 in range(0, c, cs):
            m = min(cs, c - c0)
            s = self.staging.take()
            st = s.t[:, 0:m * n].rearrange("p (c n) -> p c n", c=m)
            ld = self.load(f"staging{self.staging.slots.index(s)}", st,
                           src[c0 * P:(c0 + m) * P, :].rearrange("(c p) n -> p c n", p=P), s.free)
            done = self.split_on(q, "weights", t[:, 0, c0:c0 + m, :], t[:, 1, c0:c0 + m, :], st,
                                 [ld, *self.fence])
            s.free = [done]
        return t, done

    def build(self):
        nc, p, a = self.nc, self.p, self.a
        self.x_tok = self.sb("x_tok", [P, B, D])
        self.ctxT = self.sb("ctxT", [P, 2, DC, B * S], F32R)
        self.x_done = [None] * G
        self.ctxT_done = [None] * G
        self.ident = self.sb("ident", [P, P])
        self.head_mask = self.sb("head_mask", [P, HPT])
        self.columns = self.sb("columns", [P, sum(COLUMNS.values())])
        self.cols_done = self.load("columns", self.columns[:], a["columns"])
        bank = lambda n: self.ctx.enter_context(nc.psum_tensor(n, [P, 512], F32))
        self.ps_pair = self.ctx.enter_context(nc.psum_tensor("ps_scores", [P, 2, 512], F32))
        self.ps_tr = [bank(f"ps_tr{i}") for i in range(2)]
        self.ps_acc = [bank(f"ps_acc{i}") for i in range(2)]
        self.ps_misc = [bank(f"ps_misc{i}") for i in range(2)]
        self.scores = Ring([self.ps_pair[:, i, :] for i in range(2)])
        self.tr = Ring(self.ps_tr)
        self.acc = Ring(self.ps_acc)
        self.misc = Ring(self.ps_misc)

        z = p.pool.do("const", lambda e: e.memset(self.ident[:], 0.0))
        m1 = p.pool.do("const", lambda e: e.memset(self.head_mask[:], 1.0))
        self.ident_done = p.pool.do("const", lambda e: e.affine_select(
            out=self.ident[:], in_=self.ident[:], compare_op=ALU.not_equal, fill=1.0, base=0,
            pattern=[[-1, P]], channel_multiplier=1), [z])
        m2 = p.pool.do("const", lambda e: e.affine_select(
            out=self.head_mask[:], in_=self.head_mask[:], compare_op=ALU.is_ge, fill=0.0, base=0,
            pattern=[[-DH, HPT]], channel_multiplier=1), [m1])
        self.mask_done = p.pool.do("const", lambda e: e.affine_select(
            out=self.head_mask[:], in_=self.head_mask[:], compare_op=ALU.is_ge, fill=0.0, base=DH - 1,
            pattern=[[DH, HPT]], channel_multiplier=-1), [m2])

        with ExitStack() as scope:
            self.phase_l0_l1(scope)
            self.close_phase()
        if self.stop_after not in (0, 1):
            with ExitStack() as scope:
                self.phase_l2_attention(scope)
                self.close_phase()
            if self.stop_after != 2:
                with ExitStack() as scope:
                    self.phase_l2_mlp(scope)
                    self.close_phase()
                if self.stop_after != 3:
                    with ExitStack() as scope:
                        self.phase_l3(scope)
                        self.close_phase()
        stores = []
        for g in range(G):
            gb = slice(g * GB, (g + 1) * GB)
            stores.append(self.p.sp.do("store", lambda e, gb=gb: e.dma_start(
                self.out[gb].rearrange("b s d -> s b d"), self.x_tok[:, gb, :]), [self.x_done[g]], dma=True))
        self.p.sp.do("end", lambda e: e.nop(), stores)
        p.emit()

    def norm_transposed(self, g, tag, src, src_done, gain, shift, rms, eps, dst, bufs):
        p = self.p
        st, mv, rs, xn, tmp = (bufs[k].take() for k in ("stats", "mv", "rstd", "xn", "ntmp"))
        xn_t = xn.t[:].rearrange("p (b d) -> p b d", b=GB)
        tmp_t = tmp.t[:].rearrange("p (c t) -> p c t", c=DC)
        w = [src_done]
        for b in range(GB):
            i1 = p.dve.do("ln_stats", lambda e, b=b: e.bn_stats(st.t[:, b, :], src(b)), w + st.free)
            i2 = p.dve.do("ln_aggr", lambda e, b=b: e.bn_aggr(mv.t[:, b, :], st.t[:, b, :]), [i1, *mv.free])
        last = i2
        if rms:
            last = p.dve.do("ln_tiny", lambda e: e.tensor_tensor(rs.t[:, 0, :], mv.t[:, :, 0], mv.t[:, :, 0], ALU.mult),
                            [last, *rs.free])
            last = p.dve.do("ln_tiny", lambda e: e.tensor_tensor(rs.t[:, 1, :], rs.t[:, 0, :], mv.t[:, :, 1], ALU.add), [last])
            var, wv = rs.t[:, 1, :], []
        else:
            var, wv = mv.t[:, :, 1], rs.free
        last = p.dve.do("ln_tiny", lambda e: e.tensor_scalar(rs.t[:, 2, :], var, eps, None, ALU.add), [last, *wv])
        last = p.act.do("ln_sqrt", lambda e: e.activation(rs.t[:, 3, :], rs.t[:, 2, :], ACT.Sqrt), [last])
        last = p.dve.do("ln_tiny", lambda e: e.reciprocal(rs.t[:, 4, :], rs.t[:, 3, :]), [last])
        xw = [last, *xn.free]
        for b in range(GB):
            if rms:
                i3 = p.dve.do("ln_xn", lambda e, b=b: e.tensor_scalar(
                    xn_t[:, b, :], src(b), rs.t[:, 4, b:b + 1], None, ALU.mult), xw)
            else:
                i3 = p.dve.do("ln_xn", lambda e, b=b: e.tensor_scalar(
                    xn_t[:, b, :], src(b), mv.t[:, b, 0:1], rs.t[:, 4, b:b + 1], ALU.subtract, ALU.mult), xw)
        st.free, mv.free, rs.free = [i3], [i3], [i3]
        for c in range(DC):
            bank = self.tr.take()
            for b in range(GB):
                t = p.pe.do("ln_tr", lambda e, b=b, c=c, bank=bank: e.transpose(
                    bank.t[:, b * S:(b + 1) * S], xn_t[:, b, c * P:(c + 1) * P], self.ident[:]),
                    [i3, self.ident_done, *bank.free])
            xf = p.act.do("ln_affine", lambda e, c=c, bank=bank: e.activation(
                tmp_t[:, c, :], bank.t[:], ACT.Identity, scale=gain[:, c:c + 1],
                bias=shift[:, c:c + 1] if shift is not None else 0.0), [t, *tmp.free])
            bank.free = [xf]
            done = self.split_on(p.dve, "ln_split", dst.t[:, 0, c, :], dst.t[:, 1, c, :], tmp_t[:, c, :],
                                 [xf, *dst.free])
        xn.free = [t]
        tmp.free = [done]
        self.norm_read = i3
        return done

    def norm_bufs(self, scope):
        self.work = self.ring("work", 3, [P, GB * D], F32, scope)
        return {"stats": self.ring("st", 1, [P, GB, 6], F32, scope), "mv": self.ring("mv", 1, [P, GB, 2], F32, scope),
                "rstd": self.ring("rstd", 1, [P, 5, GB], F32, scope), "xn": self.work, "ntmp": self.work}

    def add_bias_rows(self, g, bias, waits):
        x = self.x_tok[:, g * GB:(g + 1) * GB, :]
        return self.p.pool.do("x_bias", lambda e: e.tensor_tensor(
            x, x, bias[:].unsqueeze(1).to_broadcast([P, GB, D]), ALU.add), waits)

    def add_to_x(self, g, banks, tickets, waits):
        for i, (bk, t) in enumerate(zip(banks, tickets)):
            x = self.x_tok[:, g * GB + 2 * i:g * GB + 2 * i + 2, :]
            done = self.p.dve.do("x_add", lambda e, x=x, bk=bk: e.tensor_tensor(
                x, x, bk.t[:].rearrange("p (b d) -> p b d", b=2), ALU.add), [t, *waits])
            bk.free = [done]
        return done

    def mlp(self, g, tag, inT, in_done, w1, w1_done, b1, w2, w2_done, func, bufs):
        p = self.p
        banks = [self.acc.take() for _ in range(2)]
        hid = [None] * FC
        for m in range(FC + 2):
            if m < FC:
                bk, h, hs = self.misc.take(), bufs["hid"].take(), bufs["hid_split"].take()

                def up(e, m=m, bk=bk):
                    for c in range(DC):
                        i = matmul_split(e, bk.t[:], [w1[:, s, c, m * P:(m + 1) * P] for s in (0, 1)],
                                         [inT.t[:, s, c, :] for s in (0, 1)], c == 0, c == DC - 1)
                    return i
                u = p.pe.do("mlp_up", up, [in_done, w1_done, *bk.free])
                ge = p.act.do("gelu", lambda e, m=m, bk=bk, h=h: e.activation(
                    h.t[:, 0:T], bk.t[:], func, bias=b1[:, m:m + 1]), [u, *h.free])
                bk.free = [ge]
                sp = self.split_on(p.dve, "hid", hs.t[:, 0, :], hs.t[:, 1, :], h.t[:, 0:T], [ge, *hs.free])
                h.free = [sp]
                hid[m] = (hs, sp)
                if m == FC - 1:
                    inT.free = [u]
            if m >= 2:
                hs, sp = hid[m - 2]

                def down(e, k=m - 2, hs=hs):
                    for b in range(GB):
                        o = banks[b // 2].t[:, (b % 2) * D:(b % 2 + 1) * D]
                        i = matmul_split(e, o, [hs.t[:, s, b * S:(b + 1) * S] for s in (0, 1)],
                                         [w2[:, s, k, :] for s in (0, 1)],
                                         k == 0 and b % 2 == 0, k == FC - 1, check=False)
                    return i
                d = p.pe.do("mlp_down", down, [sp, w2_done, *banks[0].free, *banks[1].free])
                hs.free = [d]
        return banks, d

    def mlp_bufs(self, scope):
        return {"hid": self.work, "hid_split": self.split_ring("hids", 3, [T], scope)}

    def project_cols(self, stage, w, w_done, off, inT, in_done, bias, dst, dst_free):
        p = self.p
        for j in range(DC):
            bk = self.misc.take()

            def mm(e, j=j, bk=bk):
                for c in range(DC):
                    i = matmul_split(e, bk.t[:], [w[:, s, c, off + j * P:off + (j + 1) * P] for s in (0, 1)],
                                     [inT[:, s, c, :] for s in (0, 1)], c == 0, c == DC - 1)
                return i
            m = p.pe.do(stage, mm, [w_done, in_done, *bk.free])
            done = p.act.do(stage, lambda e, j=j, bk=bk: e.activation(
                dst[:, j, :], bk.t[:], ACT.Identity, bias=bias[:, j:j + 1]), [m, *dst_free])
            bk.free = [done]
        return m, done

    def project_rows(self, stage, w, w_done, off, inT, in_done, dst, dst_free):
        p = self.p
        for h in range(2):
            bk = self.misc.take()

            def mm(e, h=h, bk=bk):
                for b in (2 * h, 2 * h + 1):
                    for c in range(DC):
                        i = matmul_split(e, bk.t[:, (b % 2) * D:(b % 2 + 1) * D],
                                         [inT[:, s, c, b * S:(b + 1) * S] for s in (0, 1)],
                                         [w[:, s, c, off:off + D] for s in (0, 1)], c == 0, c == DC - 1)
                return i
            m = p.pe.do(stage, mm, [w_done, in_done, *bk.free])
            done = p.dve.do(stage, lambda e, h=h, bk=bk: e.tensor_copy(
                dst[:, 2 * h:2 * h + 2, :], bk.t[:].rearrange("p (b d) -> p b d", b=2)), [m, *dst_free])
            bk.free = [done]
        return m, done

    def narrow_bufs(self, scope, nsrc):
        return {"km": self.ring("km", 1 + nsrc, [P, QH, T], F32, scope),
                "prob": self.ring("prob", 2, [P, QH, nsrc, S], F32, scope),
                "probT": self.ring("probT", 2, [P, nsrc, QH, S], F32, scope),
                "smax": self.ring("smax", 2, [P, 4, QH], F32, scope),
                "rsum": self.ring("rsum", 1, [P, GB, NH], F32, scope),
                "aoT": self.split_ring("aoT", 1, [DC, T], scope)}

    def narrow_attention(self, g, qT, q_done, kTs, k_dones, vs, v_dones, scale, bufs, mask, bv):
        p, nsrc = self.p, len(kTs)
        acc = [self.acc.take() for _ in range(2)]
        rsum = bufs["rsum"].take()
        items = [(qd, b) for qd in range(NH // QH) for b in range(GB)]
        state = {}
        km_now = {}
        last_pv = {}

        def mask_keys(qd):
            slots, tick = [], None
            for s in range(nsrc):
                km = bufs["km"].take()
                for i in range(QH):
                    h = qd * QH + i
                    j, hh = h // HPT, h % HPT
                    tick = p.pool.do("mask_keys", lambda e, s=s, km=km, i=i, j=j, hh=hh: e.tensor_scalar(
                        km.t[:, i, :], kTs[s][:, j, :], self.head_mask[:, hh:hh + 1], 1.0, ALU.mult, ALU.mult),
                        [k_dones[s], self.mask_done, *km.free])
                slots.append(km)
            km_now[qd] = (slots, tick)
            self.k_read = tick

        def scores(n):
            qd, b = items[n]
            if b == 0:
                if qd == 0:
                    mask_keys(0)
            slots, tick = km_now[qd]
            j = qd * QH // HPT
            banks = [self.scores.take() for _ in range(nsrc)]

            def mm(e):
                for s in range(nsrc):
                    first = True
                    if mask is not None and mask.get("keys") and s == 0:
                        e.matmul(banks[s].t[:], mask["ones"][:], mask["keys"][:, b, :].unsqueeze(1)
                                 .to_broadcast([1, QH, S]), start=True, stop=False)
                        first = False
                    i = e.matmul(banks[s].t[:], qT[:, j, b * S:(b + 1) * S], slots[s].t[:, :, b * S:(b + 1) * S],
                                 start=first, stop=True)
                return i
            w = [q_done, tick] + [f for bk in banks for f in bk.free]
            if mask is not None and "ready" in mask:
                w.append(mask["ready"])
            m = p.pe.do("scores", mm, w)
            if b == GB - 1:
                for sl in slots:
                    sl.free = [m]
                if qd + 1 < NH // QH:
                    mask_keys(qd + 1)
            self.q_read = m
            state[n] = {"banks": banks, "scores": m}

        def softmax(n):
            qd, b = items[n]
            st = state[n]
            banks, m = st["banks"], st["scores"]
            pr, mx = bufs["prob"].take(), bufs["smax"].take()
            if mask is not None and "mul" in mask:
                mul, add = mask["mul"](g * GB + b), mask["add"](g * GB + b)
                r = p.dve.do("mask_mul", lambda e: e.tensor_tensor(
                    pr.t[:, :, 0, :], banks[0].t.rearrange("p (h t) -> p h t", h=QH),
                    mul.unsqueeze(1).to_broadcast([P, QH, S]), ALU.mult), [m, mask["ready2"], *pr.free])
                banks[0].free = [r]
                r = p.dve.do("mask_add", lambda e: e.tensor_tensor(
                    pr.t[:, :, 0, :], pr.t[:, :, 0, :], add.unsqueeze(1).to_broadcast([P, QH, S]), ALU.add), [r])
                src = lambda i: pr.t[:, i, 0, :]
                r = p.dve.do("row_max", lambda e: e.tensor_reduce(
                    mx.t[:, 0, :], pr.t[:, :, 0, :], AX.X, ALU.max), [r, *mx.free])
            else:
                view = self.ps_pair[:, 0:2, :].rearrange("p s (h t) -> p h s t", h=QH)
                src = lambda i: self.ps_pair[:, 0:2, i * S:(i + 1) * S]
                r = p.dve.do("row_max", lambda e: e.tensor_reduce(
                    mx.t[:, 0, :], view, AX.XY, ALU.max), [m, *mx.free])
            r = p.dve.do("row_max", lambda e: e.tensor_scalar(
                mx.t[:, 1, :], mx.t[:, 0, :], -scale, None, ALU.mult), [r])
            for i in range(QH):
                dst = pr.t[:, i, 0, :] if nsrc == 1 else pr.t[:, i, :, :]
                ex = p.act.do("exp", lambda e, i=i, dst=dst: e.activation(
                    dst, src(i), ACT.Exp, bias=mx.t[:, 1, i:i + 1], scale=scale,
                    accum_out=mx.t[:, 2, i:i + 1]), [r, *pr.free])
            if not (mask is not None and "mul" in mask):
                for bk in banks:
                    bk.free = [ex]
            rc = p.dve.do("row_recip", lambda e: e.reciprocal(
                rsum.t[:, b, qd * QH:(qd + 1) * QH], mx.t[:, 2, :]), [ex, *rsum.free])
            mx.free = [rc]
            st.update(prob=pr, exp=ex, recip=rc)

        def transposes(n):
            st = state[n]
            pr, pt = st["prob"], bufs["probT"].take()
            for s in range(nsrc):
                bk = self.tr.take()

                def tr(e, s=s, bk=bk):
                    for i in range(QH):
                        ins = e.transpose(bk.t[:, i * S:(i + 1) * S], pr.t[:, i, s, :], self.ident[:])
                    return ins
                t = p.pe.do("prob_tr", tr, [st["exp"], self.ident_done, *bk.free])
                q = p.dve if nsrc == 1 or s == 1 else p.act
                if q is p.act:
                    ev = q.do("probT", lambda e, s=s, bk=bk: e.activation(
                        pt.t[:, s, :, :], bk.t[:].rearrange("p (h t) -> p h t", h=QH), ACT.Copy), [t, *pt.free])
                else:
                    ev = q.do("probT", lambda e, s=s, bk=bk: e.tensor_copy(
                        pt.t[:, s, :, :], bk.t[:].rearrange("p (h t) -> p h t", h=QH)), [t, *pt.free])
                bk.free = [ev]
                st.setdefault("ev", []).append(ev)
            pr.free = [t]
            st["probT"] = pt

        def values(n):
            qd, b = items[n]
            st = state.pop(n)
            pt, bank = st["probT"], acc[b // 2]

            def mm(e):
                for i in range(QH):
                    h = qd * QH + i
                    for s in range(nsrc):
                        ins = e.matmul(bank.t[:, (b % 2) * D + h * DH:(b % 2) * D + (h + 1) * DH],
                                       pt.t[:, s, i, :], vs[s][:, b, h * DH:(h + 1) * DH],
                                       start=s == 0, stop=s == nsrc - 1)
                return ins
            m = p.pe.do("values", mm, [*st["ev"], *v_dones, *bank.free])
            pt.free = [m]
            last_pv[b] = m
            st["done"] = m

        N = len(items)
        for step in range(N + 3):
            if step < N:
                scores(step)
                softmax(step)
            if 2 <= step < N + 2:
                values(step - 2)
            if 1 <= step < N + 1:
                transposes(step - 1)
        self.v_read = m_last = last_pv[GB - 1]
        ao, aoT = self.work.take(), bufs["aoT"].take()
        ao_t = ao.t[:].rearrange("p (b d) -> p b d", b=GB)
        for i in range(2):
            nrm = p.dve.do("ao_norm", lambda e, i=i: e.tensor_tensor(
                ao_t[:, 2 * i:2 * i + 2, :].rearrange("p b (h d) -> p (b h) d", d=DH),
                acc[i].t[:].rearrange("p (h d) -> p h d", d=DH),
                rsum.t[:, 2 * i:2 * i + 2, :].rearrange("p b h -> p (b h)").unsqueeze(2).to_broadcast([P, 2 * NH, DH]),
                ALU.mult), [m_last, *ao.free])
            acc[i].free = [nrm]
        rsum.free = [nrm]
        for c in range(DC):
            bk = self.tr.take()

            def tr(e, c=c, bk=bk):
                for b in range(GB):
                    ins = e.transpose(bk.t[:, b * S:(b + 1) * S], ao_t[:, b, c * P:(c + 1) * P], self.ident[:])
                return ins
            t = p.pe.do("ao_tr", tr, [nrm, *bk.free])
            done = self.split_psum_bias("ao", aoT.t[:, 0, c, :], aoT.t[:, 1, c, :], bk.t[:], bv[:, c:c + 1],
                                        [t, *aoT.free])
            bk.free = [done]
        ao.free = [t]
        return aoT, done

    def out_projection(self, g, w, w_done, aoT, ao_done):
        banks = [self.acc.take() for _ in range(2)]

        def mm(e):
            for b in range(GB):
                for c in range(DC):
                    i = matmul_split(e, banks[b // 2].t[:, (b % 2) * D:(b % 2 + 1) * D],
                                     [aoT.t[:, s, c, b * S:(b + 1) * S] for s in (0, 1)],
                                     [w[:, s, c, :] for s in (0, 1)], c == 0, c == DC - 1)
            return i
        m = self.p.pe.do("out_proj", mm, [ao_done, w_done, *banks[0].free, *banks[1].free])
        aoT.free = [m]
        return banks, m

    def phase_l0_l1(self, scope):
        self.phase = "l01_"
        p, a = self.p, self.a
        sb = lambda n, s, dt=F32: self.sb(n, s, dt, scope)
        wqT, wkT, wvT = (sb(n, [P, m]) for n, m in (("wqT", D0), ("wkT", D0), ("wvT", P)))
        bq0, bk0, bv0 = sb("bq0", [D0, 1]), sb("bk0", [D0, 1]), sb("bv0", [P, 1])
        loads = [self.load("l0_small", t[:], s) for t, s in (
            (wqT, a["L0_WqT"]), (wkT, a["L0_WkT"]), (wvT, a["L0_WvT"]),
            (bq0, a["L0_xattn_bq"].unsqueeze(1)), (bk0, a["L0_xattn_bk"].unsqueeze(1)),
            (bv0, a["L0_xattn_bv"].unsqueeze(1)))]
        small = loads[-1]
        p.act.do("columns_ready", lambda e: e.nop(), [self.cols_done])
        x_loaded, ctx_loaded = [], []

        def load_group(g):
            gb = slice(g * GB, (g + 1) * GB)
            x_loaded.append(self.load(f"load_x{g}", self.x_tok[:, gb, :], a["x"][gb].rearrange("b s d -> s b d")))
            s = ctx_tok.take()
            ctx_loaded.append((s, self.load(f"load_ctx{g}", s.t[:], a["ctx_2048"][gb].rearrange("b s d -> s b d"), s.free)))
        self.stage_cols = 1024
        for n, shape in (("l1_wq", [DC, D]), ("l1_wo", [DC, D]), ("l1_w1", [DC, F]), ("l1_w2", [FC, D])):
            self.weight_tiles[n] = sb(n, [P, 2] + shape, F32R)
        wkv = sb("l1_wkv", [P, 2, 2, DC, D], F32R)
        qb, bk1, bv1, pw, b1 = (self.cols(n) for n in (
            "L1_xattn_q_b", "L1_kv_b_k", "L1_kv_b_v", "L1_xattn_postnorm_w", "L1_xattn_mlp_b1"))
        ob, _ = self.load_bcast("l1_bias", "l1_ob", a["L1_xattn_out_b"], scope)
        b2, bias = self.load_bcast("l1_bias", "l1_b2", a["L1_xattn_mlp_b2"], scope)
        ones = sb("ones_row", [1, P], F32R)
        one = p.dve.do("key_mask", lambda e: e.tensor_scalar(ones[:], wvT[0:1, :], 0.0, 1.0, ALU.mult, ALU.add), [small])
        l0_scope = ExitStack()
        self.staging = self.ring("staging", 2, [P, self.stage_cols], F32, l0_scope)
        ctx_tok = self.ring("ctx_tok", 2, [P, GB, D], F32, l0_scope)
        load_group(0)
        load_group(1)
        wq, wq_done = self.load_weight("l1_wq", a["L1_xattn_q_w"], scope, p.pool)
        s = self.staging.take()
        stg = s.t[:].rearrange("p (c n s) -> p c n s", c=DC, s=2)
        ld = self.load(f"staging{self.staging.slots.index(s)}", s.t[:].rearrange("p (c n) -> p c n", c=DC),
                       a["L1_xattn_kv_w"].rearrange("(c p) n -> p c n", p=P), s.free)
        for i in range(2):
            wkv_done = self.split_on(p.pool, "weights", wkv[:, i, 0], wkv[:, i, 1], stg[:, :, :, i], [ld])
        s.free = [wkv_done]
        wk, wv = wkv[:, 0], wkv[:, 1]
        wo, wo_done = self.load_weight("l1_wo", a["L1_xattn_out_w"], scope, p.pool)
        w1, w1_done = self.load_weight("l1_w1", a["L1_xattn_mlp_w1"], scope, p.pool)
        w2, w2_done = self.load_weight("l1_w2", a["L1_xattn_mlp_w2"], scope, p.pool)
        l0 = {k: self.ring("l0_" + k, n, s, F32, l0_scope) for k, n, s in (
            ("qk", 2, [D0, 2, D]), ("v", 4, [P, 2, P]), ("prob", 2, [P, 2, D]), ("probT", 2, [P, 2, D]),
            ("mx", 2, [P, 4, 2]))}
        def l0_project(st):
            b, g = st["b"], st["b"] // GB
            x1, x2 = self.x_tok[:, b, :], ctx_loaded[g][0].t[:, b % GB, :]
            bk, qk = self.misc.take(), l0["qk"].take()

            def mm(e):
                e.matmul(bk.t[0:D0, 0:D], wqT[:], x1, start=True, stop=True)
                return e.matmul(bk.t[0:D0, D:2 * D], wkT[:], x2, start=True, stop=True)
            m = p.pe.do("l0_qk", mm, [small, x_loaded[g], ctx_loaded[g][1], *bk.free])
            for i, bb in enumerate((bq0, bk0)):
                st["qk_done"] = p.act.do("l0_qk", lambda e, i=i, bb=bb: e.activation(
                    qk.t[:, i, :], bk.t[0:D0, i * D:(i + 1) * D], ACT.Identity, bias=bb[:, 0:1]), [m, *qk.free])
            bk.free = [st["qk_done"]]
            st["qk"] = qk
            bv_bank, v = self.misc.take(), l0["v"].take()

            def mm_v(e):
                for c in range(2):
                    i = e.matmul(bv_bank.t[:, c * P:(c + 1) * P], x2[:, c * P:(c + 1) * P], wvT[:], start=True, stop=True)
                for c in range(2):
                    i = e.transpose(bv_bank.t[:, (2 + c) * P:(3 + c) * P], x2[:, c * P:(c + 1) * P], self.ident[:])
                return i
            m = p.pe.do("l0_v", mm_v, [self.ident_done, *bv_bank.free])
            if b % GB == GB - 1:
                ctx_loaded[g][0].free = [m]
            st["v_done"] = p.dve.do("l0_v", lambda e: e.tensor_copy(
                v.t[:].rearrange("p c n -> p (c n)"), bv_bank.t[:, 0:2 * P]), [m, *v.free])
            st["v"] = v
            h = slice(b * S, (b + 1) * S)
            src = bv_bank.t[:, 2 * P:4 * P].rearrange("p (c n) -> p c n", c=2)
            self.ctxT_done[g] = self.split_psum("ctxT", self.ctxT[:, 0, :, h], self.ctxT[:, 1, :, h], src,
                                                [m, st["v_done"]])
            bv_bank.free = [self.ctxT_done[g]]

        def l0_scores(st):
            bk, qk, pr, mx = self.scores.take(), st["qk"], l0["prob"].take(), l0["mx"].take()

            def mm(e):
                for c in range(2):
                    i = e.matmul(bk.t[:, c * D:(c + 1) * D], qk.t[:, 0, c * P:(c + 1) * P], qk.t[:, 1, :],
                                 start=True, stop=True)
                return i
            m = p.pe.do("l0_scores", mm, [st["qk_done"], *bk.free])
            qk.free = [m]
            r = p.dve.do("l0_max", lambda e: e.tensor_reduce(
                mx.t[:, 0, :], bk.t.rearrange("p (c n) -> p c n", c=2), AX.X, ALU.max, negate=True), [m, *mx.free])
            for c in range(2):
                ex = p.act.do("l0_exp", lambda e, c=c: e.activation(
                    pr.t[:, c, :], bk.t[:, c * D:(c + 1) * D], ACT.Exp, bias=mx.t[:, 0, c:c + 1],
                    accum_out=mx.t[:, 1, c:c + 1]), [r, *pr.free])
            bk.free = [ex]
            rc = p.dve.do("l0_recip", lambda e: e.reciprocal(mx.t[:, 2, :], mx.t[:, 1, :]), [ex])
            nm = p.pool.do("l0_norm", lambda e: e.tensor_tensor(
                pr.t[:], pr.t[:], mx.t[:, 2, :].unsqueeze(2).to_broadcast([P, 2, D]), ALU.mult), [rc])
            mx.free = [nm]
            st.update(prob=pr, prob_done=nm)

        def l0_values(st):
            b = st["b"]
            bk, pr, pt = self.tr.take(), st["prob"], l0["probT"].take()

            def tr(e):
                for m in range(2):
                    for n in range(2):
                        i = e.transpose(bk.t[:, m * D + n * P:m * D + (n + 1) * P],
                                        pr.t[:, n, m * P:(m + 1) * P], self.ident[:])
                return i
            t = p.pe.do("l0_tr", tr, [st["prob_done"], *bk.free])
            pr.free = [t]
            ev = p.dve.do("l0_probT", lambda e: e.tensor_copy(pt.t[:].rearrange("p m n -> p (m n)"), bk.t[:]), [t, *pt.free])
            bk.free = [ev]
            st.update(probT=pt, probT_done=ev)

        def l0_out(st):
            b, bk, pt, v = st["b"], self.acc.take(), st["probT"], st["v"]

            def mm(e):
                for m in range(2):
                    i = e.matmul(bk.t[:, 0:D], v.t[:, m, :], pt.t[:, m, :], start=m == 0, stop=m == 1)
                return i
            m = p.pe.do("l0_out", mm, [st["probT_done"], st["v_done"], *bk.free])
            pt.free = v.free = [m]
            x = self.x_tok[:, b, :]
            done = p.dve.do("l0_x", lambda e: e.scalar_tensor_tensor(
                out=x, in0=bk.t[:, 0:D], scalar=bv0[:, 0:1], in1=x, op0=ALU.add, op1=ALU.add), [m])
            bk.free = [done]
            self.x_done[b // GB] = done

        def l0_group(g):
            sts = [{"b": g * GB + i} for i in range(GB)]
            for step in range(GB + 3):
                for off, f in ((0, l0_project), (1, l0_scores), (3, l0_out), (2, l0_values)):
                    if 0 <= step - off < GB:
                        f(sts[step - off])
            if g + 2 < G:
                load_group(g + 2)

        def l1_group(g):
            xs = xT.take()
            for c in range(DC):
                bk = self.tr.take()

                def tr(e, c=c, bk=bk):
                    for b in range(GB):
                        i = e.transpose(bk.t[:, b * S:(b + 1) * S], self.x_tok[:, g * GB + b, c * P:(c + 1) * P], self.ident[:])
                    return i
                t = p.pe.do("l1_xT", tr, [self.x_done[g], *bk.free])
                x_tdone = self.split_psum("l1_xT", xs.t[:, 0, c, :], xs.t[:, 1, c, :], bk.t[:], [t, *xs.free])
                bk.free = [x_tdone]
            cT = self.ctxT[:, :, :, g * T:(g + 1) * T]
            cd = self.ctxT_done[g]
            q, k0, k1, v0, v1 = qT.take(), kT[0].take(), kT[1].take(), vv[0].take(), vv[1].take()
            _, q_done = self.project_cols("l1_q", wq, wq_done, 0, xs.t, x_tdone, qb, q.t, q.free + [bias])
            _, k0_done = self.project_cols("l1_k", wk, wkv_done, 0, cT, cd, bk1, k0.t, k0.free)
            _, k1_done = self.project_cols("l1_k", wk, wkv_done, 0, xs.t, x_tdone, bk1, k1.t, k1.free)
            _, v0_done = self.project_rows("l1_v", wv, wkv_done, 0, cT, cd, v0.t, v0.free)
            m, v1_done = self.project_rows("l1_v", wv, wkv_done, 0, xs.t, x_tdone, v1.t, v1.free)
            xs.free = [m]
            mi, ky = mask_i.take(), keys.take()
            ld = self.load("l1_mask", mi.t[:], a["mask_BxS2_ik0"][g * GB:(g + 1) * GB].unsqueeze(0), mi.free)
            kmask = p.dve.do("key_mask", lambda e: e.tensor_scalar(
                ky.t[:], mi.t[:], 0.0, NEG, ALU.is_equal, ALU.mult), [ld, *ky.free])
            mi.free = [kmask]
            mask = {"keys": ky.t, "ones": ones, "ready": kmask}
            aoT, ao_done = self.narrow_attention(g, q.t, q_done, [k0.t, k1.t], [k0_done, k1_done], [v0.t, v1.t],
                                                 [v0_done, v1_done], 1.0 / DH, ab, mask, bv1)
            ky.free = [self.q_read]
            q.free, k0.free, k1.free = [self.q_read], [self.k_read], [self.k_read]
            v0.free = v1.free = [self.v_read]
            banks, m = self.out_projection(g, wo, wo_done, aoT, ao_done)
            ys = self.work.take()
            ys_t = ys.t[:].rearrange("p (b d) -> p b d", b=GB)
            xg = self.x_tok[:, g * GB:(g + 1) * GB, :]
            y0 = p.pool.do("l1_y", lambda e: e.tensor_tensor(
                ys_t, xg, ob[:].unsqueeze(1).to_broadcast([P, GB, D]), ALU.add), [self.x_done[g], bias, *ys.free])
            for i in range(2):
                yd = p.dve.do("l1_y", lambda e, i=i, banks=banks: e.tensor_tensor(
                    ys_t[:, 2 * i:2 * i + 2, :], ys_t[:, 2 * i:2 * i + 2, :],
                    banks[i].t[:].rearrange("p (b d) -> p b d", b=2), ALU.add), [y0, m])
                banks[i].free = [yd]
            xb = self.add_bias_rows(g, b2, [y0, t])
            hs = xT.take()
            h_done = self.norm_transposed(g, "l1", lambda b: ys_t[:, b, :], yd, pw, None, True, 1e-6, hs, nb)
            ys.free = [self.norm_read]
            banks, m = self.mlp(g, "l1", hs, h_done, w1, w1_done, b1, w2, w2_done, ACT.Gelu_apprx_tanh, mb)
            self.x_done[g] = self.add_to_x(g, banks, [m, m], [xb])

        for g in range(G):
            l0_group(g)
        l0_scope.close()
        self.close_phase()
        if self.stop_after == 0:
            return
        nb, mb, ab = self.norm_bufs(scope), None, self.narrow_bufs(scope, 2)
        xT = self.split_ring("xT", 1, [DC, T], scope)
        qT = self.ring("qT", 1, [P, DC, T], F32, scope)
        kT = [self.ring(f"kT{i}", 1, [P, DC, T], F32, scope) for i in range(2)]
        vv = [self.ring(f"vv{i}", 1, [P, GB, D], F32, scope) for i in range(2)]

        mask_i = self.ring("mask_i", 1, [1, GB, S], I32, scope)
        keys = self.ring("mask_keys", 1, [1, GB, S], F32R, scope)
        mb = self.mlp_bufs(scope)
        for g in range(G):
            l1_group(g)

    def phase_l2_attention(self, scope):
        self.phase = "l2a_"
        p, a = self.p, self.a
        sb = lambda n, s, dt=F32: self.sb(n, s, dt, scope)
        hT = [self.split_ring(f"l2_hT{g}", 1, [DC, T], scope).slots[0] for g in range(G)]
        W = {k: self.ring("l2_" + k, 2, [P, 2, DC, HG * K2], F32R, scope) for k in ("wq", "wk", "wv")}
        W["wo"] = self.ring("l2_wo", 2, [P, 2, HG, D], F32R, scope)
        staging = self.ring("l2_staging", 2, [P, DC * HG * K2], F32, scope)
        V = self.ring("l2_V", 2, [P, GB, HG * K2], F32, scope)
        QT = self.ring("l2_qT", 2, [P, T], F32, scope)
        KT = self.ring("l2_kT", 2, [P, GB, S + 2], F32, scope)
        PR = self.ring("l2_prob", 2, [P, GB, S + 2], F32, scope)
        PT = self.ring("l2_probT", 1, [P, T], F32, scope)
        AO = self.split_ring("l2_ao", 1, [T], scope)
        MX = self.ring("l2_mx", 2, [P, 4, GB], F32, scope)
        pb = sb("l2_pb", [P, B, H2])
        pbT = self.ring("l2_pbT", 1, [H2, GB, S], F32, scope)
        BW = sb("l2_bw", [H2, D])
        dv = sb("l2_dv", [P, H2])
        dsel = sb("l2_dsel", [P, H2, H2])
        nb = {"stats": self.ring("st2_", 1, [P, GB, 6], F32, scope), "mv": self.ring("mv2_", 1, [P, GB, 2], F32, scope),
              "rstd": self.ring("rs2_", 1, [P, 5, GB], F32, scope)}
        proj = self.misc
        scale = float(K2) ** -0.5
        cols = {}
        for i in ("1", "2"):
            for n in (f"ln{i}_scale", f"ln{i}_offset", f"bq{i}", f"bk{i}", f"bv{i}", f"bias_k{i}", f"bias_v{i}"):
                cols[n] = self.cols("L2_xattn_" + n)
            cols["bo" + i], cols_done = self.load_bcast("l2_bias", "l2_bo" + i, a["L2_xattn_bo" + i], scope)

        wslots = {}

        def load_weights(at, hg):
            n = str(at + 1)
            got = {}
            for k in ("wk", "wv", "wq", "wo"):
                w, s = W[k].take(), staging.take()
                if k == "wo":
                    src = a["L2_xattn_wo" + n][hg * HG * K2:(hg + 1) * HG * K2, :].rearrange("(c p) n -> p c n", p=P)
                    st = s.t[:].rearrange("p (c n) -> p c n", c=HG)
                else:
                    src = a[f"L2_xattn_{k}{n}"].rearrange("(c p) n -> p c n", p=P)[:, :, hg * HG * K2:(hg + 1) * HG * K2]
                    st = s.t[:].rearrange("p (c n) -> p c n", c=DC)
                ld = self.load(f"l2_staging{staging.slots.index(s)}", st, src, s.free)
                done = self.split_on(p.pool, "l2_weights", w.t[:, 0], w.t[:, 1], st, [ld, *w.free])
                s.free = [done]
                got[k] = (w, done)
            wslots[at, hg] = got

        def normalise(at, g):
            n = str(at + 1)
            bufs = dict(nb, xn=staging, ntmp=staging)
            done = self.norm_transposed(g, "l2", lambda b: self.x_tok[:, g * GB + b, :], self.x_done[g],
                                        cols["ln" + n + "_scale"], cols["ln" + n + "_offset"], False, 1e-5, hT[g], bufs)
            hT_done[g] = done
            self.x_done[g] = self.add_bias_rows(g, cols["bo" + n], [self.norm_read, cols_done])

        hT_done = [None] * G
        items = [(at, hg, g, h) for at in range(2) for hg in range(H2 // HG) for g in range(G) for h in range(HG)]
        N = len(items)
        st = [dict() for _ in items]
        vslot = {}
        acc_now = {}
        bw_done = {}

        def bias_rows(at, hg):
            n = str(at + 1)
            w, wd = wslots[at, hg]["wo"]
            if hg == 0:
                d = p.dve.do("l2_dv", lambda e: e.tensor_tensor(dv[:], cols["bias_v" + n], cols["bv" + n], ALU.subtract),
                             [cols_done])
                z = p.dve.do("l2_dv", lambda e: e.memset(dsel[:], 0.0), bw_free["dsel"])
                for h in range(H2):
                    d = p.dve.do("l2_dv", lambda e, h=h: e.tensor_copy(dsel[:, h, h:h + 1], dv[:, h:h + 1]), [d, z])
                bw_free["dv"] = d
            bk = self.misc.take()

            def mm(e):
                for i in range(HG):
                    for s in (0, 1):
                        ins = e.matmul(bk.t[0:H2, 0:D], dsel[:, hg * HG + i, :], f32(w.t[:, s, i, :]),
                                       start=i == 0 and s == 0, stop=i == HG - 1 and s == 1)
                return ins
            m = p.pe.do("l2_bw", mm, [wd, bw_free["dv"], *bk.free])
            bw_free["dsel"] = [m]
            if hg == 0:
                b = p.dve.do("l2_bw", lambda e: e.tensor_copy(BW[:], bk.t[0:H2, 0:D]), [m, *bw_free["bw"]])
            else:
                b = p.dve.do("l2_bw", lambda e: e.tensor_tensor(BW[:], BW[:], bk.t[0:H2, 0:D], ALU.add), [m, bw_done[at]])
            bk.free = [b]
            bw_done[at] = b
        bw_free = {"dsel": list(self.fence), "bw": list(self.fence)}

        def project(n, what):
            if what == "v":
                tgt, b = n - n % HG + HG, n % HG
                if tgt >= N:
                    return
                at, hg, g, _ = items[tgt]
                if b == 0:
                    if (at, hg) not in wslots:
                        load_weights(at, hg)
                    vslot[tgt] = [V.take(), None]
                v = vslot[tgt][0]
                w, wd = wslots[at, hg]["wv"]
                bk = proj.take()

                def mm(e):
                    for c in range(DC):
                        t0 = g * T + b * S
                        i = matmul_split(e, bk.t[:], [self.ctxT[:, s, c, t0:t0 + S] for s in (0, 1)],
                                         [w.t[:, s, c, :] for s in (0, 1)], c == 0, c == DC - 1)
                    return i
                m = p.pe.do("l2_v", mm, [wd, *bk.free])
                ev = p.dve.do("l2_v", lambda e: e.tensor_copy(v.t[:, b, :], bk.t[:]), [m, *v.free])
                bk.free = [ev]
                vslot[tgt][1] = ev
                if b == GB - 1 and g == G - 1:
                    w.free = [m]
                return
            at, hg, g, h = items[n]
            nm = str(at + 1)
            if what == "q":
                w, wd = wslots[at, hg]["wq"]
                bk, q = proj.take(), QT.take()

                def mm(e):
                    for c in range(DC):
                        i = matmul_split(e, bk.t[:], [w.t[:, s, c, h * K2:(h + 1) * K2] for s in (0, 1)],
                                         [hT[g].t[:, s, c, :] for s in (0, 1)], c == 0, c == DC - 1)
                    return i
                m = p.pe.do("l2_q", mm, [wd, hT_done[g], *bk.free])
                hd = hg * HG + h
                st[n]["q_done"] = p.act.do("l2_q", lambda e: e.activation(
                    q.t[:], bk.t[:], ACT.Identity, bias=cols["bq" + nm][:, hd:hd + 1]), [m, *q.free])
                bk.free = [st[n]["q_done"]]
                st[n]["q"] = q
                if hg == H2 // HG - 1 and h == HG - 1:
                    hT[g].free = [m]
            else:
                w, wd = wslots[at, hg]["wk"]
                bk, k = proj.take(), KT.take()

                def mm(e):
                    for c in range(DC):
                        i = matmul_split(e, bk.t[:], [w.t[:, s, c, h * K2:(h + 1) * K2] for s in (0, 1)],
                                         [self.ctxT[:, s, c, g * T:(g + 1) * T] for s in (0, 1)], c == 0, c == DC - 1)
                    return i
                m = p.pe.do("l2_k", mm, [wd, *bk.free])
                hd = hg * HG + h
                st[n]["k_done"] = p.act.do("l2_k", lambda e: e.activation(
                    k.t[:, :, 0:S], bk.t[:].rearrange("p (b t) -> p b t", b=GB), ACT.Identity,
                    bias=cols["bk" + nm][:, hd:hd + 1]), [m, *k.free])
                bk.free = [st[n]["k_done"]]
                st[n]["bk_done"] = p.pool.do("l2_bias_k", lambda e: e.tensor_copy(
                    k.t[:, :, S:S + 2], cols["bias_k" + nm][:, hd:hd + 1].unsqueeze(2).to_broadcast([P, GB, 2])), k.free)
                st[n]["k"] = k
            if h == HG - 1 and g == G - 1:
                w.free = [m]

        def scores(n):
            s = st[n]
            q, k = s["q"], s["k"]
            banks = [self.scores.take() for _ in range(2)]
            pr, mx = PR.take(), MX.take()
            for i, bk in enumerate(banks):
                def mm(e, i=i, bk=bk):
                    for b in (2 * i, 2 * i + 1):
                        ins = e.matmul(bk.t[:, (b % 2) * (S + 2):(b % 2 + 1) * (S + 2)], q.t[:, b * S:(b + 1) * S],
                                       k.t[:, b, :], start=True, stop=True)
                    return ins
                m = p.pe.do("l2_scores", mm, [s["q_done"], s["k_done"], s["bk_done"], *bk.free])
                r = p.dve.do("l2_max", lambda e, i=i, bk=bk: e.tensor_reduce(
                    mx.t[:, 0, 2 * i:2 * i + 2], bk.t[:, 0:2 * (S + 2)].rearrange("p (b t) -> p b t", b=2)[:, :, 0:S + 1],
                    AX.X, ALU.max), [m, *mx.free])
            q.free = k.free = [m]
            r = p.dve.do("l2_max", lambda e: e.tensor_scalar(mx.t[:, 1, :], mx.t[:, 0, :], -scale, None, ALU.mult), [r])
            for b in range(GB):
                ex = p.act.do("l2_exp", lambda e, b=b: e.activation(
                    pr.t[:, b, 0:S + 1], banks[b // 2].t[:, (b % 2) * (S + 2):(b % 2) * (S + 2) + S + 1], ACT.Exp,
                    bias=mx.t[:, 1, b:b + 1], scale=scale, accum_out=mx.t[:, 2, b:b + 1]), [r, *pr.free])
                banks[b // 2].free = [ex]
            rc = p.dve.do("l2_recip", lambda e: e.reciprocal(mx.t[:, 3, :], mx.t[:, 2, :]), [ex])
            nm = p.pool.do("l2_norm", lambda e: e.tensor_tensor(
                pr.t[:, :, 0:S + 1], pr.t[:, :, 0:S + 1], mx.t[:, 3, :].unsqueeze(2).to_broadcast([P, GB, S + 1]), ALU.mult),
                [rc])
            at, hg, g, h = items[n]
            hd = hg * HG + h
            pbc = p.pool.do("l2_pb", lambda e: e.tensor_copy(
                pb[:, g * GB:(g + 1) * GB, hd:hd + 1], pr.t[:, :, S:S + 1]), [nm, *pb_free[g]])
            mx.free = [nm]
            s.update(prob=pr, prob_done=nm, pb_done=pbc)
        pb_free = [list(self.fence) for _ in range(G)]

        def transposes(n):
            s = st[n]
            bk, pt, pr = tr_ring.take(), PT.take(), s["prob"]

            def tr(e):
                for b in range(GB):
                    i = e.transpose(bk.t[:, b * S:(b + 1) * S], pr.t[:, b, 0:S], self.ident[:])
                return i
            t = p.pe.do("l2_tr", tr, [s["prob_done"], *bk.free])
            pr.free = [t, s["pb_done"]]
            ev = p.dve.do("l2_probT", lambda e: e.tensor_copy(pt.t[:], bk.t[:]), [t, *pt.free])
            bk.free = [ev]
            s.update(probT=pt, probT_done=ev)
        tr_ring, pv_ring = Ring(self.tr.slots[0:1]), Ring(self.tr.slots[1:2])

        def values(n):
            at, hg, g, h = items[n]
            s = st[n]
            bk, ao, pt = pv_ring.take(), AO.take(), s["probT"]
            v, vd = vslot[n - h]

            def mm(e):
                for b in range(GB):
                    i = e.matmul(bk.t[:, b * S:(b + 1) * S], v.t[:, b, h * K2:(h + 1) * K2], pt.t[:, b * S:(b + 1) * S],
                                 start=True, stop=True)
                return i
            m = p.pe.do("l2_values", mm, [s["probT_done"], vd, *bk.free])
            pt.free = [m]
            if h == HG - 1:
                v.free = [m]
            hd = hg * HG + h
            done = self.split_psum_bias("l2_ao", ao.t[:, 0, :], ao.t[:, 1, :], bk.t[:], cols["bv" + str(at + 1)][:, hd:hd + 1],
                                        [m, *ao.free])
            bk.free = [done]
            s.update(ao=ao, ao_done=done)

        def output(n):
            at, hg, g, h = items[n]
            s = st[n]
            ao = s["ao"]
            w, wd = wslots[at, hg]["wo"]
            if h == 0:
                acc_now[0] = [self.acc.take() for _ in range(2)]
                if g == 0:
                    bias_rows(at, hg)
            banks = acc_now[0]
            last = hg == H2 // HG - 1
            if last and h == HG - 1:
                bk, pt = self.misc.take(), pbT.take()

                def tr(e):
                    for b in range(GB):
                        i = e.transpose(bk.t[0:H2, b * S:(b + 1) * S], pb[:, g * GB + b, :], self.ident[:])
                    return i
                t = p.pe.do("l2_pbT", tr, [s["pb_done"], *bk.free])
                pb_free[g] = [t]
                ev = p.act.do("l2_pbT", lambda e: e.activation(
                    pt.t[:].rearrange("h b t -> h (b t)"), bk.t[0:H2, :], ACT.Copy), [t, *pt.free])
                bk.free = [ev]

            def mm(e):
                for b in range(GB):
                    i = matmul_split(e, banks[b // 2].t[:, (b % 2) * D:(b % 2 + 1) * D],
                                     [ao.t[:, x, b * S:(b + 1) * S] for x in (0, 1)], [w.t[:, x, h, :] for x in (0, 1)],
                                     h == 0 and b % 2 == 0, h == HG - 1 and not last, check=False)
                return i
            m = p.pe.do("l2_out", mm, [s["ao_done"], wd, *banks[0].free, *banks[1].free])
            ao.free = [m]
            if g == G - 1 and h == HG - 1:
                w.free = [m]
            if last and h == HG - 1:
                def mm(e):
                    for b in range(GB):
                        i = e.matmul(banks[b // 2].t[:, (b % 2) * D:(b % 2 + 1) * D], pt.t[:, b, :], BW[:],
                                     start=False, stop=True, skip_group_check=True)
                    return i
                m = p.pe.do("l2_out_bias", mm, [ev, bw_done[at]])
                pt.free = [m]
                bw_free["bw"] = [m]
            if h == HG - 1:
                self.x_done[g] = self.add_to_x(g, banks, [m, m], [self.x_done[g]])
                if last and at == 0:
                    normalise(1, g)
            nxt = (at, hg + 1) if not last else (at + 1, 0)
            if g == 1 and h == 0 and nxt[0] < 2 and nxt not in wslots:
                load_weights(*nxt)
            st[n] = None

        load_weights(0, 0)
        for g in range(G):
            normalise(0, g)
        for n in range(-HG, -2):
            project(n, "v")
        for step in range(N + 3):
            if 1 <= step <= N:
                scores(step - 1)
            if step < N:
                project(step, "q")
            if 2 <= step <= N + 1:
                values(step - 2)
            if step < N:
                project(step, "k")
            project(step - 2, "v")
            if 2 <= step <= N + 1:
                output(step - 2)
            if 1 <= step <= N:
                transposes(step - 1)

    def phase_l2_mlp(self, scope):
        self.phase = "l2m_"
        p, a = self.p, self.a
        self.stage_cols = 1024
        self.staging = self.ring("staging_m", 2, [P, self.stage_cols], F32, scope)
        cols = {n: self.cols("L2_xattn_" + n)
                for n in ("ln_mlp_scale", "ln_mlp_offset", "b_fc1")}
        b2, cd = self.load_bcast("l2m_bias", "l2m_b2", a["L2_xattn_b_fc2"], scope)
        w1, w1_done = self.load_weight("l2_w1", a["L2_xattn_w_fc1"], scope, p.dve)
        w2, w2_done = self.load_weight("l2_w2", a["L2_xattn_w_fc2"], scope, p.dve)
        nb, mb = self.norm_bufs(scope), self.mlp_bufs(scope)
        hT = self.split_ring("l2m_hT", 2, [DC, T], scope)
        ready = {}

        def norm(g):
            hs = hT.take()
            ready[g] = (hs, self.norm_transposed(g, "l2m", lambda b: self.x_tok[:, g * GB + b, :], self.x_done[g],
                        cols["ln_mlp_scale"], cols["ln_mlp_offset"], False, 1e-5, hs, nb))
            self.x_done[g] = self.add_bias_rows(g, b2, [self.norm_read, cd])
        p.act.do("l2m_ready", lambda e: e.nop(), [cd])
        norm(0)
        for g in range(G):
            if g + 1 < G:
                norm(g + 1)
            hs, hd = ready[g]
            banks, m = self.mlp(g, "l2", hs, hd, w1, w1_done, cols["b_fc1"], w2, w2_done, ACT.Gelu, mb)
            self.x_done[g] = self.add_to_x(g, banks, [m, m], [self.x_done[g]])

    def phase_l3(self, scope):
        self.phase = "l3_"
        p, a = self.p, self.a
        sb = lambda n, s, dt=F32: self.sb(n, s, dt, scope)
        self.stage_cols = 1024
        self.staging = self.ring("staging3_", 2, [P, self.stage_cols], F32, scope)
        cols = {n: self.cols("L3_xattn_" + n)
                for n in ("ln1_s", "ln1_b", "ln2_s", "ln2_b", "ln3_s", "ln3_b", "b_qkv", "b_q", "b_kv", "b1")}
        rows = {n: self.load_bcast("l3_bias", "l3_" + n, a["L3_xattn_" + n], scope)[0] for n in ("b_ao", "b_co", "b2")}
        mask1 = sb("mask1", [P, 2, S])
        cd = self.load("l3_bias", mask1[:, 0, :], a["mask_1x1xSxS2_fc1"][0, 0], self.fence)
        MS = self.ring("mask2_", 1, [P, 2, GB, S], F32, scope)
        ws, wd = {}, {}
        for n in ("w_qkv", "w_ao", "w_q", "w_kv", "w_co", "w1", "w2"):
            ws[n], wd[n] = self.load_weight("l3_" + n, a["L3_xattn_" + n], scope, p.dve if n in ("w_qkv",) else p.pool)
        m1 = p.dve.do("mask_prep", lambda e: e.tensor_scalar(
            mask1[:, 1, :], mask1[:, 0, :], -1.0, 40000.0, ALU.add, ALU.mult), [cd])
        nb, mb, ab = self.norm_bufs(scope), self.mlp_bufs(scope), self.narrow_bufs(scope, 1)
        hT = self.split_ring("l3_hT", 1, [DC, T], scope)
        qT = self.ring("l3_qT", 1, [P, DC, T], F32, scope)
        kT = self.ring("l3_kT", 1, [P, DC, T], F32, scope)
        vv = self.ring("l3_v", 1, [P, GB, D], F32, scope)
        p.act.do("l3_ready", lambda e: e.nop(), [cd])
        scale = float(DH) ** -0.5

        def group(g):
            x = lambda b: self.x_tok[:, g * GB + b, :]
            ms = MS.take()
            ml = self.load(f"mask2_{MS.slots.index(ms)}", ms.t[:, 0], a["mask_Bx1xSxS2_ff1"][g * GB:(g + 1) * GB, 0]
                           .rearrange("b s t -> s b t"), ms.free)
            m2 = p.pool.do("mask_prep", lambda e: e.tensor_scalar(
                ms.t[:, 1], ms.t[:, 0], -1.0, 40000.0, ALU.add, ALU.mult), [ml])
            hs = hT.take()
            hd = self.norm_transposed(g, "l3", x, self.x_done[g], cols["ln1_s"], cols["ln1_b"], False, 1e-5, hs, nb)
            xb = self.add_bias_rows(g, rows["b_ao"], [self.norm_read, cd])
            q, k, v = qT.take(), kT.take(), vv.take()
            _, qd = self.project_cols("l3_q", ws["w_qkv"], wd["w_qkv"], 0, hs.t, hd, cols["b_qkv"][:, 0:2], q.t, q.free)
            _, kd = self.project_cols("l3_k", ws["w_qkv"], wd["w_qkv"], D, hs.t, hd, cols["b_qkv"][:, 2:4], k.t, k.free)
            m, vd = self.project_rows("l3_v", ws["w_qkv"], wd["w_qkv"], 2 * D, hs.t, hd, v.t, v.free)
            hs.free = [m]
            mask = {"mul": lambda b: mask1[:, 0, :], "add": lambda b: mask1[:, 1, :], "ready2": m1}
            aoT, ad = self.narrow_attention(g, q.t, qd, [k.t], [kd], [v.t], [vd], scale, ab, mask, cols["b_qkv"][:, 4:6])
            q.free, k.free, v.free = [self.q_read], [self.k_read], [self.v_read]
            banks, m = self.out_projection(g, ws["w_ao"], wd["w_ao"], aoT, ad)
            xd = self.add_to_x(g, banks, [m, m], [xb])
            hs = hT.take()
            hd = self.norm_transposed(g, "l3", x, xd, cols["ln2_s"], cols["ln2_b"], False, 1e-5, hs, nb)
            xb = self.add_bias_rows(g, rows["b_co"], [self.norm_read])
            q, k, v = qT.take(), kT.take(), vv.take()
            cT = self.ctxT[:, :, :, g * T:(g + 1) * T]
            m, qd = self.project_cols("l3_q", ws["w_q"], wd["w_q"], 0, hs.t, hd, cols["b_q"], q.t, q.free)
            hs.free = [m]
            _, kd = self.project_cols("l3_k", ws["w_kv"], wd["w_kv"], 0, cT, self.ctxT_done[g], cols["b_kv"][:, 0:2], k.t, k.free)
            _, vd = self.project_rows("l3_v", ws["w_kv"], wd["w_kv"], D, cT, self.ctxT_done[g], v.t, v.free)
            mask = {"mul": lambda b: ms.t[:, 0, b % GB, :], "add": lambda b: ms.t[:, 1, b % GB, :], "ready2": m2}
            aoT, ad = self.narrow_attention(g, q.t, qd, [k.t], [kd], [v.t], [vd], scale, ab, mask, cols["b_kv"][:, 2:4])
            ms.free = [ad]
            q.free, k.free, v.free = [self.q_read], [self.k_read], [self.v_read]
            banks, m = self.out_projection(g, ws["w_co"], wd["w_co"], aoT, ad)
            xd = self.add_to_x(g, banks, [m, m], [xb])
            hs = hT.take()
            hd = self.norm_transposed(g, "l3", x, xd, cols["ln3_s"], cols["ln3_b"], False, 1e-5, hs, nb)
            xb = self.add_bias_rows(g, rows["b2"], [self.norm_read])
            banks, m = self.mlp(g, "l3", hs, hd, ws["w1"], wd["w1"], cols["b1"], ws["w2"], wd["w2"], ACT.Gelu_apprx_tanh, mb)
            self.x_done[g] = self.add_to_x(g, banks, [m, m], [xb])

        for g in range(G):
            group(g)


def xattn_stack_kernel(nc, args, out, stop_after=None):
    with ExitStack() as ctx:
        Kernel(nc, ctx, args, out, stop_after).build()


STOP = None


def kernel(**inputs):
    import numpy as np
    from concourse import bacc, mybir
    from concourse.bass_utils import run_bass_kernel_spmd

    arrays = {n: v for n, v in inputs.items() if not n.startswith("L0_xattn_W")}
    packed = dict(inputs)
    kv_b = inputs["L1_xattn_kv_b"].reshape(-1, 2)
    packed["L1_kv_b_k"], packed["L1_kv_b_v"] = kv_b[:, 0], kv_b[:, 1]
    arrays = {n: v for n, v in arrays.items() if n not in COLUMNS and n != "L1_xattn_kv_b"}
    arrays["columns"] = np.concatenate([np.reshape(packed[n], (-1, P)).T for n in COLUMNS], axis=1)
    arrays.update({f"L0_W{c}T": np.transpose(inputs[f"L0_xattn_W{c}"]) for c in "qkv"})
    nc = bacc.Bacc("TRN2", target_bir_lowering=False, num_devices=1)
    feed, args = {}, {}
    for name, v in arrays.items():
        v = np.ascontiguousarray(v)
        feed["in_" + name] = v
        args[name] = nc.dram_tensor("in_" + name, v.shape, mybir.dt.from_np(v.dtype), kind="ExternalInput").ap()
    out = nc.dram_tensor("out_0", inputs["x"].shape, mybir.dt.float32, kind="ExternalOutput").ap()
    xattn_stack_kernel(nc, args, out, STOP)
    r = run_bass_kernel_spmd(nc, [feed], core_ids=[0])
    return r.results[0]["out_0"]
```

```python
from contextlib import ExitStack

import concourse.bass as bass
from concourse import mybir

F32 = mybir.dt.float32
F32R = mybir.dt.float32r
I32 = mybir.dt.int32
ALU = mybir.AluOpType
ACT = mybir.ActivationFunctionType
AX = mybir.AxisListType

P = 128
B, S, D = 16, 128, 256
DC = D // P
GB = 4
G = B // GB
T = GB * S
D0 = 16
NH, DH = 16, 16
HPT = P // DH
QH = 4
H2, K2 = 16, 128
HG = 4
F = 1024
FC = F // P
L1_RATE = (0.3, 1.2, 1.2, 1.0)
L3_RATE = (0.5, 0.5, 0.5, 1.2, 1.2, 0.5, 0.5, 1.0)
NEG = -1.0e30


COLUMNS = {"L1_xattn_q_b": 2, "L1_kv_b_k": 2, "L1_kv_b_v": 2, "L1_xattn_postnorm_w": 2, "L1_xattn_mlp_b1": 8}
for _i in "12":
    COLUMNS.update({f"L2_xattn_ln{_i}_scale": 2, f"L2_xattn_ln{_i}_offset": 2, f"L2_xattn_bq{_i}": 16,
                    f"L2_xattn_bk{_i}": 16, f"L2_xattn_bv{_i}": 16, f"L2_xattn_bias_k{_i}": 16,
                    f"L2_xattn_bias_v{_i}": 16})
COLUMNS.update({"L2_xattn_ln_mlp_scale": 2, "L2_xattn_ln_mlp_offset": 2, "L2_xattn_b_fc1": 8})
COLUMNS.update({f"L3_xattn_ln{_i}_{_s}": 2 for _i in "123" for _s in "sb"})
COLUMNS.update({"L3_xattn_b_qkv": 6, "L3_xattn_b_q": 2, "L3_xattn_b_kv": 4, "L3_xattn_b1": 8})


class Op:

    def __init__(self, stage, emit, waits, dma):
        self.stage, self.emit, self.waits, self.dma = stage, emit, waits, dma
        self.signals, self.value = dma, None


class Queue:

    def __init__(self):
        self.ops = []

    def do(self, stage, emit, waits=(), dma=False):
        op = Op(stage, emit, [w for w in waits if w is not None], dma)
        for w in op.waits:
            w.signals = True
        self.ops.append(op)
        return op


class Slot:

    def __init__(self, t):
        self.t, self.taken, self._free = t, False, []

    @property
    def free(self):
        return self._free

    @free.setter
    def free(self, ops):
        self._free, self.taken = ops, False


class Ring:

    def __init__(self, slots):
        self.slots, self.n = [s if isinstance(s, Slot) else Slot(s) for s in slots], 0

    def spare(self):
        return sum(not s.taken for s in self.slots)

    def full(self):
        return self.spare() == 0

    def take(self):
        assert not self.full(), "the ring is too short"
        while self.slots[self.n % len(self.slots)].taken:
            self.n += 1
        slot = self.slots[self.n % len(self.slots)]
        self.n += 1
        slot.taken = True
        return slot


def acquire(ring):
    for _ in range(1000):
        if not ring.full():
            return ring.take()
        yield
    raise AssertionError("two chains of stages wait for each other's buffers")


def interleave(main, side, rate):
    due = 0.0
    for _ in main:
        due += rate
        while due >= 1.0:
            due -= 1.0
            next(side, None)
    for _ in side:
        pass


def run(stages):
    while True:
        try:
            next(stages)
        except StopIteration as end:
            return end.value


def chain(*parts):
    for part in parts:
        yield from part


class Program:
    def __init__(self, nc, ctx):
        self.nc, self.ctx = nc, ctx
        self.pe, self.act, self.dve, self.pool, self.sp = (Queue() for _ in range(5))
        self.queues = {"pe": self.pe, "act": self.act, "dve": self.dve, "pool": self.pool, "sp": self.sp}

    def emit(self):
        sems, counts = {}, {}
        for name, q in self.queues.items():
            for op in q.ops:
                if op.signals:
                    key = (name, op.stage)
                    if key not in sems:
                        sems[key] = self.ctx.enter_context(self.nc.semaphore(f"{name}_{op.stage}"))
                    counts[key] = counts.get(key, 0) + (16 if op.dma else 1)
                    op.sem, op.value = sems[key], counts[key]
        block = self.ctx.enter_context(self.nc.Block())

        def program(q):
            def body(eng):
                seen = {}
                for op in q.ops:
                    need = {}
                    for w in op.waits:
                        if need.get(w.sem.name, (None, 0))[1] < w.value:
                            need[w.sem.name] = (w.sem, w.value)
                    for k, (s, v) in need.items():
                        if seen.get(k, 0) < v:
                            eng.wait_ge(s, v)
                            seen[k] = v
                    ins = op.emit(eng)
                    if op.signals:
                        ins.then_inc(op.sem, 16 if op.dma else 1)
            return body

        block.sync(program(self.sp))
        block.gpsimd(program(self.pool))
        block.scalar(program(self.act))
        block.vector(program(self.dve))
        block.tensor(program(self.pe))


def matmul_split(eng, out, st, mv, start, stop, check=True):
    passes = [(st[0], mv[0]), (st[0], mv[1]), (st[1], mv[0])]
    for i, (a, b) in enumerate(passes):
        ins = eng.matmul(out, a, b, start=start and i == 0, stop=stop and i == 2, skip_group_check=not check)
    return ins


def f32(ap):
    return ap.bitcast(F32)


class Kernel:
    def __init__(self, nc, ctx, a, out, stop_after=None):
        self.nc, self.a, self.out = nc, a, out
        self.p = Program(nc, ctx)
        self.ctx = ctx
        self.fence = []
        self.weight_tiles = {}
        self.phase = ""
        self.stop_after = stop_after

    def share_banks(self, scores=(), tr=(), acc=(), side=(), misc=None):
        ring = lambda ids: Ring([self.banks[i] for i in ids])
        self.scores, self.tr, self.acc, self.side = (ring(i) for i in (scores, tr, acc, side))
        self.misc = self.tr if misc is None else ring(misc)

    def sb(self, name, shape, dt=F32, scope=None):
        return (scope or self.ctx).enter_context(self.nc.sbuf_tensor(self.phase + name, shape, dt))

    def ring(self, name, n, shape, dt=F32, scope=None):
        r = Ring([self.sb(f"{name}{i}", shape, dt, scope) for i in range(n)])
        for s in r.slots:
            s.free = list(self.fence)
        return r

    def split_ring(self, name, n, shape, scope):
        return self.ring(name, n, [P, 2] + shape, F32R, scope)

    def close_phase(self):
        p = self.p
        self.fence = [q.ops[-1] for q in (p.pe, p.act, p.dve, p.pool, p.sp) if q.ops]

    def load(self, stage, dst, src, waits=(), q=None):
        return (q or self.p.sp).do(stage, lambda e: e.dma_start(dst, src), waits, dma=True)

    def cols(self, name):
        at = 0
        for n, c in COLUMNS.items():
            if n == name:
                return self.columns[:, at:at + c]
            at += c
        raise KeyError(name)

    def load_bcast(self, stage, name, src, scope):
        t = self.sb(name, [P, src.shape[0]], F32, scope)
        return t, self.load(stage, t[:], src.partition_broadcast(P), self.fence)

    def split_on(self, q, stage, hi, lo, src, waits):
        if q is self.p.pool:
            h = q.do(stage + "_hi", lambda e: e.tensor_scalar(hi, src, 1.0, 1.0, ALU.mult, ALU.mult), waits)
        else:
            h = q.do(stage + "_hi", lambda e: e.tensor_copy(hi, src), waits)
        return q.do(stage + "_lo", lambda e: e.tensor_tensor(lo, src, f32(hi), ALU.subtract), [h])

    def split_psum(self, stage, hi, lo, src, waits, lo_waits=()):
        h = self.p.act.do(stage + "_hi", lambda e: e.activation(hi, src, ACT.Copy), waits)
        return self.p.dve.do(stage + "_lo", lambda e: e.tensor_tensor(lo, src, f32(hi), ALU.subtract),
                             [h, *lo_waits])

    def split_psum_bias(self, stage, hi, lo, src, bias, waits):
        h = self.p.act.do(stage + "_hi", lambda e: e.activation(hi, src, ACT.Identity, bias=bias), waits)
        return self.p.dve.do(stage + "_lo", lambda e: e.scalar_tensor_tensor(
            out=lo, in0=src, scalar=bias, in1=f32(hi), op0=ALU.add, op1=ALU.subtract), [h])

    def load_weight(self, name, src, scope, q, view=None):
        k, n = src.shape
        c = k // P
        t = self.weight_tiles.pop(name, None) or self.sb(name, [P, 2, c, n], F32R, scope)
        done, cs = None, max(1, self.stage_cols // n)
        for c0 in range(0, c, cs):
            m = min(cs, c - c0)
            s = self.staging.take()
            st = s.t[:, 0:m * n].rearrange("p (c n) -> p c n", c=m)
            ld = self.load(f"staging{self.staging.slots.index(s)}", st,
                           src[c0 * P:(c0 + m) * P, :].rearrange("(c p) n -> p c n", p=P), s.free)
            done = self.split_on(q, "weights", t[:, 0, c0:c0 + m, :], t[:, 1, c0:c0 + m, :], st,
                                 [ld, *self.fence])
            s.free = [done]
        return t, done

    def build(self):
        nc, p, a = self.nc, self.p, self.a
        self.x_tok = self.sb("x_tok", [P, B, D])
        self.ctxT = self.sb("ctxT", [P, 2, DC, B * S], F32R)
        self.x_done = [None] * G
        self.ctxT_done = [None] * G
        self.ident = self.sb("ident", [P, P])
        self.head_mask = self.sb("head_mask", [P, HPT])
        self.columns = self.sb("columns", [P, sum(COLUMNS.values())])
        self.cols_done = self.load("columns", self.columns[:], a["columns"])
        self.ps_pair = self.ctx.enter_context(nc.psum_tensor("ps_scores", [P, 2, 512], F32))
        self.banks = [Slot(self.ps_pair[:, i, :]) for i in range(2)]
        self.banks += [Slot(self.ctx.enter_context(nc.psum_tensor(f"ps_{i}", [P, 512], F32))[:]) for i in range(2, 8)]

        z = p.pool.do("const", lambda e: e.memset(self.ident[:], 0.0))
        m1 = p.pool.do("const", lambda e: e.memset(self.head_mask[:], 1.0))
        self.ident_done = p.pool.do("const", lambda e: e.affine_select(
            out=self.ident[:], in_=self.ident[:], compare_op=ALU.not_equal, fill=1.0, base=0,
            pattern=[[-1, P]], channel_multiplier=1), [z])
        m2 = p.pool.do("const", lambda e: e.affine_select(
            out=self.head_mask[:], in_=self.head_mask[:], compare_op=ALU.is_ge, fill=0.0, base=0,
            pattern=[[-DH, HPT]], channel_multiplier=1), [m1])
        self.mask_done = p.pool.do("const", lambda e: e.affine_select(
            out=self.head_mask[:], in_=self.head_mask[:], compare_op=ALU.is_ge, fill=0.0, base=DH - 1,
            pattern=[[DH, HPT]], channel_multiplier=-1), [m2])

        with ExitStack() as scope:
            self.phase_l0_l1(scope)
            self.close_phase()
        if self.stop_after not in (0, 1):
            with ExitStack() as scope:
                self.phase_l2_attention(scope)
                self.close_phase()
            if self.stop_after != 2:
                with ExitStack() as scope:
                    self.phase_l2_mlp(scope)
                    self.close_phase()
                if self.stop_after != 3:
                    with ExitStack() as scope:
                        self.phase_l3(scope)
                        self.close_phase()
        stores = []
        for g in range(G):
            gb = slice(g * GB, (g + 1) * GB)
            stores.append(self.p.sp.do("store", lambda e, gb=gb: e.dma_start(
                self.out[gb].rearrange("b s d -> s b d"), self.x_tok[:, gb, :]), [self.x_done[g]], dma=True))
        self.p.sp.do("end", lambda e: e.nop(), stores)
        p.emit()

    def norm_transposed(self, g, src, src_done, gain, shift, rms, eps, dst, bufs, after_read=None):
        p = self.p
        st, mv, rs = (bufs[k].take() for k in ("stats", "mv", "rstd"))
        xn = yield from acquire(bufs["xn"])
        xn_t = xn.t[:].rearrange("p (b d) -> p b d", b=GB)
        w = [src_done]
        for b in range(GB):
            i1 = p.dve.do("ln_stats", lambda e, b=b: e.bn_stats(st.t[:, b, :], src(b)), w + st.free)
            if b % 2:
                yield
        for b in range(GB):
            i2 = p.dve.do("ln_aggr", lambda e, b=b: e.bn_aggr(mv.t[:, b, :], st.t[:, b, :]), [i1, *mv.free])
        last = i2
        if rms:
            last = p.dve.do("ln_tiny", lambda e: e.tensor_tensor(rs.t[:, 0, :], mv.t[:, :, 0], mv.t[:, :, 0], ALU.mult),
                            [last, *rs.free])
            last = p.dve.do("ln_tiny", lambda e: e.tensor_tensor(rs.t[:, 1, :], rs.t[:, 0, :], mv.t[:, :, 1], ALU.add), [last])
            var = rs.t[:, 1, :]
        else:
            var = mv.t[:, :, 1]
        last = p.dve.do("ln_tiny", lambda e: e.tensor_scalar(rs.t[:, 2, :], var, eps, None, ALU.add), [last, *rs.free])
        yield
        last = p.act.do("ln_sqrt", lambda e: e.activation(rs.t[:, 3, :], rs.t[:, 2, :], ACT.Sqrt), [last])
        yield
        yield
        last = p.dve.do("ln_tiny", lambda e: e.reciprocal(rs.t[:, 4, :], rs.t[:, 3, :]), [last])
        xw = [last, *xn.free]
        for b in range(GB):
            if rms:
                i3 = p.dve.do("ln_xn", lambda e, b=b: e.tensor_scalar(
                    xn_t[:, b, :], src(b), rs.t[:, 4, b:b + 1], None, ALU.mult), xw)
            else:
                i3 = p.dve.do("ln_xn", lambda e, b=b: e.tensor_scalar(
                    xn_t[:, b, :], src(b), mv.t[:, b, 0:1], rs.t[:, 4, b:b + 1], ALU.subtract, ALU.mult), xw)
            if b % 2:
                yield
        st.free = mv.free = rs.free = [i3]
        if after_read is not None:
            after_read(i3)
        tmp = yield from acquire(bufs["ntmp"])
        tmp_t = tmp.t[:].rearrange("p (c t) -> p c t", c=DC)
        yield
        for c in range(DC):
            bank = yield from acquire(self.tr)

            def tr(e, c=c, bank=bank):
                for b in range(GB):
                    i = e.transpose(bank.t[:, b * S:(b + 1) * S], xn_t[:, b, c * P:(c + 1) * P], self.ident[:])
                return i
            t = p.pe.do("ln_tr", tr, [i3, self.ident_done, *bank.free])
            xf = p.act.do("ln_affine", lambda e, c=c, bank=bank: e.activation(
                tmp_t[:, c, :], bank.t, ACT.Identity, scale=gain[:, c:c + 1],
                bias=shift[:, c:c + 1] if shift is not None else 0.0), [t, *tmp.free])
            bank.free = [xf]
            yield
            done = self.split_on(p.dve, "ln_split", dst.t[:, 0, c, :], dst.t[:, 1, c, :], tmp_t[:, c, :],
                                 [xf, *dst.free])
        xn.free = [t]
        tmp.free = [done]
        yield
        return done

    def norm_bufs(self, scope):
        self.work = self.ring("work", 3, [P, GB * D], F32, scope)
        return {"stats": self.ring("st", 1, [P, GB, 6], F32, scope), "mv": self.ring("mv", 1, [P, GB, 2], F32, scope),
                "rstd": self.ring("rstd", 1, [P, 5, GB], F32, scope), "xn": self.work, "ntmp": self.work}

    def add_bias_rows(self, g, bias, waits):
        x = self.x_tok[:, g * GB:(g + 1) * GB, :]
        return self.p.pool.do("x_bias", lambda e: e.tensor_tensor(
            x, x, bias[:].unsqueeze(1).to_broadcast([P, GB, D]), ALU.add), waits)

    def add_to_x(self, g, banks, tickets, waits):
        for i, (bk, t) in enumerate(zip(banks, tickets)):
            x = self.x_tok[:, g * GB + 2 * i:g * GB + 2 * i + 2, :]
            done = self.p.dve.do("x_add", lambda e, x=x, bk=bk: e.tensor_tensor(
                x, x, bk.t.rearrange("p (b d) -> p b d", b=2), ALU.add), [t, *waits])
            bk.free = [done]
        return done

    def mlp(self, inT, in_done, w1, w1_done, b1, w2, w2_done, func, bufs):
        p = self.p
        banks, parts = None, []

        def down(parts):
            for k, hs, sp in parts:
                def mm(e, k=k, hs=hs):
                    for b in range(GB):
                        o = banks[b // 2].t[:, (b % 2) * D:(b % 2 + 1) * D]
                        i = matmul_split(e, o, [hs.t[:, s, b * S:(b + 1) * S] for s in (0, 1)],
                                         [w2[:, s, k, :] for s in (0, 1)],
                                         k == 0 and b % 2 == 0, k == FC - 1, check=False)
                    return i
                d = p.pe.do("mlp_down", mm, [sp, w2_done, *banks[0].free, *banks[1].free])
                hs.free = [d]
            return d

        for pair in range(FC // 2):
            hid = yield from acquire(bufs["hid"])
            for i in range(2):
                m = 2 * pair + i
                bk = yield from acquire(self.misc)

                def up(e, m=m, bk=bk):
                    for c in range(DC):
                        i = matmul_split(e, bk.t, [w1[:, s, c, m * P:(m + 1) * P] for s in (0, 1)],
                                         [inT.t[:, s, c, :] for s in (0, 1)], c == 0, c == DC - 1)
                    return i
                u = p.pe.do("mlp_up", up, [in_done, w1_done, *bk.free])
                ev = p.dve.do("mlp_up", lambda e, m=m, i=i, bk=bk, hid=hid: e.tensor_scalar(
                    hid.t[:, i * T:(i + 1) * T], bk.t, b1[:, m:m + 1], None, ALU.add), [u, *hid.free])
                bk.free = [ev]
                yield
            if pair == FC // 2 - 1:
                inT.free = [u]
            ge = p.act.do("gelu", lambda e, hid=hid: e.activation(hid.t[:], hid.t[:], func), [ev])
            if parts:
                if banks is None:
                    banks = [(yield from acquire(self.side)), (yield from acquire(self.side))]
                down(parts)
                yield
            parts = []
            for i in range(2):
                hs = yield from acquire(bufs["hid_split"])
                sp = self.split_on(p.dve, "hid", hs.t[:, 0, :], hs.t[:, 1, :], hid.t[:, i * T:(i + 1) * T],
                                   [ge, *hs.free])
                parts.append((2 * pair + i, hs, sp))
                yield
            hid.free = [sp]
        d = down(parts)
        yield
        return banks, d

    def mlp_bufs(self, scope):
        return {"hid": self.work, "hid_split": self.split_ring("hids", 2, [T], scope)}

    def project_cols(self, stage, w, w_done, off, inT, in_done, bias, dst, dst_free):
        p = self.p
        for j in range(DC):
            bk = yield from acquire(self.misc)

            def mm(e, j=j, bk=bk):
                for c in range(DC):
                    i = matmul_split(e, bk.t, [w[:, s, c, off + j * P:off + (j + 1) * P] for s in (0, 1)],
                                     [inT[:, s, c, :] for s in (0, 1)], c == 0, c == DC - 1)
                return i
            m = p.pe.do(stage, mm, [w_done, in_done, *bk.free])
            done = p.act.do(stage, lambda e, j=j, bk=bk: e.activation(
                dst[:, j, :], bk.t, ACT.Identity, bias=bias[:, j:j + 1]), [m, *dst_free])
            bk.free = [done]
            yield
        return m, done

    def project_rows(self, stage, w, w_done, off, inT, in_done, dst, dst_free):
        p = self.p
        for h in range(2):
            bk = yield from acquire(self.misc)

            def mm(e, h=h, bk=bk):
                for b in (2 * h, 2 * h + 1):
                    for c in range(DC):
                        i = matmul_split(e, bk.t[:, (b % 2) * D:(b % 2 + 1) * D],
                                         [inT[:, s, c, b * S:(b + 1) * S] for s in (0, 1)],
                                         [w[:, s, c, off:off + D] for s in (0, 1)], c == 0, c == DC - 1)
                return i
            m = p.pe.do(stage, mm, [w_done, in_done, *bk.free])
            done = p.dve.do(stage, lambda e, h=h, bk=bk: e.tensor_copy(
                dst[:, 2 * h:2 * h + 2, :], bk.t.rearrange("p (b d) -> p b d", b=2)), [m, *dst_free])
            bk.free = [done]
            yield
        return m, done

    def narrow_bufs(self, scope, nsrc, prob, km):
        return {"km": self.ring("km", km, [P, QH, T], F32, scope),
                "prob": self.ring("prob", prob, [P, QH, nsrc, S], F32, scope),
                "probT": self.ring("probT", 2, [P, nsrc, QH, S], F32, scope),
                "smax": self.ring("smax", prob, [P, 4, QH], F32, scope),
                "rsum": self.ring("rsum", 2, [P, GB, NH], F32, scope)}

    def mask_keys(self, qd, ks, bufs):
        slots, done = [], None
        for k, k_done in ks:
            km = yield from acquire(bufs["km"])
            for i in range(QH):
                h = qd * QH + i
                j, hh = h // HPT, h % HPT
                done = self.p.pool.do("mask_keys", lambda e, k=k, km=km, i=i, j=j, hh=hh: e.tensor_scalar(
                    km.t[:, i, :], k.t[:, j, :], self.head_mask[:, hh:hh + 1], 1.0, ALU.mult, ALU.mult),
                    [k_done, self.mask_done, *km.free])
            slots.append(km)
        if qd == NH // QH - 1:
            for k, _ in ks:
                k.free = [done]
        return slots, done

    def narrow_attention(self, g, q, q_done, ks, first_km, project_v, scale, bufs, mask, after_scores=None):
        p, nsrc = self.p, len(ks)
        acc = [(yield from acquire(self.acc)), (yield from acquire(self.acc))]
        rsum = bufs["rsum"].take()
        items = [(qd, b) for qd in range(NH // QH) for b in range(GB)]
        state = {}
        km_of = {0: first_km}
        km_next = {}

        def scores(n):
            qd, b = items[n]
            slots, tick = km_of[qd]
            j = qd * QH // HPT
            banks = [self.scores.take() for _ in range(nsrc)]

            def mm(e):
                for s in range(nsrc):
                    first = True
                    if "keys" in mask and s == 0:
                        e.matmul(banks[s].t, mask["ones"][:], mask["keys"][:, b, :].unsqueeze(1)
                                 .to_broadcast([1, QH, S]), start=True, stop=False)
                        first = False
                    i = e.matmul(banks[s].t, q.t[:, j, b * S:(b + 1) * S], slots[s].t[:, :, b * S:(b + 1) * S],
                                 start=first, stop=True)
                return i
            m = p.pe.do("scores", mm, [q_done, tick, mask["ready"]] + [f for bk in banks for f in bk.free])
            if b == GB - 1:
                for sl in slots:
                    sl.free = [m]
            if n == len(items) - 1:
                q.free = [m]
                if after_scores is not None:
                    after_scores(m)
            state[n] = {"banks": banks, "scores": m}

        def softmax(n):
            qd, b = items[n]
            st = state[n]
            banks, m = st["banks"], st["scores"]
            pr, mx = bufs["prob"].take(), bufs["smax"].take()
            if "mul" in mask:
                mul, add = mask["mul"](b), mask["add"](b)
                r = p.dve.do("mask_mul", lambda e: e.tensor_tensor(
                    pr.t[:, :, 0, :], banks[0].t.rearrange("p (h t) -> p h t", h=QH),
                    mul.unsqueeze(1).to_broadcast([P, QH, S]), ALU.mult), [m, *pr.free])
                banks[0].free = [r]
                r = p.pool.do("mask_add", lambda e: e.tensor_tensor(
                    pr.t[:, :, 0, :], pr.t[:, :, 0, :], add.unsqueeze(1).to_broadcast([P, QH, S]), ALU.add), [r])
            st.update(prob=pr, mx=mx, masked=m if "mul" not in mask else r)

        def exps(n):
            st = state[n]
            banks, r, pr, mx = st["banks"], st["masked"], st["prob"], st["mx"]
            if "mul" in mask:
                src = lambda i: pr.t[:, i, 0, :]
                r = p.dve.do("row_max", lambda e: e.tensor_reduce(
                    mx.t[:, 0, :], pr.t[:, :, 0, :], AX.X, ALU.max), [r, *mx.free])
            else:
                view = self.ps_pair[:, 0:2, :].rearrange("p s (h t) -> p h s t", h=QH)
                src = lambda i: self.ps_pair[:, 0:2, i * S:(i + 1) * S]
                r = p.dve.do("row_max", lambda e: e.tensor_reduce(
                    mx.t[:, 0, :], view, AX.XY, ALU.max), [r, *mx.free])
            r = p.dve.do("row_max", lambda e: e.tensor_scalar(
                mx.t[:, 1, :], mx.t[:, 0, :], -scale, None, ALU.mult), [r])
            for i in range(QH):
                dst = pr.t[:, i, 0, :] if nsrc == 1 else pr.t[:, i, :, :]
                ex = p.act.do("exp", lambda e, i=i, dst=dst: e.activation(
                    dst, src(i), ACT.Exp, bias=mx.t[:, 1, i:i + 1], scale=scale,
                    accum_out=mx.t[:, 2, i:i + 1]), [r, *pr.free])
            if "mul" not in mask:
                for bk in banks:
                    bk.free = [ex]
            st.update(exp=ex)

        def row_sums(n):
            qd, b = items[n]
            mx = state[n]["mx"]
            rc = p.dve.do("row_recip", lambda e: e.reciprocal(
                rsum.t[:, b, qd * QH:(qd + 1) * QH], mx.t[:, 2, :]), [state[n]["exp"], *rsum.free])
            mx.free = [rc]
            return rc

        def transposes(n):
            st = state[n]
            pr, pt = st["prob"], bufs["probT"].take()
            for s in range(nsrc):
                bk = yield from acquire(self.tr)

                def tr(e, s=s, bk=bk):
                    for i in range(QH):
                        ins = e.transpose(bk.t[:, i * S:(i + 1) * S], pr.t[:, i, s, :], self.ident[:])
                    return ins
                t = p.pe.do("prob_tr", tr, [st["exp"], self.ident_done, *bk.free])
                on_dve = s == 1 if nsrc == 2 else n % 2 == 0
                if on_dve:
                    ev = p.dve.do("probT", lambda e, s=s, bk=bk: e.tensor_copy(
                        pt.t[:, s, :, :], bk.t.rearrange("p (h t) -> p h t", h=QH)), [t, *pt.free])
                else:
                    ev = p.act.do("probT", lambda e, s=s, bk=bk: e.activation(
                        pt.t[:, s, :, :], bk.t.rearrange("p (h t) -> p h t", h=QH), ACT.Copy), [t, *pt.free])
                bk.free = [ev]
                st.setdefault("ev", []).append(ev)
            pr.free = [t]
            st["probT"] = pt

        def values(n):
            qd, b = items[n]
            st = state.pop(n)
            pt, bank = st["probT"], acc[b // 2]

            def mm(e):
                for i in range(QH):
                    h = qd * QH + i
                    for s in range(nsrc):
                        ins = e.matmul(bank.t[:, (b % 2) * D + h * DH:(b % 2) * D + (h + 1) * DH],
                                       pt.t[:, s, i, :], vs[s][0].t[:, b, h * DH:(h + 1) * DH],
                                       start=s == 0, stop=s == nsrc - 1)
                return ins
            m = p.pe.do("values", mm, [*st["ev"], *[d for _, d in vs], *bank.free])
            pt.free = [m]
            return m

        N, lag = len(items), 1 if "mul" in mask else 0
        for step in range(N + 3 + lag):
            if step < N:
                qd, b = items[step]
                if qd not in km_of:
                    km_of[qd] = yield from self.mask_keys(qd, ks, bufs)
                scores(step)
                softmax(step)
            if lag <= step < N + lag:
                exps(step - lag)
                yield
            if step == 1:
                vs = yield from project_v
            if 2 + lag <= step < N + 2 + lag:
                m_last = values(step - 2 - lag)
                yield
            if step < N and qd + 1 < NH // QH and qd + 1 not in km_of and bufs["km"].spare() >= nsrc:
                km_of[qd + 1] = yield from self.mask_keys(qd + 1, ks, bufs)
            if 1 + lag <= step < N + 1 + lag:
                sums = row_sums(step - 1 - lag)
                yield from transposes(step - 1 - lag)
                yield
        for v, _ in vs:
            v.free = [m_last]
        ao = yield from acquire(self.work)
        ao_t = ao.t[:].rearrange("p (b d) -> p b d", b=GB)
        for i in range(2):
            nrm = p.dve.do("ao_norm", lambda e, i=i: e.tensor_tensor(
                ao_t[:, 2 * i:2 * i + 2, :].rearrange("p b (h d) -> p (b h) d", d=DH),
                acc[i].t.rearrange("p (h d) -> p h d", d=DH),
                rsum.t[:, 2 * i:2 * i + 2, :].rearrange("p b h -> p (b h)").unsqueeze(2).to_broadcast([P, 2 * NH, DH]),
                ALU.mult), [m_last, sums, *ao.free])
            acc[i].free = [nrm]
        rsum.free = [nrm]
        return ao, nrm

    def out_projection(self, g, w, w_done, ao, ao_done, wide, bv):
        p = self.p
        aoT = yield from acquire(wide)
        ao_t = ao.t[:].rearrange("p (b d) -> p b d", b=GB)
        for c in range(DC):
            bk = yield from acquire(self.tr)

            def tr(e, c=c, bk=bk):
                for b in range(GB):
                    ins = e.transpose(bk.t[:, b * S:(b + 1) * S], ao_t[:, b, c * P:(c + 1) * P], self.ident[:])
                return ins
            t = p.pe.do("ao_tr", tr, [ao_done, *bk.free])
            done = self.split_psum_bias("ao", aoT.t[:, 0, c, :], aoT.t[:, 1, c, :], bk.t, bv[:, c:c + 1],
                                        [t, *aoT.free])
            bk.free = [done]
            yield
        ao.free = [t]
        banks = [(yield from acquire(self.side)), (yield from acquire(self.side))]
        for b in range(GB):
            def mm(e, b=b):
                for c in range(DC):
                    i = matmul_split(e, banks[b // 2].t[:, (b % 2) * D:(b % 2 + 1) * D],
                                     [aoT.t[:, s, c, b * S:(b + 1) * S] for s in (0, 1)],
                                     [w[:, s, c, :] for s in (0, 1)], c == 0, c == DC - 1)
                return i
            m = p.pe.do("out_proj", mm, [done, w_done, *banks[0].free, *banks[1].free])
            if b % 2:
                yield
        aoT.free = [m]
        return banks, m

    def phase_l0_l1(self, scope):
        self.phase = "l01_"
        p, a = self.p, self.a
        sb = lambda n, s, dt=F32: self.sb(n, s, dt, scope)
        wqT, wkT, wvT = (sb(n, [P, m]) for n, m in (("wqT", D0), ("wkT", D0), ("wvT", P)))
        bq0, bk0, bv0 = sb("bq0", [D0, 1]), sb("bk0", [D0, 1]), sb("bv0", [P, 1])
        loads = [self.load("l0_small", t[:], s) for t, s in (
            (wqT, a["L0_WqT"]), (wkT, a["L0_WkT"]), (wvT, a["L0_WvT"]),
            (bq0, a["L0_xattn_bq"].unsqueeze(1)), (bk0, a["L0_xattn_bk"].unsqueeze(1)),
            (bv0, a["L0_xattn_bv"].unsqueeze(1)))]
        small = loads[-1]
        p.act.do("columns_ready", lambda e: e.nop(), [self.cols_done])
        x_loaded, ctx_loaded = [], []
        self.share_banks(scores=(0, 1), tr=(2, 3), acc=(4, 5), misc=(6, 7))

        def load_group(g):
            gb = slice(g * GB, (g + 1) * GB)
            x_loaded.append(self.load(f"load_x{g}", self.x_tok[:, gb, :], a["x"][gb].rearrange("b s d -> s b d")))
            s = ctx_tok.take()
            ctx_loaded.append((s, self.load(f"load_ctx{g}", s.t[:], a["ctx_2048"][gb].rearrange("b s d -> s b d"), s.free)))
        self.stage_cols = 1024
        for n, shape in (("l1_wq", [DC, D]), ("l1_wo", [DC, D]), ("l1_w1", [DC, F]), ("l1_w2", [FC, D])):
            self.weight_tiles[n] = sb(n, [P, 2] + shape, F32R)
        wkv = sb("l1_wkv", [P, 2, 2, DC, D], F32R)
        qb, bk1, bv1, pw, b1 = (self.cols(n) for n in (
            "L1_xattn_q_b", "L1_kv_b_k", "L1_kv_b_v", "L1_xattn_postnorm_w", "L1_xattn_mlp_b1"))
        ob, _ = self.load_bcast("l1_bias", "l1_ob", a["L1_xattn_out_b"], scope)
        b2, bias = self.load_bcast("l1_bias", "l1_b2", a["L1_xattn_mlp_b2"], scope)
        ones = sb("ones_row", [1, P], F32R)
        one = p.dve.do("key_mask", lambda e: e.tensor_scalar(ones[:], wvT[0:1, :], 0.0, 1.0, ALU.mult, ALU.add), [small])
        l0_scope = ExitStack()
        self.staging = self.ring("staging", 2, [P, self.stage_cols], F32, l0_scope)
        ctx_tok = self.ring("ctx_tok", 2, [P, GB, D], F32, l0_scope)
        load_group(0)
        load_group(1)
        wq, wq_done = self.load_weight("l1_wq", a["L1_xattn_q_w"], scope, p.pool)
        s = self.staging.take()
        stg = s.t[:].rearrange("p (c n s) -> p c n s", c=DC, s=2)
        ld = self.load(f"staging{self.staging.slots.index(s)}", s.t[:].rearrange("p (c n) -> p c n", c=DC),
                       a["L1_xattn_kv_w"].rearrange("(c p) n -> p c n", p=P), s.free)
        for i in range(2):
            wkv_done = self.split_on(p.pool, "weights", wkv[:, i, 0], wkv[:, i, 1], stg[:, :, :, i], [ld])
        s.free = [wkv_done]
        wk, wv = wkv[:, 0], wkv[:, 1]
        wo, wo_done = self.load_weight("l1_wo", a["L1_xattn_out_w"], scope, p.pool)
        w1, w1_done = self.load_weight("l1_w1", a["L1_xattn_mlp_w1"], scope, p.pool)
        w2, w2_done = self.load_weight("l1_w2", a["L1_xattn_mlp_w2"], scope, p.pool)
        l0 = {k: self.ring("l0_" + k, n, s, F32, l0_scope) for k, n, s in (
            ("qk", 2, [D0, 2, D]), ("v", 4, [P, 2, P]), ("prob", 2, [P, 2, D]), ("probT", 2, [P, 2, D]),
            ("mx", 2, [P, 4, 2]))}
        def l0_project(st):
            b, g = st["b"], st["b"] // GB
            x1, x2 = self.x_tok[:, b, :], ctx_loaded[g][0].t[:, b % GB, :]
            bk, qk = self.misc.take(), l0["qk"].take()

            def mm(e):
                e.matmul(bk.t[0:D0, 0:D], wqT[:], x1, start=True, stop=True)
                return e.matmul(bk.t[0:D0, D:2 * D], wkT[:], x2, start=True, stop=True)
            m = p.pe.do("l0_qk", mm, [small, x_loaded[g], ctx_loaded[g][1], *bk.free])
            for i, bb in enumerate((bq0, bk0)):
                st["qk_done"] = p.act.do("l0_qk", lambda e, i=i, bb=bb: e.activation(
                    qk.t[:, i, :], bk.t[0:D0, i * D:(i + 1) * D], ACT.Identity, bias=bb[:, 0:1]), [m, *qk.free])
            bk.free = [st["qk_done"]]
            st["qk"] = qk
            bv_bank, v = self.misc.take(), l0["v"].take()

            def mm_v(e):
                for c in range(2):
                    i = e.matmul(bv_bank.t[:, c * P:(c + 1) * P], x2[:, c * P:(c + 1) * P], wvT[:], start=True, stop=True)
                for c in range(2):
                    i = e.transpose(bv_bank.t[:, (2 + c) * P:(3 + c) * P], x2[:, c * P:(c + 1) * P], self.ident[:])
                return i
            m = p.pe.do("l0_v", mm_v, [self.ident_done, *bv_bank.free])
            if b % GB == GB - 1:
                ctx_loaded[g][0].free = [m]
            st["v_done"] = p.dve.do("l0_v", lambda e: e.tensor_copy(
                v.t[:].rearrange("p c n -> p (c n)"), bv_bank.t[:, 0:2 * P]), [m, *v.free])
            st["v"] = v
            h = slice(b * S, (b + 1) * S)
            src = bv_bank.t[:, 2 * P:4 * P].rearrange("p (c n) -> p c n", c=2)
            self.ctxT_done[g] = self.split_psum("ctxT", self.ctxT[:, 0, :, h], self.ctxT[:, 1, :, h], src,
                                                [m, st["v_done"]])
            bv_bank.free = [self.ctxT_done[g]]

        def l0_scores(st):
            bk, qk, pr, mx = self.scores.take(), st["qk"], l0["prob"].take(), l0["mx"].take()

            def mm(e):
                for c in range(2):
                    i = e.matmul(bk.t[:, c * D:(c + 1) * D], qk.t[:, 0, c * P:(c + 1) * P], qk.t[:, 1, :],
                                 start=True, stop=True)
                return i
            m = p.pe.do("l0_scores", mm, [st["qk_done"], *bk.free])
            qk.free = [m]
            r = p.dve.do("l0_max", lambda e: e.tensor_reduce(
                mx.t[:, 0, :], bk.t.rearrange("p (c n) -> p c n", c=2), AX.X, ALU.max, negate=True), [m, *mx.free])
            for c in range(2):
                ex = p.act.do("l0_exp", lambda e, c=c: e.activation(
                    pr.t[:, c, :], bk.t[:, c * D:(c + 1) * D], ACT.Exp, bias=mx.t[:, 0, c:c + 1],
                    accum_out=mx.t[:, 1, c:c + 1]), [r, *pr.free])
            bk.free = [ex]
            rc = p.dve.do("l0_recip", lambda e: e.reciprocal(mx.t[:, 2, :], mx.t[:, 1, :]), [ex])
            nm = p.pool.do("l0_norm", lambda e: e.tensor_tensor(
                pr.t[:], pr.t[:], mx.t[:, 2, :].unsqueeze(2).to_broadcast([P, 2, D]), ALU.mult), [rc])
            mx.free = [nm]
            st.update(prob=pr, prob_done=nm)

        def l0_values(st):
            b = st["b"]
            bk, pr, pt = self.tr.take(), st["prob"], l0["probT"].take()

            def tr(e):
                for m in range(2):
                    for n in range(2):
                        i = e.transpose(bk.t[:, m * D + n * P:m * D + (n + 1) * P],
                                        pr.t[:, n, m * P:(m + 1) * P], self.ident[:])
                return i
            t = p.pe.do("l0_tr", tr, [st["prob_done"], *bk.free])
            pr.free = [t]
            ev = p.dve.do("l0_probT", lambda e: e.tensor_copy(pt.t[:].rearrange("p m n -> p (m n)"), bk.t), [t, *pt.free])
            bk.free = [ev]
            st.update(probT=pt, probT_done=ev)

        def l0_out(st):
            b, bk, pt, v = st["b"], self.acc.take(), st["probT"], st["v"]

            def mm(e):
                for m in range(2):
                    i = e.matmul(bk.t[:, 0:D], v.t[:, m, :], pt.t[:, m, :], start=m == 0, stop=m == 1)
                return i
            m = p.pe.do("l0_out", mm, [st["probT_done"], st["v_done"], *bk.free])
            pt.free = v.free = [m]
            x = self.x_tok[:, b, :]
            done = p.dve.do("l0_x", lambda e: e.scalar_tensor_tensor(
                out=x, in0=bk.t[:, 0:D], scalar=bv0[:, 0:1], in1=x, op0=ALU.add, op1=ALU.add), [m])
            bk.free = [done]
            self.x_done[b // GB] = done

        def l0_group(g):
            sts = [{"b": g * GB + i} for i in range(GB)]
            for step in range(GB + 3):
                for off, f in ((0, l0_project), (1, l0_scores), (3, l0_out), (2, l0_values)):
                    if 0 <= step - off < GB:
                        f(sts[step - off])
            if g + 2 < G:
                load_group(g + 2)

        def l1_begin(g):
            xs = yield from acquire(wide)
            for c in range(DC):
                bk = yield from acquire(self.tr)

                def tr(e, c=c, bk=bk):
                    for b in range(GB):
                        i = e.transpose(bk.t[:, b * S:(b + 1) * S], self.x_tok[:, g * GB + b, c * P:(c + 1) * P], self.ident[:])
                    return i
                t = p.pe.do("l1_xT", tr, [self.x_done[g], *bk.free])
                x_tdone = self.split_psum("l1_xT", xs.t[:, 0, c, :], xs.t[:, 1, c, :], bk.t, [t, *xs.free])
                bk.free = [x_tdone]
                yield
            mi, ky = (yield from acquire(mask_i)), (yield from acquire(keys))
            ld = self.load("l1_mask", mi.t[:], a["mask_BxS2_ik0"][g * GB:(g + 1) * GB].unsqueeze(0), mi.free)
            q = yield from acquire(qT)
            _, q_done = yield from self.project_cols("l1_q", wq, wq_done, 0, xs.t, x_tdone, qb, q.t, q.free + [bias])
            ks = []
            for i, (src, done) in enumerate(((ctx_of(g), self.ctxT_done[g]), (xs.t, x_tdone))):
                k = yield from acquire(kT[i])
                _, k_done = yield from self.project_cols("l1_k", wk, wkv_done, 0, src, done, bk1, k.t, k.free)
                ks.append((k, k_done))
            kmask = p.dve.do("key_mask", lambda e: e.tensor_scalar(
                ky.t[:], mi.t[:], 0.0, NEG, ALU.is_equal, ALU.mult), [ld, *ky.free])
            mi.free = [kmask]
            yield
            km = yield from self.mask_keys(0, ks, ab)
            begun[g] = dict(xs=xs, xs_done=x_tdone, q=q, q_done=q_done, ks=ks, km=km, tr=t, ky=ky,
                            mask={"keys": ky.t, "ones": ones, "ready": kmask})

        def l1_values(g):
            st = begun[g]
            vs = []
            for i, (src, done) in enumerate(((ctx_of(g), self.ctxT_done[g]), (st["xs"].t, st["xs_done"]))):
                v = yield from acquire(vv[i])
                m, v_done = yield from self.project_rows("l1_v", wv, wkv_done, 0, src, done, v.t, v.free)
                vs.append((v, v_done))
            st["xs"].free = [m]
            return vs

        def l1_attention(g):
            st = begun[g]

            def mask_read(m):
                st["ky"].free = [m]
            st["ao"] = yield from self.narrow_attention(
                g, st["q"], st["q_done"], st["ks"], st["km"], l1_values(g), 1.0 / DH, ab, st["mask"], mask_read)

        def l1_end(g):
            st = begun.pop(g)
            banks, m = yield from self.out_projection(g, wo, wo_done, *st["ao"], wide, bv1)
            ys = yield from acquire(self.work)
            ys_t = ys.t[:].rearrange("p (b d) -> p b d", b=GB)
            xg = self.x_tok[:, g * GB:(g + 1) * GB, :]
            y0 = p.pool.do("l1_y", lambda e: e.tensor_tensor(
                ys_t, xg, ob[:].unsqueeze(1).to_broadcast([P, GB, D]), ALU.add), [self.x_done[g], bias, *ys.free])
            yield
            for i in range(2):
                yd = p.dve.do("l1_y", lambda e, i=i, banks=banks: e.tensor_tensor(
                    ys_t[:, 2 * i:2 * i + 2, :], ys_t[:, 2 * i:2 * i + 2, :],
                    banks[i].t.rearrange("p (b d) -> p b d", b=2), ALU.add), [y0, m])
                banks[i].free = [yd]
            xb = self.add_bias_rows(g, b2, [y0, st["tr"]])

            def y_read(op):
                ys.free = [op]
            hs = yield from acquire(wide)
            h_done = yield from self.norm_transposed(g, lambda b: ys_t[:, b, :], yd, pw, None, True, 1e-6, hs, nb, y_read)
            banks, m = yield from self.mlp(hs, h_done, w1, w1_done, b1, w2, w2_done, ACT.Gelu_apprx_tanh, mb)
            self.x_done[g] = self.add_to_x(g, banks, [m, m], [xb])

        for g in range(G):
            l0_group(g)
        l0_scope.close()
        self.close_phase()
        if self.stop_after == 0:
            return
        self.share_banks(scores=(0, 1), tr=(2, 3), acc=(4, 5), side=(6, 7))
        nb, mb, ab = self.norm_bufs(scope), self.mlp_bufs(scope), self.narrow_bufs(scope, 2, 2, 3)
        wide = self.split_ring("wide", 2, [DC, T], scope)
        qT = self.ring("qT", 2, [P, DC, T], F32, scope)
        kT = [self.ring(f"kT{i}", 1, [P, DC, T], F32, scope) for i in range(2)]
        vv = [self.ring(f"vv{i}", 1, [P, GB, D], F32, scope) for i in range(2)]
        mask_i = self.ring("mask_i", 1, [1, GB, S], I32, scope)
        keys = self.ring("mask_keys", 1, [1, GB, S], F32R, scope)
        ctx_of = lambda g: self.ctxT[:, :, :, g * T:(g + 1) * T]
        begun = {}
        run(l1_begin(0))
        for g in range(G):
            side = [l1_end(g - 1)] if g > 0 else []
            side += [l1_begin(g + 1)] if g + 1 < G else []
            interleave(l1_attention(g), chain(*side), L1_RATE[g])
        run(l1_end(G - 1))

    def phase_l2_attention(self, scope):
        self.phase = "l2a_"
        p, a = self.p, self.a
        sb = lambda n, s, dt=F32: self.sb(n, s, dt, scope)
        hT = [self.split_ring(f"l2_hT{g}", 1, [DC, T], scope).slots[0] for g in range(G)]
        W = {k: self.ring("l2_" + k, 2, [P, 2, DC, HG * K2], F32R, scope) for k in ("wq", "wk", "wv")}
        W["wo"] = self.ring("l2_wo", 2, [P, 2, HG, D], F32R, scope)
        staging = self.ring("l2_staging", 2, [P, DC * HG * K2], F32, scope)
        V = self.ring("l2_V", 2, [P, GB, HG * K2], F32, scope)
        QT = self.ring("l2_qT", 2, [P, T], F32, scope)
        KT = self.ring("l2_kT", 2, [P, GB, S + 2], F32, scope)
        PR = self.ring("l2_prob", 2, [P, GB, S + 2], F32, scope)
        PT = self.ring("l2_probT", 1, [P, T], F32, scope)
        AO = self.split_ring("l2_ao", 1, [T], scope)
        MX = self.ring("l2_mx", 2, [P, 4, GB], F32, scope)
        pb = sb("l2_pb", [P, B, H2])
        pbT = self.ring("l2_pbT", 1, [H2, GB, S], F32, scope)
        BW = sb("l2_bw", [H2, D])
        dv = sb("l2_dv", [P, H2])
        dsel = sb("l2_dsel", [P, H2, H2])
        nb = {"stats": self.ring("st2_", 1, [P, GB, 6], F32, scope), "mv": self.ring("mv2_", 1, [P, GB, 2], F32, scope),
              "rstd": self.ring("rs2_", 1, [P, 5, GB], F32, scope)}
        self.share_banks(scores=(0, 1), tr=(2, 3), acc=(4, 5), misc=(6, 7))
        proj = self.misc
        scale = float(K2) ** -0.5
        cols = {}
        for i in ("1", "2"):
            for n in (f"ln{i}_scale", f"ln{i}_offset", f"bq{i}", f"bk{i}", f"bv{i}", f"bias_k{i}", f"bias_v{i}"):
                cols[n] = self.cols("L2_xattn_" + n)
            cols["bo" + i], cols_done = self.load_bcast("l2_bias", "l2_bo" + i, a["L2_xattn_bo" + i], scope)

        wslots = {}

        def load_weights(at, hg):
            n = str(at + 1)
            got = {}
            for k in ("wk", "wv", "wq", "wo"):
                w, s = W[k].take(), staging.take()
                if k == "wo":
                    src = a["L2_xattn_wo" + n][hg * HG * K2:(hg + 1) * HG * K2, :].rearrange("(c p) n -> p c n", p=P)
                    st = s.t[:].rearrange("p (c n) -> p c n", c=HG)
                else:
                    src = a[f"L2_xattn_{k}{n}"].rearrange("(c p) n -> p c n", p=P)[:, :, hg * HG * K2:(hg + 1) * HG * K2]
                    st = s.t[:].rearrange("p (c n) -> p c n", c=DC)
                ld = self.load(f"l2_staging{staging.slots.index(s)}", st, src, s.free)
                done = self.split_on(p.pool, "l2_weights", w.t[:, 0], w.t[:, 1], st, [ld, *w.free])
                s.free = [done]
                got[k] = (w, done)
            wslots[at, hg] = got

        def normalise(at, g):
            n = str(at + 1)
            bufs = dict(nb, xn=staging, ntmp=staging)

            def add_bias(read):
                self.x_done[g] = self.add_bias_rows(g, cols["bo" + n], [read, cols_done])
            hT_done[g] = run(self.norm_transposed(
                g, lambda b: self.x_tok[:, g * GB + b, :], self.x_done[g], cols["ln" + n + "_scale"],
                cols["ln" + n + "_offset"], False, 1e-5, hT[g], bufs, add_bias))

        hT_done = [None] * G
        items = [(at, hg, g, h) for at in range(2) for hg in range(H2 // HG) for g in range(G) for h in range(HG)]
        N = len(items)
        st = [dict() for _ in items]
        vslot = {}
        acc_now = {}
        bw_done = {}

        def bias_rows(at, hg):
            n = str(at + 1)
            w, wd = wslots[at, hg]["wo"]
            if hg == 0:
                d = p.dve.do("l2_dv", lambda e: e.tensor_tensor(dv[:], cols["bias_v" + n], cols["bv" + n], ALU.subtract),
                             [cols_done])
                z = p.dve.do("l2_dv", lambda e: e.memset(dsel[:], 0.0), bw_free["dsel"])
                for h in range(H2):
                    d = p.dve.do("l2_dv", lambda e, h=h: e.tensor_copy(dsel[:, h, h:h + 1], dv[:, h:h + 1]), [d, z])
                bw_free["dv"] = d
            bk = self.misc.take()

            def mm(e):
                for i in range(HG):
                    for s in (0, 1):
                        ins = e.matmul(bk.t[0:H2, 0:D], dsel[:, hg * HG + i, :], f32(w.t[:, s, i, :]),
                                       start=i == 0 and s == 0, stop=i == HG - 1 and s == 1)
                return ins
            m = p.pe.do("l2_bw", mm, [wd, bw_free["dv"], *bk.free])
            bw_free["dsel"] = [m]
            if hg == 0:
                b = p.dve.do("l2_bw", lambda e: e.tensor_copy(BW[:], bk.t[0:H2, 0:D]), [m, *bw_free["bw"]])
            else:
                b = p.dve.do("l2_bw", lambda e: e.tensor_tensor(BW[:], BW[:], bk.t[0:H2, 0:D], ALU.add), [m, bw_done[at]])
            bk.free = [b]
            bw_done[at] = b
        bw_free = {"dsel": list(self.fence), "bw": list(self.fence)}

        def project(n, what):
            if what == "v":
                tgt, b = n - n % HG + HG, n % HG
                if tgt >= N:
                    return
                at, hg, g, _ = items[tgt]
                if b == 0:
                    if (at, hg) not in wslots:
                        load_weights(at, hg)
                    vslot[tgt] = [V.take(), None]
                v = vslot[tgt][0]
                w, wd = wslots[at, hg]["wv"]
                bk = proj.take()

                def mm(e):
                    for c in range(DC):
                        t0 = g * T + b * S
                        i = matmul_split(e, bk.t, [self.ctxT[:, s, c, t0:t0 + S] for s in (0, 1)],
                                         [w.t[:, s, c, :] for s in (0, 1)], c == 0, c == DC - 1)
                    return i
                m = p.pe.do("l2_v", mm, [wd, *bk.free])
                ev = p.dve.do("l2_v", lambda e: e.tensor_copy(v.t[:, b, :], bk.t), [m, *v.free])
                bk.free = [ev]
                vslot[tgt][1] = ev
                if b == GB - 1 and g == G - 1:
                    w.free = [m]
                return
            at, hg, g, h = items[n]
            nm = str(at + 1)
            if what == "q":
                w, wd = wslots[at, hg]["wq"]
                bk, q = proj.take(), QT.take()

                def mm(e):
                    for c in range(DC):
                        i = matmul_split(e, bk.t, [w.t[:, s, c, h * K2:(h + 1) * K2] for s in (0, 1)],
                                         [hT[g].t[:, s, c, :] for s in (0, 1)], c == 0, c == DC - 1)
                    return i
                m = p.pe.do("l2_q", mm, [wd, hT_done[g], *bk.free])
                hd = hg * HG + h
                st[n]["q_done"] = p.act.do("l2_q", lambda e: e.activation(
                    q.t[:], bk.t, ACT.Identity, bias=cols["bq" + nm][:, hd:hd + 1]), [m, *q.free])
                bk.free = [st[n]["q_done"]]
                st[n]["q"] = q
                if hg == H2 // HG - 1 and h == HG - 1:
                    hT[g].free = [m]
            else:
                w, wd = wslots[at, hg]["wk"]
                bk, k = proj.take(), KT.take()

                def mm(e):
                    for c in range(DC):
                        i = matmul_split(e, bk.t, [w.t[:, s, c, h * K2:(h + 1) * K2] for s in (0, 1)],
                                         [self.ctxT[:, s, c, g * T:(g + 1) * T] for s in (0, 1)], c == 0, c == DC - 1)
                    return i
                m = p.pe.do("l2_k", mm, [wd, *bk.free])
                hd = hg * HG + h
                st[n]["k_done"] = p.act.do("l2_k", lambda e: e.activation(
                    k.t[:, :, 0:S], bk.t.rearrange("p (b t) -> p b t", b=GB), ACT.Identity,
                    bias=cols["bk" + nm][:, hd:hd + 1]), [m, *k.free])
                bk.free = [st[n]["k_done"]]
                st[n]["bk_done"] = p.pool.do("l2_bias_k", lambda e: e.tensor_copy(
                    k.t[:, :, S:S + 2], cols["bias_k" + nm][:, hd:hd + 1].unsqueeze(2).to_broadcast([P, GB, 2])), k.free)
                st[n]["k"] = k
            if h == HG - 1 and g == G - 1:
                w.free = [m]

        def scores(n):
            s = st[n]
            q, k = s["q"], s["k"]
            banks = [self.scores.take() for _ in range(2)]
            pr, mx = PR.take(), MX.take()
            for i, bk in enumerate(banks):
                def mm(e, i=i, bk=bk):
                    for b in (2 * i, 2 * i + 1):
                        ins = e.matmul(bk.t[:, (b % 2) * (S + 2):(b % 2 + 1) * (S + 2)], q.t[:, b * S:(b + 1) * S],
                                       k.t[:, b, :], start=True, stop=True)
                    return ins
                m = p.pe.do("l2_scores", mm, [s["q_done"], s["k_done"], s["bk_done"], *bk.free])
                r = p.dve.do("l2_max", lambda e, i=i, bk=bk: e.tensor_reduce(
                    mx.t[:, 0, 2 * i:2 * i + 2], bk.t[:, 0:2 * (S + 2)].rearrange("p (b t) -> p b t", b=2)[:, :, 0:S + 1],
                    AX.X, ALU.max), [m, *mx.free])
            q.free = k.free = [m]
            r = p.dve.do("l2_max", lambda e: e.tensor_scalar(mx.t[:, 1, :], mx.t[:, 0, :], -scale, None, ALU.mult), [r])
            for b in range(GB):
                ex = p.act.do("l2_exp", lambda e, b=b: e.activation(
                    pr.t[:, b, 0:S + 1], banks[b // 2].t[:, (b % 2) * (S + 2):(b % 2) * (S + 2) + S + 1], ACT.Exp,
                    bias=mx.t[:, 1, b:b + 1], scale=scale, accum_out=mx.t[:, 2, b:b + 1]), [r, *pr.free])
                banks[b // 2].free = [ex]
            s.update(prob=pr, exp=ex, mx=mx)

        def normalise_rows(n):
            s = st[n]
            pr, mx = s["prob"], s["mx"]
            rc = p.dve.do("l2_recip", lambda e: e.reciprocal(mx.t[:, 3, :], mx.t[:, 2, :]), [s["exp"]])
            nm = p.pool.do("l2_norm", lambda e: e.tensor_tensor(
                pr.t[:, :, 0:S + 1], pr.t[:, :, 0:S + 1], mx.t[:, 3, :].unsqueeze(2).to_broadcast([P, GB, S + 1]), ALU.mult),
                [rc])
            at, hg, g, h = items[n]
            hd = hg * HG + h
            pbc = p.pool.do("l2_pb", lambda e: e.tensor_copy(
                pb[:, g * GB:(g + 1) * GB, hd:hd + 1], pr.t[:, :, S:S + 1]), [nm, *pb_free[g]])
            mx.free = [nm]
            s.update(prob_done=nm, pb_done=pbc)
        pb_free = [list(self.fence) for _ in range(G)]

        def transposes(n):
            s = st[n]
            bk, pt, pr = tr_ring.take(), PT.take(), s["prob"]

            def tr(e):
                for b in range(GB):
                    i = e.transpose(bk.t[:, b * S:(b + 1) * S], pr.t[:, b, 0:S], self.ident[:])
                return i
            t = p.pe.do("l2_tr", tr, [s["prob_done"], *bk.free])
            pr.free = [t, s["pb_done"]]
            ev = p.dve.do("l2_probT", lambda e: e.tensor_copy(pt.t[:], bk.t), [t, *pt.free])
            bk.free = [ev]
            s.update(probT=pt, probT_done=ev)
        tr_ring, pv_ring = Ring(self.tr.slots[0:1]), Ring(self.tr.slots[1:2])

        def values(n):
            at, hg, g, h = items[n]
            s = st[n]
            bk, ao, pt = pv_ring.take(), AO.take(), s["probT"]
            v, vd = vslot[n - h]

            def mm(e):
                for b in range(GB):
                    i = e.matmul(bk.t[:, b * S:(b + 1) * S], v.t[:, b, h * K2:(h + 1) * K2], pt.t[:, b * S:(b + 1) * S],
                                 start=True, stop=True)
                return i
            m = p.pe.do("l2_values", mm, [s["probT_done"], vd, *bk.free])
            pt.free = [m]
            if h == HG - 1:
                v.free = [m]
            hd = hg * HG + h
            done = self.split_psum_bias("l2_ao", ao.t[:, 0, :], ao.t[:, 1, :], bk.t, cols["bv" + str(at + 1)][:, hd:hd + 1],
                                        [m, *ao.free])
            bk.free = [done]
            s.update(ao=ao, ao_done=done)

        def output(n):
            at, hg, g, h = items[n]
            s = st[n]
            ao = s["ao"]
            w, wd = wslots[at, hg]["wo"]
            if h == 0:
                acc_now[0] = [self.acc.take() for _ in range(2)]
                if g == 0:
                    bias_rows(at, hg)
            banks = acc_now[0]
            last = hg == H2 // HG - 1
            if last and h == HG - 1:
                bk, pt = self.misc.take(), pbT.take()

                def tr(e):
                    for b in range(GB):
                        i = e.transpose(bk.t[0:H2, b * S:(b + 1) * S], pb[:, g * GB + b, :], self.ident[:])
                    return i
                t = p.pe.do("l2_pbT", tr, [s["pb_done"], *bk.free])
                pb_free[g] = [t]
                ev = p.act.do("l2_pbT", lambda e: e.activation(
                    pt.t[:].rearrange("h b t -> h (b t)"), bk.t[0:H2, :], ACT.Copy), [t, *pt.free])
                bk.free = [ev]

            def mm(e):
                for b in range(GB):
                    i = matmul_split(e, banks[b // 2].t[:, (b % 2) * D:(b % 2 + 1) * D],
                                     [ao.t[:, x, b * S:(b + 1) * S] for x in (0, 1)], [w.t[:, x, h, :] for x in (0, 1)],
                                     h == 0 and b % 2 == 0, h == HG - 1 and not last, check=False)
                return i
            m = p.pe.do("l2_out", mm, [s["ao_done"], wd, *banks[0].free, *banks[1].free])
            ao.free = [m]
            if g == G - 1 and h == HG - 1:
                w.free = [m]
            if last and h == HG - 1:
                def mm(e):
                    for b in range(GB):
                        i = e.matmul(banks[b // 2].t[:, (b % 2) * D:(b % 2 + 1) * D], pt.t[:, b, :], BW[:],
                                     start=False, stop=True, skip_group_check=True)
                    return i
                m = p.pe.do("l2_out_bias", mm, [ev, bw_done[at]])
                pt.free = [m]
                bw_free["bw"] = [m]
            if h == HG - 1:
                self.x_done[g] = self.add_to_x(g, banks, [m, m], [self.x_done[g]])
                if last and at == 0:
                    normalise(1, g)
            nxt = (at, hg + 1) if not last else (at + 1, 0)
            if g == 1 and h == 0 and nxt[0] < 2 and nxt not in wslots:
                load_weights(*nxt)
            st[n] = None

        load_weights(0, 0)
        for g in range(G):
            normalise(0, g)
        for n in range(-HG, -2):
            project(n, "v")
        for step in range(N + 3):
            if 1 <= step <= N:
                scores(step - 1)
            if step < N:
                project(step, "q")
            if 1 <= step <= N:
                normalise_rows(step - 1)
            if 2 <= step <= N + 1:
                values(step - 2)
            if step < N:
                project(step, "k")
            project(step - 2, "v")
            if 2 <= step <= N + 1:
                output(step - 2)
            if 1 <= step <= N:
                transposes(step - 1)

    def phase_l2_mlp(self, scope):
        self.phase = "l2m_"
        p, a = self.p, self.a
        self.stage_cols = 1024
        self.staging = self.ring("staging_m", 2, [P, self.stage_cols], F32, scope)
        cols = {n: self.cols("L2_xattn_" + n)
                for n in ("ln_mlp_scale", "ln_mlp_offset", "b_fc1")}
        b2, cd = self.load_bcast("l2m_bias", "l2m_b2", a["L2_xattn_b_fc2"], scope)
        w1, w1_done = self.load_weight("l2_w1", a["L2_xattn_w_fc1"], scope, p.dve)
        w2, w2_done = self.load_weight("l2_w2", a["L2_xattn_w_fc2"], scope, p.dve)
        nb, mb = self.norm_bufs(scope), self.mlp_bufs(scope)
        hT = self.split_ring("l2m_hT", 2, [DC, T], scope)
        self.share_banks(tr=(2, 3), side=(4, 5, 0, 1), misc=(6, 7))
        ready = {}

        def norm(g):
            def add_bias(read):
                self.x_done[g] = self.add_bias_rows(g, b2, [read, cd])
            hs = yield from acquire(hT)
            ready[g] = (hs, (yield from self.norm_transposed(
                g, lambda b: self.x_tok[:, g * GB + b, :], self.x_done[g], cols["ln_mlp_scale"],
                cols["ln_mlp_offset"], False, 1e-5, hs, nb, add_bias)))

        def mlp(g):
            banks, m = yield from self.mlp(*ready[g], w1, w1_done, cols["b_fc1"], w2, w2_done, ACT.Gelu, mb)
            self.x_done[g] = self.add_to_x(g, banks, [m, m], [self.x_done[g]])
        run(norm(0))
        for g in range(G):
            interleave(mlp(g), norm(g + 1) if g + 1 < G else iter(()), 0.5)

    def phase_l3(self, scope):
        self.phase = "l3_"
        p, a = self.p, self.a
        sb = lambda n, s, dt=F32: self.sb(n, s, dt, scope)
        self.stage_cols = 1024
        self.share_banks(scores=(0, 1), tr=(2, 3), acc=(4, 5), side=(6, 7))
        cols = {n: self.cols("L3_xattn_" + n)
                for n in ("ln1_s", "ln1_b", "ln2_s", "ln2_b", "ln3_s", "ln3_b", "b_qkv", "b_q", "b_kv", "b1")}
        rows = {n: self.load_bcast("l3_bias", "l3_" + n, a["L3_xattn_" + n], scope)[0] for n in ("b_ao", "b_co", "b2")}
        mask1 = sb("mask1", [P, 2, S])
        cd = self.load("l3_bias", mask1[:, 0, :], a["mask_1x1xSxS2_fc1"][0, 0], self.fence)
        MS = self.ring("mask2_", 1, [P, 2, GB, S], F32, scope)
        nb, mb, ab = self.norm_bufs(scope), self.mlp_bufs(scope), self.narrow_bufs(scope, 1, 3, 2)
        self.staging = self.work
        wide = self.split_ring("l3_wide", 2, [DC, T], scope)
        qT = self.ring("l3_qT", 2, [P, DC, T], F32, scope)
        kT = self.ring("l3_kT", 2, [P, DC, T], F32, scope)
        vv = self.ring("l3_v", 1, [P, GB, D], F32, scope)
        W = {}

        def weights(names, q):
            for n in names:
                W[n] = self.load_weight("l3_" + n, a["L3_xattn_" + n], scope, q)
                yield
        run(weights(["w_qkv"], p.dve))
        m1 = p.dve.do("mask_prep", lambda e: e.tensor_scalar(
            mask1[:, 1, :], mask1[:, 0, :], -1.0, 40000.0, ALU.add, ALU.mult), [cd])
        scale = float(DH) ** -0.5
        begun, after = {}, {}
        tokens = lambda g: (lambda b: self.x_tok[:, g * GB + b, :])
        ctx_of = lambda g: self.ctxT[:, :, :, g * T:(g + 1) * T]

        def normalised(g, i, bias):
            def add_bias(read):
                self.x_done[g] = self.add_bias_rows(g, rows[bias], [read, cd])
            hs = yield from acquire(wide)
            return hs, (yield from self.norm_transposed(
                g, tokens(g), self.x_done[g], cols[f"ln{i}_s"], cols[f"ln{i}_b"], False, 1e-5, hs, nb, add_bias))

        def begin(g):
            hs, hd = yield from normalised(g, 1, "b_ao")
            q = yield from acquire(qT)
            _, qd = yield from self.project_cols("l3_q", *W["w_qkv"], 0, hs.t, hd, cols["b_qkv"][:, 0:2], q.t, q.free)
            k = yield from acquire(kT)
            _, kd = yield from self.project_cols("l3_k", *W["w_qkv"], D, hs.t, hd, cols["b_qkv"][:, 2:4], k.t, k.free)
            km = yield from self.mask_keys(0, [(k, kd)], ab)
            begun[g] = hs, hd, q, qd, k, kd, km

        def attention1(g):
            hs, hd, q, qd, k, kd, km = begun.pop(g)

            def project_v():
                v = yield from acquire(vv)
                m, vd = yield from self.project_rows("l3_v", *W["w_qkv"], 2 * D, hs.t, hd, v.t, v.free)
                hs.free = [m]
                return [(v, vd)]
            mask = {"mul": lambda b: mask1[:, 0, :], "add": lambda b: mask1[:, 1, :], "ready": m1}
            after[g] = yield from self.narrow_attention(g, q, qd, [(k, kd)], km, project_v(), scale, ab, mask)

        def middle(g):
            banks, m = yield from self.out_projection(g, *W["w_ao"], *after.pop(g), wide, cols["b_qkv"][:, 4:6])
            self.x_done[g] = self.add_to_x(g, banks, [m, m], [self.x_done[g]])
            yield
            hs, hd = yield from normalised(g, 2, "b_co")
            q = yield from acquire(qT)
            m, qd = yield from self.project_cols("l3_q", *W["w_q"], 0, hs.t, hd, cols["b_q"], q.t, q.free)
            hs.free = [m]
            k = yield from acquire(kT)
            _, kd = yield from self.project_cols("l3_k", *W["w_kv"], 0, ctx_of(g), self.ctxT_done[g], cols["b_kv"][:, 0:2], k.t, k.free)
            km = yield from self.mask_keys(0, [(k, kd)], ab)
            ms = yield from acquire(MS)
            ml = self.load("mask2", ms.t[:, 0], a["mask_Bx1xSxS2_ff1"][g * GB:(g + 1) * GB, 0]
                           .rearrange("b s t -> s b t"), ms.free)
            m2 = p.pool.do("mask_prep", lambda e: e.tensor_scalar(
                ms.t[:, 1], ms.t[:, 0], -1.0, 40000.0, ALU.add, ALU.mult), [ml])
            begun[g] = ms, m2, q, qd, k, kd, km

        def attention2(g):
            ms, m2, q, qd, k, kd, km = begun.pop(g)

            def project_v():
                v = yield from acquire(vv)
                _, vd = yield from self.project_rows("l3_v", *W["w_kv"], D, ctx_of(g), self.ctxT_done[g], v.t, v.free)
                return [(v, vd)]
            mask = {"mul": lambda b: ms.t[:, 0, b, :], "add": lambda b: ms.t[:, 1, b, :], "ready": m2}
            after[g] = yield from self.narrow_attention(g, q, qd, [(k, kd)], km, project_v(), scale, ab, mask)
            ms.free = [after[g][1]]

        def end(g):
            banks, m = yield from self.out_projection(g, *W["w_co"], *after.pop(g), wide, cols["b_kv"][:, 2:4])
            self.x_done[g] = self.add_to_x(g, banks, [m, m], [self.x_done[g]])
            yield
            hs, hd = yield from normalised(g, 3, "b2")
            banks, m = yield from self.mlp(hs, hd, *W["w1"], cols["b1"], *W["w2"], ACT.Gelu_apprx_tanh, mb)
            self.x_done[g] = self.add_to_x(g, banks, [m, m], [self.x_done[g]])

        run(begin(0))
        turns = [(attention1(0), weights(["w_ao", "w_q", "w_kv", "w_co", "w1", "w2"], p.pool), begin(1)),
                 (attention1(1), middle(0)), (attention2(0), middle(1)), (attention2(1), end(0), begin(2)),
                 (attention1(2), end(1), begin(3)), (attention1(3), middle(2)), (attention2(2), middle(3)),
                 (attention2(3), end(2))]
        for (main, *side), rate in zip(turns, L3_RATE):
            interleave(main, chain(*side), rate)
        run(end(3))


def xattn_stack_kernel(nc, args, out, stop_after=None):
    with ExitStack() as ctx:
        Kernel(nc, ctx, args, out, stop_after).build()


STOP = None


def kernel(**inputs):
    import numpy as np
    from concourse import bacc, mybir
    from concourse.bass_utils import run_bass_kernel_spmd

    arrays = {n: v for n, v in inputs.items() if not n.startswith("L0_xattn_W")}
    packed = dict(inputs)
    kv_b = inputs["L1_xattn_kv_b"].reshape(-1, 2)
    packed["L1_kv_b_k"], packed["L1_kv_b_v"] = kv_b[:, 0], kv_b[:, 1]
    arrays = {n: v for n, v in arrays.items() if n not in COLUMNS and n != "L1_xattn_kv_b"}
    arrays["columns"] = np.concatenate([np.reshape(packed[n], (-1, P)).T for n in COLUMNS], axis=1)
    arrays.update({f"L0_W{c}T": np.transpose(inputs[f"L0_xattn_W{c}"]) for c in "qkv"})
    nc = bacc.Bacc("TRN2", target_bir_lowering=False, num_devices=1)
    feed, args = {}, {}
    for name, v in arrays.items():
        v = np.ascontiguousarray(v)
        feed["in_" + name] = v
        args[name] = nc.dram_tensor("in_" + name, v.shape, mybir.dt.from_np(v.dtype), kind="ExternalInput").ap()
    out = nc.dram_tensor("out_0", inputs["x"].shape, mybir.dt.float32, kind="ExternalOutput").ap()
    xattn_stack_kernel(nc, args, out, STOP)
    r = run_bass_kernel_spmd(nc, [feed], core_ids=[0])
    return r.results[0]["out_0"]
```

```python
from contextlib import ExitStack

import concourse.bass as bass
from concourse import mybir

F32 = mybir.dt.float32
F32R = mybir.dt.float32r
I32 = mybir.dt.int32
ALU = mybir.AluOpType
ACT = mybir.ActivationFunctionType
AX = mybir.AxisListType

P = 128
B, S, D = 16, 128, 256
DC = D // P
GB = 4
G = B // GB
T = GB * S
D0 = 16
NH, DH = 16, 16
HPT = P // DH
QH = 4
H2, K2 = 16, 128
HG = 4
F = 1024
FC = F // P
NEG = -1.0e30


L1_RATE = (0.5, 1.05, 1.05, 0.6)
L3_RATE = (0.45, 0.45, 0.45, 0.9, 0.9, 0.45, 0.45, 0.65)
L1_STEPS = (0, 1, 2)
L3_STEPS = (1, 2, 4)

COLUMNS = {"L1_xattn_q_b": 2, "L1_kv_b_k": 2, "L1_kv_b_v": 2, "L1_xattn_postnorm_w": 2, "L1_xattn_mlp_b1": 8}
for _i in "12":
    COLUMNS.update({f"L2_xattn_ln{_i}_scale": 2, f"L2_xattn_ln{_i}_offset": 2, f"L2_xattn_bq{_i}": 16,
                    f"L2_xattn_bk{_i}": 16, f"L2_xattn_bv{_i}": 16, f"L2_xattn_bias_k{_i}": 16,
                    f"L2_xattn_bias_v{_i}": 16})
COLUMNS.update({"L2_xattn_ln_mlp_scale": 2, "L2_xattn_ln_mlp_offset": 2, "L2_xattn_b_fc1": 8})
COLUMNS.update({f"L3_xattn_ln{_i}_{_s}": 2 for _i in "123" for _s in "sb"})
COLUMNS.update({"L3_xattn_b_qkv": 6, "L3_xattn_b_q": 2, "L3_xattn_b_kv": 4, "L3_xattn_b1": 8})


class Op:

    def __init__(self, stage, emit, waits, dma):
        self.stage, self.emit, self.waits, self.dma = stage, emit, waits, dma
        self.signals, self.value = dma, None


class Queue:

    def __init__(self):
        self.ops = []

    def do(self, stage, emit, waits=(), dma=False):
        op = Op(stage, emit, [w for w in waits if w is not None], dma)
        for w in op.waits:
            w.signals = True
        self.ops.append(op)
        return op


class Slot:

    def __init__(self, t):
        self.t, self.taken, self._free = t, False, []

    @property
    def free(self):
        return self._free

    @free.setter
    def free(self, ops):
        self._free, self.taken = ops, False


class Ring:

    def __init__(self, slots):
        self.slots, self.n = [s if isinstance(s, Slot) else Slot(s) for s in slots], 0

    def spare(self):
        return sum(not s.taken for s in self.slots)

    def full(self):
        return self.spare() == 0

    def take(self):
        assert not self.full(), "the ring is too short"
        while self.slots[self.n % len(self.slots)].taken:
            self.n += 1
        slot = self.slots[self.n % len(self.slots)]
        self.n += 1
        slot.taken = True
        return slot


def acquire(ring):
    for _ in range(1000):
        if not ring.full():
            return ring.take()
        yield
    raise AssertionError("two chains of stages wait for each other's buffers")


def interleave(main, side, rate):
    due = 0.0
    for _ in main:
        due += rate
        while due >= 1.0:
            due -= 1.0
            next(side, None)
    for _ in side:
        pass


def run(stages):
    while True:
        try:
            next(stages)
        except StopIteration as end:
            return end.value


def chain(*parts):
    for part in parts:
        yield from part


class Program:
    def __init__(self, nc, ctx):
        self.nc, self.ctx = nc, ctx
        self.pe, self.act, self.dve, self.pool, self.sp = (Queue() for _ in range(5))
        self.queues = {"pe": self.pe, "act": self.act, "dve": self.dve, "pool": self.pool, "sp": self.sp}

    def emit(self):
        sems, counts = {}, {}
        for name, q in self.queues.items():
            for op in q.ops:
                if op.signals:
                    key = (name, op.stage)
                    if key not in sems:
                        sems[key] = self.ctx.enter_context(self.nc.semaphore(f"{name}_{op.stage}"))
                    counts[key] = counts.get(key, 0) + (16 if op.dma else 1)
                    op.sem, op.value = sems[key], counts[key]
        block = self.ctx.enter_context(self.nc.Block())

        def program(q):
            def body(eng):
                seen = {}
                for op in q.ops:
                    need = {}
                    for w in op.waits:
                        if need.get(w.sem.name, (None, 0))[1] < w.value:
                            need[w.sem.name] = (w.sem, w.value)
                    for k, (s, v) in need.items():
                        if seen.get(k, 0) < v:
                            eng.wait_ge(s, v)
                            seen[k] = v
                    ins = op.emit(eng)
                    if op.signals:
                        ins.then_inc(op.sem, 16 if op.dma else 1)
            return body

        block.sync(program(self.sp))
        block.gpsimd(program(self.pool))
        block.scalar(program(self.act))
        block.vector(program(self.dve))
        block.tensor(program(self.pe))


def matmul_split(eng, out, st, mv, start, stop, check=True):
    passes = [(st[0], mv[0]), (st[0], mv[1]), (st[1], mv[0])]
    for i, (a, b) in enumerate(passes):
        ins = eng.matmul(out, a, b, start=start and i == 0, stop=stop and i == 2, skip_group_check=not check)
    return ins


def f32(ap):
    return ap.bitcast(F32)


class Kernel:
    def __init__(self, nc, ctx, a, out):
        self.nc, self.a, self.out = nc, a, out
        self.p = Program(nc, ctx)
        self.ctx = ctx
        self.fence = []
        self.weight_tiles = {}
        self.phase = ""

    def share_banks(self, scores=(), tr=(), acc=(), side=(), misc=None):
        ring = lambda ids: Ring([self.banks[i] for i in ids])
        self.scores, self.tr, self.acc, self.side = (ring(i) for i in (scores, tr, acc, side))
        self.misc = self.tr if misc is None else ring(misc)

    def sb(self, name, shape, dt=F32, scope=None):
        return (scope or self.ctx).enter_context(self.nc.sbuf_tensor(self.phase + name, shape, dt))

    def ring(self, name, n, shape, dt=F32, scope=None):
        r = Ring([self.sb(f"{name}{i}", shape, dt, scope) for i in range(n)])
        for s in r.slots:
            s.free = list(self.fence)
        return r

    def split_ring(self, name, n, shape, scope):
        return self.ring(name, n, [P, 2] + shape, F32R, scope)

    def close_phase(self):
        p = self.p
        self.fence = [q.ops[-1] for q in (p.pe, p.act, p.dve, p.pool, p.sp) if q.ops]

    def load(self, stage, dst, src, waits=(), q=None):
        return (q or self.p.sp).do(stage, lambda e: e.dma_start(dst, src), waits, dma=True)

    def cols(self, name):
        at = 0
        for n, c in COLUMNS.items():
            if n == name:
                return self.columns[:, at:at + c]
            at += c
        raise KeyError(name)

    def load_bcast(self, stage, name, src, scope):
        t = self.sb(name, [P, src.shape[0]], F32, scope)
        return t, self.load(stage, t[:], src.partition_broadcast(P), self.fence)

    def split_on(self, q, stage, hi, lo, src, waits):
        if q is self.p.pool:
            h = q.do(stage + "_hi", lambda e: e.tensor_scalar(hi, src, 1.0, 1.0, ALU.mult, ALU.mult), waits)
        else:
            h = q.do(stage + "_hi", lambda e: e.tensor_copy(hi, src), waits)
        return q.do(stage + "_lo", lambda e: e.tensor_tensor(lo, src, f32(hi), ALU.subtract), [h])

    def split_psum(self, stage, hi, lo, src, waits, lo_waits=()):
        h = self.p.act.do(stage + "_hi", lambda e: e.activation(hi, src, ACT.Copy), waits)
        return self.p.dve.do(stage + "_lo", lambda e: e.tensor_tensor(lo, src, f32(hi), ALU.subtract),
                             [h, *lo_waits])

    def split_psum_bias(self, stage, hi, lo, src, bias, waits):
        h = self.p.act.do(stage + "_hi", lambda e: e.activation(hi, src, ACT.Identity, bias=bias), waits)
        return self.p.dve.do(stage + "_lo", lambda e: e.scalar_tensor_tensor(
            out=lo, in0=src, scalar=bias, in1=f32(hi), op0=ALU.add, op1=ALU.subtract), [h])

    def load_weight(self, name, src, scope, q, view=None):
        k, n = src.shape
        c = k // P
        t = self.weight_tiles.pop(name, None) or self.sb(name, [P, 2, c, n], F32R, scope)
        done, cs = None, max(1, self.stage_cols // n)
        for c0 in range(0, c, cs):
            m = min(cs, c - c0)
            s = self.staging.take()
            st = s.t[:, 0:m * n].rearrange("p (c n) -> p c n", c=m)
            ld = self.load(f"staging{self.staging.slots.index(s)}", st,
                           src[c0 * P:(c0 + m) * P, :].rearrange("(c p) n -> p c n", p=P), s.free)
            done = self.split_on(q, "weights", t[:, 0, c0:c0 + m, :], t[:, 1, c0:c0 + m, :], st,
                                 [ld, *self.fence])
            s.free = [done]
            yield
        return t, done

    def build(self):
        nc, p, a = self.nc, self.p, self.a
        self.x_tok = self.sb("x_tok", [P, B, D])
        self.ctxT = self.sb("ctxT", [P, 2, DC, B * S], F32R)
        self.x_done = [None] * G
        self.ctxT_done = [None] * G
        self.ident = self.sb("ident", [P, P])
        self.head_mask = self.sb("head_mask", [P, HPT])
        self.columns = self.sb("columns", [P, sum(COLUMNS.values())])
        self.cols_done = self.load("columns", self.columns[:], a["columns"])
        self.ps_pair = self.ctx.enter_context(nc.psum_tensor("ps_scores", [P, 2, 512], F32))
        self.banks = [Slot(self.ps_pair[:, i, :]) for i in range(2)]
        self.banks += [Slot(self.ctx.enter_context(nc.psum_tensor(f"ps_{i}", [P, 512], F32))[:]) for i in range(2, 8)]

        z = p.pool.do("const", lambda e: e.memset(self.ident[:], 0.0))
        m1 = p.pool.do("const", lambda e: e.memset(self.head_mask[:], 1.0))
        self.ident_done = p.pool.do("const", lambda e: e.affine_select(
            out=self.ident[:], in_=self.ident[:], compare_op=ALU.not_equal, fill=1.0, base=0,
            pattern=[[-1, P]], channel_multiplier=1), [z])
        m2 = p.pool.do("const", lambda e: e.affine_select(
            out=self.head_mask[:], in_=self.head_mask[:], compare_op=ALU.is_ge, fill=0.0, base=0,
            pattern=[[-DH, HPT]], channel_multiplier=1), [m1])
        self.mask_done = p.pool.do("const", lambda e: e.affine_select(
            out=self.head_mask[:], in_=self.head_mask[:], compare_op=ALU.is_ge, fill=0.0, base=DH - 1,
            pattern=[[DH, HPT]], channel_multiplier=-1), [m2])

        for phase in (self.phase_l0_l1, self.phase_l2_attention, self.phase_l2_mlp, self.phase_l3):
            with ExitStack() as scope:
                phase(scope)
                self.close_phase()
        stores = []
        for g in range(G):
            gb = slice(g * GB, (g + 1) * GB)
            stores.append(self.p.sp.do("store", lambda e, gb=gb: e.dma_start(
                self.out[gb].rearrange("b s d -> s b d"), self.x_tok[:, gb, :]), [self.x_done[g]], dma=True))
        self.p.sp.do("end", lambda e: e.nop(), stores)
        p.emit()

    def norm_transposed(self, g, src, src_done, gain, shift, rms, eps, dst, bufs, after_read=None):
        p = self.p
        st, mv, rs = (bufs[k].take() for k in ("stats", "mv", "rstd"))
        xn = yield from acquire(bufs["xn"])
        xn_t = xn.t[:].rearrange("p (b d) -> p b d", b=GB)
        w = [src_done]
        for b in range(GB):
            i1 = p.dve.do("ln_stats", lambda e, b=b: e.bn_stats(st.t[:, b, :], src(b)), w + st.free)
            if b % 2:
                yield
        for b in range(GB):
            i2 = p.dve.do("ln_aggr", lambda e, b=b: e.bn_aggr(mv.t[:, b, :], st.t[:, b, :]), [i1, *mv.free])
        last = i2
        if rms:
            last = p.dve.do("ln_tiny", lambda e: e.tensor_tensor(rs.t[:, 0, :], mv.t[:, :, 0], mv.t[:, :, 0], ALU.mult),
                            [last, *rs.free])
            last = p.dve.do("ln_tiny", lambda e: e.tensor_tensor(rs.t[:, 1, :], rs.t[:, 0, :], mv.t[:, :, 1], ALU.add), [last])
            var = rs.t[:, 1, :]
        else:
            var = mv.t[:, :, 1]
        last = p.dve.do("ln_tiny", lambda e: e.tensor_scalar(rs.t[:, 2, :], var, eps, None, ALU.add), [last, *rs.free])
        yield
        last = p.act.do("ln_sqrt", lambda e: e.activation(rs.t[:, 3, :], rs.t[:, 2, :], ACT.Sqrt), [last])
        yield
        yield
        last = p.dve.do("ln_tiny", lambda e: e.reciprocal(rs.t[:, 4, :], rs.t[:, 3, :]), [last])
        xw = [last, *xn.free]
        for b in range(GB):
            if rms:
                i3 = p.dve.do("ln_xn", lambda e, b=b: e.tensor_scalar(
                    xn_t[:, b, :], src(b), rs.t[:, 4, b:b + 1], None, ALU.mult), xw)
            else:
                i3 = p.dve.do("ln_xn", lambda e, b=b: e.tensor_scalar(
                    xn_t[:, b, :], src(b), mv.t[:, b, 0:1], rs.t[:, 4, b:b + 1], ALU.subtract, ALU.mult), xw)
            if b % 2:
                yield
        st.free = mv.free = rs.free = [i3]
        if after_read is not None:
            after_read(i3)
        tmp = yield from acquire(bufs["ntmp"])
        tmp_t = tmp.t[:].rearrange("p (c t) -> p c t", c=DC)
        yield
        for c in range(DC):
            bank = yield from acquire(self.tr)

            def tr(e, c=c, bank=bank):
                for b in range(GB):
                    i = e.transpose(bank.t[:, b * S:(b + 1) * S], xn_t[:, b, c * P:(c + 1) * P], self.ident[:])
                return i
            t = p.pe.do("ln_tr", tr, [i3, self.ident_done, *bank.free])
            xf = p.act.do("ln_affine", lambda e, c=c, bank=bank: e.activation(
                tmp_t[:, c, :], bank.t, ACT.Identity, scale=gain[:, c:c + 1],
                bias=shift[:, c:c + 1] if shift is not None else 0.0), [t, *tmp.free])
            bank.free = [xf]
            yield
            done = self.split_on(p.dve, "ln_split", dst.t[:, 0, c, :], dst.t[:, 1, c, :], tmp_t[:, c, :],
                                 [xf, *dst.free])
        xn.free = [t]
        tmp.free = [done]
        yield
        return done

    def norm_bufs(self, scope):
        self.work = self.ring("work", 3, [P, GB * D], F32, scope)
        return {"stats": self.ring("st", 1, [P, GB, 6], F32, scope), "mv": self.ring("mv", 1, [P, GB, 2], F32, scope),
                "rstd": self.ring("rstd", 1, [P, 5, GB], F32, scope), "xn": self.work, "ntmp": self.work}

    def add_bias_rows(self, g, bias, waits):
        x = self.x_tok[:, g * GB:(g + 1) * GB, :]
        return self.p.pool.do("x_bias", lambda e: e.tensor_tensor(
            x, x, bias[:].unsqueeze(1).to_broadcast([P, GB, D]), ALU.add), waits)

    def add_to_x(self, g, banks, tickets, waits):
        for i, (bk, t) in enumerate(zip(banks, tickets)):
            x = self.x_tok[:, g * GB + 2 * i:g * GB + 2 * i + 2, :]
            done = self.p.dve.do("x_add", lambda e, x=x, bk=bk: e.tensor_tensor(
                x, x, bk.t.rearrange("p (b d) -> p b d", b=2), ALU.add), [t, *waits])
            bk.free = [done]
        return done

    def mlp(self, inT, in_done, w1, w1_done, b1, w2, w2_done, func, bufs):
        p = self.p
        banks, parts = None, []

        def down(parts):
            for k, hs, sp in parts:
                def mm(e, k=k, hs=hs):
                    for b in range(GB):
                        o = banks[b // 2].t[:, (b % 2) * D:(b % 2 + 1) * D]
                        i = matmul_split(e, o, [hs.t[:, s, b * S:(b + 1) * S] for s in (0, 1)],
                                         [w2[:, s, k, :] for s in (0, 1)],
                                         k == 0 and b % 2 == 0, k == FC - 1, check=False)
                    return i
                d = p.pe.do("mlp_down", mm, [sp, w2_done, *banks[0].free, *banks[1].free])
                hs.free = [d]
            return d

        for pair in range(FC // 2):
            hid = yield from acquire(bufs["hid"])
            for i in range(2):
                m = 2 * pair + i
                bk = yield from acquire(self.misc)

                def up(e, m=m, bk=bk):
                    for c in range(DC):
                        i = matmul_split(e, bk.t, [w1[:, s, c, m * P:(m + 1) * P] for s in (0, 1)],
                                         [inT.t[:, s, c, :] for s in (0, 1)], c == 0, c == DC - 1)
                    return i
                u = p.pe.do("mlp_up", up, [in_done, w1_done, *bk.free])
                ev = p.dve.do("mlp_up", lambda e, m=m, i=i, bk=bk, hid=hid: e.tensor_scalar(
                    hid.t[:, i * T:(i + 1) * T], bk.t, b1[:, m:m + 1], None, ALU.add), [u, *hid.free])
                bk.free = [ev]
                yield
            if pair == FC // 2 - 1:
                inT.free = [u]
            ge = p.act.do("gelu", lambda e, hid=hid: e.activation(hid.t[:], hid.t[:], func), [ev])
            if parts:
                if banks is None:
                    banks = [(yield from acquire(self.side)), (yield from acquire(self.side))]
                down(parts)
                yield
            parts = []
            for i in range(2):
                hs = yield from acquire(bufs["hid_split"])
                sp = self.split_on(p.dve, "hid", hs.t[:, 0, :], hs.t[:, 1, :], hid.t[:, i * T:(i + 1) * T],
                                   [ge, *hs.free])
                parts.append((2 * pair + i, hs, sp))
                yield
            hid.free = [sp]
        d = down(parts)
        yield
        return banks, d

    def mlp_bufs(self, scope):
        return {"hid": self.work, "hid_split": self.split_ring("hids", 2, [T], scope)}

    def project_cols(self, stage, w, w_done, off, inT, in_done, bias, dst, dst_free):
        p = self.p
        for j in range(DC):
            bk = yield from acquire(self.misc)

            def mm(e, j=j, bk=bk):
                for c in range(DC):
                    i = matmul_split(e, bk.t, [w[:, s, c, off + j * P:off + (j + 1) * P] for s in (0, 1)],
                                     [inT[:, s, c, :] for s in (0, 1)], c == 0, c == DC - 1)
                return i
            m = p.pe.do(stage, mm, [w_done, in_done, *bk.free])
            done = p.act.do(stage, lambda e, j=j, bk=bk: e.activation(
                dst(j), bk.t.rearrange("p (b t) -> p b t", b=GB), ACT.Identity, bias=bias[:, j:j + 1]), [m, *dst_free])
            bk.free = [done]
            yield
        return m, done

    def project_rows(self, stage, w, w_done, off, inT, in_done, dst, dst_free):
        p = self.p
        for h in range(2):
            bk = yield from acquire(self.misc)

            def mm(e, h=h, bk=bk):
                for b in (2 * h, 2 * h + 1):
                    for c in range(DC):
                        i = matmul_split(e, bk.t[:, (b % 2) * D:(b % 2 + 1) * D],
                                         [inT[:, s, c, b * S:(b + 1) * S] for s in (0, 1)],
                                         [w[:, s, c, off:off + D] for s in (0, 1)], c == 0, c == DC - 1)
                return i
            m = p.pe.do(stage, mm, [w_done, in_done, *bk.free])
            done = p.dve.do(stage, lambda e, h=h, bk=bk: e.tensor_copy(
                dst[:, 2 * h:2 * h + 2, :], bk.t.rearrange("p (b d) -> p b d", b=2)), [m, *dst_free])
            bk.free = [done]
            yield
        return m, done

    def narrow_bufs(self, scope, nsrc, prob, probT):
        return {"qm": self.ring("qm", 2, [P, QH, GB, S], F32, scope),
                "prob": self.ring("prob", prob, [P, QH, nsrc, S], F32, scope),
                "probT": self.ring("probT", probT, [P, nsrc, QH, S], F32, scope),
                "smax": self.ring("smax", prob, [P, 4, QH], F32, scope),
                "rsum": self.ring("rsum", 2, [P, GB, NH], F32, scope)}

    def mask_queries(self, qd, q, q_done, bufs):
        qm = yield from acquire(bufs["qm"])
        eng = self.p.dve if qd == 0 else self.p.pool
        for i in range(QH):
            h = qd * QH + i
            j, hh = h // HPT, h % HPT
            done = eng.do("mask_queries", lambda e, i=i, j=j, hh=hh: e.tensor_scalar(
                qm.t[:, i], q.t[:, j], self.head_mask[:, hh:hh + 1], 1.0, ALU.mult, ALU.mult),
                [q_done, self.mask_done, *qm.free])
        if qd == NH // QH - 1:
            q.free = [done]
        return qm, done

    def narrow_attention(self, g, q, q_done, k, k_done, first_qm, project_v, scale, bufs, mask, after_scores=None):
        p, nsrc = self.p, k.t.shape[3]
        keys = nsrc * S
        hpb = 512 // keys
        acc = [(yield from acquire(self.acc)), (yield from acquire(self.acc))]
        rsum = bufs["rsum"].take()
        items = [(qd, b) for qd in range(NH // QH) for b in range(GB)]
        state = {}
        qm_of = {0: first_qm}

        def scores(n):
            qd, b = items[n]
            qm, tick = qm_of[qd]
            j = qd * QH // HPT
            banks = [self.scores.take() for _ in range(nsrc)]

            def mm(e):
                for s, bk in enumerate(banks):
                    for i in range(hpb):
                        last = e.matmul(bk.t[:, i * keys:(i + 1) * keys], qm.t[:, s * hpb + i, b, :],
                                        k.t[:, j, b].rearrange("p s t -> p (s t)"), start=i == 0,
                                        stop="keys" not in mask, skip_group_check=True)
                    if "keys" in mask:
                        last = e.matmul(bk.t.rearrange("p (h s t) -> p h s t", h=hpb, s=nsrc)[:, :, 0, :], mask["ones"][:],
                                        mask["keys"][:, b, :].unsqueeze(1).to_broadcast([1, hpb, S]),
                                        start=False, stop=True, skip_group_check=True)
                return last
            m = p.pe.do("scores", mm, [k_done, tick, mask["ready"]] + [f for bk in banks for f in bk.free])
            if b == GB - 1:
                qm.free = [m]
            if n == len(items) - 1:
                k.free = [m]
                if after_scores is not None:
                    after_scores(m)
            state[n] = {"banks": banks, "scores": m}

        def softmax(n):
            qd, b = items[n]
            st = state[n]
            banks, m = st["banks"], st["scores"]
            pr, mx = bufs["prob"].take(), bufs["smax"].take()
            if "mul" in mask:
                mul, add = mask["mul"](b), mask["add"](b)
                r = p.dve.do("mask_mul", lambda e: e.tensor_tensor(
                    pr.t[:, :, 0, :], banks[0].t.rearrange("p (h t) -> p h t", h=QH),
                    mul.unsqueeze(1).to_broadcast([P, QH, S]), ALU.mult), [m, *pr.free])
                banks[0].free = [r]
                r = p.pool.do("mask_add", lambda e: e.tensor_tensor(
                    pr.t[:, :, 0, :], pr.t[:, :, 0, :], add.unsqueeze(1).to_broadcast([P, QH, S]), ALU.add), [r])
            st.update(prob=pr, mx=mx, masked=m if "mul" not in mask else r)

        def exps(n):
            st = state[n]
            banks, r, pr, mx = st["banks"], st["masked"], st["prob"], st["mx"]
            if "mul" in mask:
                src = lambda i: pr.t[:, i, 0, :]
                r = p.dve.do("row_max", lambda e: e.tensor_reduce(
                    mx.t[:, 0, :], pr.t[:, :, 0, :], AX.X, ALU.max), [r, *mx.free])
            else:
                view = self.ps_pair[:].rearrange("p k (h t) -> p (k h) t", h=hpb)
                src = lambda i: view[:, i, :]
                r = p.dve.do("row_max", lambda e: e.tensor_reduce(
                    mx.t[:, 0, :], view, AX.X, ALU.max), [r, *mx.free])
            r = p.dve.do("row_max", lambda e: e.tensor_scalar(
                mx.t[:, 1, :], mx.t[:, 0, :], -scale, None, ALU.mult), [r])
            for i in range(QH):
                dst = pr.t[:, i].rearrange("p s t -> p (s t)")
                ex = p.act.do("exp", lambda e, i=i, dst=dst: e.activation(
                    dst, src(i), ACT.Exp, bias=mx.t[:, 1, i:i + 1], scale=scale,
                    accum_out=mx.t[:, 2, i:i + 1]), [r, *pr.free])
            if "mul" not in mask:
                for bk in banks:
                    bk.free = [ex]
            st.update(exp=ex)

        def row_sums(n):
            qd, b = items[n]
            mx = state[n]["mx"]
            rc = p.dve.do("row_recip", lambda e: e.reciprocal(
                rsum.t[:, b, qd * QH:(qd + 1) * QH], mx.t[:, 2, :]), [state[n]["exp"], *rsum.free])
            mx.free = [rc]
            return rc

        def transposes(n):
            st = state[n]
            pr, pt = st["prob"], bufs["probT"].take()
            for s in range(nsrc):
                bk = yield from acquire(self.tr)

                def tr(e, s=s, bk=bk):
                    for i in range(QH):
                        ins = e.transpose(bk.t[:, i * S:(i + 1) * S], pr.t[:, i, s, :], self.ident[:])
                    return ins
                t = p.pe.do("prob_tr", tr, [st["exp"], self.ident_done, *bk.free])
                on_dve = s == 1 if nsrc == 2 else n % 2 == 0
                if on_dve:
                    ev = p.dve.do("probT", lambda e, s=s, bk=bk: e.tensor_copy(
                        pt.t[:, s, :, :], bk.t.rearrange("p (h t) -> p h t", h=QH)), [t, *pt.free])
                else:
                    ev = p.act.do("probT", lambda e, s=s, bk=bk: e.activation(
                        pt.t[:, s, :, :], bk.t.rearrange("p (h t) -> p h t", h=QH), ACT.Copy), [t, *pt.free])
                bk.free = [ev]
                st.setdefault("ev", []).append(ev)
            pr.free = [t]
            st["probT"] = pt

        def values(n):
            qd, b = items[n]
            st = state.pop(n)
            pt, bank = st["probT"], acc[b // 2]

            def mm(e):
                for i in range(QH):
                    h = qd * QH + i
                    for s in range(nsrc):
                        ins = e.matmul(bank.t[:, (b % 2) * D + h * DH:(b % 2) * D + (h + 1) * DH],
                                       pt.t[:, s, i, :], vs[s][0].t[:, b, h * DH:(h + 1) * DH],
                                       start=s == 0, stop=s == nsrc - 1)
                return ins
            m = p.pe.do("values", mm, [*st["ev"], *[d for _, d in vs], *bank.free])
            pt.free = [m]
            return m

        N, masked = len(items), "mul" in mask
        at_exp, at_tr, at_values = L3_STEPS if masked else L1_STEPS
        for step in range(N + at_values + 1):
            if masked and 0 <= step - at_exp < N:
                exps(step - at_exp)
            if step < N:
                qd, b = items[step]
                if qd not in qm_of:
                    qm_of[qd] = yield from self.mask_queries(qd, q, q_done, bufs)
                scores(step)
                softmax(step)
            if not masked and step < N:
                exps(step)
            yield
            if step == 1:
                vs = yield from project_v
            if 0 <= step - at_values < N:
                m_last = values(step - at_values)
                yield
            if step < N and qd + 1 < NH // QH and qd + 1 not in qm_of and bufs["qm"].spare():
                qm_of[qd + 1] = yield from self.mask_queries(qd + 1, q, q_done, bufs)
            if 0 <= step - at_tr < N:
                sums = row_sums(step - at_tr)
                yield from transposes(step - at_tr)
                yield
        for v, _ in vs:
            v.free = [m_last]
        ao = yield from acquire(self.work)
        ao_t = ao.t[:].rearrange("p (b d) -> p b d", b=GB)
        for i in range(2):
            nrm = p.dve.do("ao_norm", lambda e, i=i: e.tensor_tensor(
                ao_t[:, 2 * i:2 * i + 2, :].rearrange("p b (h d) -> p (b h) d", d=DH),
                acc[i].t.rearrange("p (h d) -> p h d", d=DH),
                rsum.t[:, 2 * i:2 * i + 2, :].rearrange("p b h -> p (b h)").unsqueeze(2).to_broadcast([P, 2 * NH, DH]),
                ALU.mult), [m_last, sums, *ao.free])
            acc[i].free = [nrm]
        rsum.free = [nrm]
        return ao, nrm

    def out_projection(self, g, w, w_done, ao, ao_done, wide, bv):
        p = self.p
        aoT = yield from acquire(wide)
        ao_t = ao.t[:].rearrange("p (b d) -> p b d", b=GB)
        for c in range(DC):
            bk = yield from acquire(self.tr)

            def tr(e, c=c, bk=bk):
                for b in range(GB):
                    ins = e.transpose(bk.t[:, b * S:(b + 1) * S], ao_t[:, b, c * P:(c + 1) * P], self.ident[:])
                return ins
            t = p.pe.do("ao_tr", tr, [ao_done, *bk.free])
            done = self.split_psum_bias("ao", aoT.t[:, 0, c, :], aoT.t[:, 1, c, :], bk.t, bv[:, c:c + 1],
                                        [t, *aoT.free])
            bk.free = [done]
            yield
        ao.free = [t]
        banks = [(yield from acquire(self.side)), (yield from acquire(self.side))]
        for b in range(GB):
            def mm(e, b=b):
                for c in range(DC):
                    i = matmul_split(e, banks[b // 2].t[:, (b % 2) * D:(b % 2 + 1) * D],
                                     [aoT.t[:, s, c, b * S:(b + 1) * S] for s in (0, 1)],
                                     [w[:, s, c, :] for s in (0, 1)], c == 0, c == DC - 1)
                return i
            m = p.pe.do("out_proj", mm, [done, w_done, *banks[0].free, *banks[1].free])
            if b % 2:
                yield
        aoT.free = [m]
        return banks, m

    def phase_l0_l1(self, scope):
        self.phase = "l01_"
        p, a = self.p, self.a
        sb = lambda n, s, dt=F32: self.sb(n, s, dt, scope)
        wqT, wkT, wvT = (sb(n, [P, m]) for n, m in (("wqT", D0), ("wkT", D0), ("wvT", P)))
        bq0, bk0, bv0 = sb("bq0", [D0, 1]), sb("bk0", [D0, 1]), sb("bv0", [P, 1])
        loads = [self.load("l0_small", t[:], s) for t, s in (
            (wqT, a["L0_WqT"]), (wkT, a["L0_WkT"]), (wvT, a["L0_WvT"]),
            (bq0, a["L0_xattn_bq"].unsqueeze(1)), (bk0, a["L0_xattn_bk"].unsqueeze(1)),
            (bv0, a["L0_xattn_bv"].unsqueeze(1)))]
        small = loads[-1]
        p.act.do("columns_ready", lambda e: e.nop(), [self.cols_done])
        x_loaded, ctx_loaded = [], []
        self.share_banks(scores=(0, 1), tr=(2, 3), acc=(4, 5), misc=(6, 7))

        def load_group(g):
            gb = slice(g * GB, (g + 1) * GB)
            x_loaded.append(self.load(f"load_x{g}", self.x_tok[:, gb, :], a["x"][gb].rearrange("b s d -> s b d")))
            s = ctx_tok.take()
            ctx_loaded.append((s, self.load(f"load_ctx{g}", s.t[:], a["ctx_2048"][gb].rearrange("b s d -> s b d"), s.free)))
        self.stage_cols = 1024
        for n, shape in (("l1_wq", [DC, D]), ("l1_wo", [DC, D]), ("l1_w1", [DC, F]), ("l1_w2", [FC, D])):
            self.weight_tiles[n] = sb(n, [P, 2] + shape, F32R)
        wkv = sb("l1_wkv", [P, 2, 2, DC, D], F32R)
        qb, bk1, bv1, pw, b1 = (self.cols(n) for n in (
            "L1_xattn_q_b", "L1_kv_b_k", "L1_kv_b_v", "L1_xattn_postnorm_w", "L1_xattn_mlp_b1"))
        ob, _ = self.load_bcast("l1_bias", "l1_ob", a["L1_xattn_out_b"], scope)
        b2, bias = self.load_bcast("l1_bias", "l1_b2", a["L1_xattn_mlp_b2"], scope)
        ones = sb("ones_row", [1, P], F32R)
        one = p.dve.do("key_mask", lambda e: e.tensor_scalar(ones[:], wvT[0:1, :], 0.0, 1.0, ALU.mult, ALU.add), [small])
        l0_scope = ExitStack()
        self.staging = self.ring("staging", 2, [P, self.stage_cols], F32, l0_scope)
        ctx_tok = self.ring("ctx_tok", 2, [P, GB, D], F32, l0_scope)
        load_group(0)
        load_group(1)

        def l1_weights():
            for n, name in (("wq", "q_w"), ("wkv", None), ("wo", "out_w"), ("w1", "mlp_w1"), ("w2", "mlp_w2")):
                if name is not None:
                    _, done_of[n] = yield from self.load_weight("l1_" + n, a["L1_xattn_" + name], scope, p.pool)
                    continue
                s = self.staging.take()
                stg = s.t[:].rearrange("p (c n s) -> p c n s", c=DC, s=2)
                ld = self.load(f"staging{self.staging.slots.index(s)}", s.t[:].rearrange("p (c n) -> p c n", c=DC),
                               a["L1_xattn_kv_w"].rearrange("(c p) n -> p c n", p=P), s.free)
                for i in range(2):
                    done_of[n] = self.split_on(p.pool, "weights", wkv[:, i, 0], wkv[:, i, 1], stg[:, :, :, i], [ld])
                    s.free = [done_of[n]]
                    yield
        done_of = {}
        wq, wo, w1, w2 = (self.weight_tiles["l1_" + n] for n in ("wq", "wo", "w1", "w2"))
        wk, wv = wkv[:, 0], wkv[:, 1]
        l0 = {k: self.ring("l0_" + k, n, s, F32, l0_scope) for k, n, s in (
            ("qk", 2, [D0, 2, D]), ("v", 4, [P, 2, P]), ("prob", 2, [P, 2, D]), ("probT", 2, [P, 2, D]),
            ("mx", 2, [P, 4, 2]))}
        def l0_project(st):
            b, g = st["b"], st["b"] // GB
            x1, x2 = self.x_tok[:, b, :], ctx_loaded[g][0].t[:, b % GB, :]
            bk, qk = self.misc.take(), l0["qk"].take()

            def mm(e):
                e.matmul(bk.t[0:D0, 0:D], wqT[:], x1, start=True, stop=True)
                return e.matmul(bk.t[0:D0, D:2 * D], wkT[:], x2, start=True, stop=True)
            m = p.pe.do("l0_qk", mm, [small, x_loaded[g], ctx_loaded[g][1], *bk.free])
            for i, bb in enumerate((bq0, bk0)):
                st["qk_done"] = p.act.do("l0_qk", lambda e, i=i, bb=bb: e.activation(
                    qk.t[:, i, :], bk.t[0:D0, i * D:(i + 1) * D], ACT.Identity, bias=bb[:, 0:1]), [m, *qk.free])
            bk.free = [st["qk_done"]]
            st["qk"] = qk
            bv_bank, v = self.misc.take(), l0["v"].take()

            def mm_v(e):
                for c in range(2):
                    i = e.matmul(bv_bank.t[:, c * P:(c + 1) * P], x2[:, c * P:(c + 1) * P], wvT[:], start=True, stop=True)
                for c in range(2):
                    i = e.transpose(bv_bank.t[:, (2 + c) * P:(3 + c) * P], x2[:, c * P:(c + 1) * P], self.ident[:])
                return i
            m = p.pe.do("l0_v", mm_v, [self.ident_done, *bv_bank.free])
            if b % GB == GB - 1:
                ctx_loaded[g][0].free = [m]
            st["v_done"] = p.dve.do("l0_v", lambda e: e.tensor_copy(
                v.t[:].rearrange("p c n -> p (c n)"), bv_bank.t[:, 0:2 * P]), [m, *v.free])
            st["v"] = v
            h = slice(b * S, (b + 1) * S)
            src = bv_bank.t[:, 2 * P:4 * P].rearrange("p (c n) -> p c n", c=2)
            self.ctxT_done[g] = self.split_psum("ctxT", self.ctxT[:, 0, :, h], self.ctxT[:, 1, :, h], src,
                                                [m, st["v_done"]])
            bv_bank.free = [self.ctxT_done[g]]

        def l0_scores(st):
            bk, qk, pr, mx = self.scores.take(), st["qk"], l0["prob"].take(), l0["mx"].take()

            def mm(e):
                for c in range(2):
                    i = e.matmul(bk.t[:, c * D:(c + 1) * D], qk.t[:, 0, c * P:(c + 1) * P], qk.t[:, 1, :],
                                 start=True, stop=True)
                return i
            m = p.pe.do("l0_scores", mm, [st["qk_done"], *bk.free])
            qk.free = [m]
            r = p.dve.do("l0_max", lambda e: e.tensor_reduce(
                mx.t[:, 0, :], bk.t.rearrange("p (c n) -> p c n", c=2), AX.X, ALU.max, negate=True), [m, *mx.free])
            for c in range(2):
                ex = p.act.do("l0_exp", lambda e, c=c: e.activation(
                    pr.t[:, c, :], bk.t[:, c * D:(c + 1) * D], ACT.Exp, bias=mx.t[:, 0, c:c + 1],
                    accum_out=mx.t[:, 1, c:c + 1]), [r, *pr.free])
            bk.free = [ex]
            rc = p.dve.do("l0_recip", lambda e: e.reciprocal(mx.t[:, 2, :], mx.t[:, 1, :]), [ex])
            nm = p.pool.do("l0_norm", lambda e: e.tensor_tensor(
                pr.t[:], pr.t[:], mx.t[:, 2, :].unsqueeze(2).to_broadcast([P, 2, D]), ALU.mult), [rc])
            mx.free = [nm]
            st.update(prob=pr, prob_done=nm)

        def l0_values(st):
            b = st["b"]
            bk, pr, pt = self.tr.take(), st["prob"], l0["probT"].take()

            def tr(e):
                for m in range(2):
                    for n in range(2):
                        i = e.transpose(bk.t[:, m * D + n * P:m * D + (n + 1) * P],
                                        pr.t[:, n, m * P:(m + 1) * P], self.ident[:])
                return i
            t = p.pe.do("l0_tr", tr, [st["prob_done"], *bk.free])
            pr.free = [t]
            ev = p.dve.do("l0_probT", lambda e: e.tensor_copy(pt.t[:].rearrange("p m n -> p (m n)"), bk.t), [t, *pt.free])
            bk.free = [ev]
            st.update(probT=pt, probT_done=ev)

        def l0_out(st):
            b, bk, pt, v = st["b"], self.acc.take(), st["probT"], st["v"]

            def mm(e):
                for m in range(2):
                    i = e.matmul(bk.t[:, 0:D], v.t[:, m, :], pt.t[:, m, :], start=m == 0, stop=m == 1)
                return i
            m = p.pe.do("l0_out", mm, [st["probT_done"], st["v_done"], *bk.free])
            pt.free = v.free = [m]
            x = self.x_tok[:, b, :]
            done = p.dve.do("l0_x", lambda e: e.scalar_tensor_tensor(
                out=x, in0=bk.t[:, 0:D], scalar=bv0[:, 0:1], in1=x, op0=ALU.add, op1=ALU.add), [m])
            bk.free = [done]
            self.x_done[b // GB] = done

        def l1_begin(g):
            xs = yield from acquire(wide)
            for c in range(DC):
                bk = yield from acquire(self.tr)

                def tr(e, c=c, bk=bk):
                    for b in range(GB):
                        i = e.transpose(bk.t[:, b * S:(b + 1) * S], self.x_tok[:, g * GB + b, c * P:(c + 1) * P], self.ident[:])
                    return i
                t = p.pe.do("l1_xT", tr, [self.x_done[g], *bk.free])
                x_tdone = self.split_psum("l1_xT", xs.t[:, 0, c, :], xs.t[:, 1, c, :], bk.t, [t, *xs.free])
                bk.free = [x_tdone]
                yield
            mi, ky = (yield from acquire(mask_i)), (yield from acquire(keys))
            ld = self.load("l1_mask", mi.t[:], a["mask_BxS2_ik0"][g * GB:(g + 1) * GB].unsqueeze(0), mi.free)
            k = yield from acquire(kT)
            for i, (src, done) in enumerate(((ctx_of(g), self.ctxT_done[g]), (xs.t, x_tdone))):
                _, k_done = yield from self.project_cols("l1_k", wk, wkv_done, 0, src, done, bk1,
                                                         lambda j, i=i: k.t[:, j, :, i, :], k.free)
            q = yield from acquire(qT)
            _, q_done = yield from self.project_cols("l1_q", wq, wq_done, 0, xs.t, x_tdone, qb,
                                                     lambda j: q.t[:, j], q.free + [bias])
            kmask = p.dve.do("key_mask", lambda e: e.tensor_scalar(
                ky.t[:], mi.t[:], 0.0, NEG, ALU.is_equal, ALU.mult), [ld, *ky.free])
            mi.free = [kmask]
            yield
            qm = yield from self.mask_queries(0, q, q_done, ab)
            begun[g] = dict(xs=xs, xs_done=x_tdone, qk=(q, q_done, k, k_done, qm), tr=t, ky=ky,
                            mask={"keys": ky.t, "ones": ones, "ready": kmask})

        def l1_values(g):
            st = begun[g]
            vs = []
            for i, (src, done) in enumerate(((ctx_of(g), self.ctxT_done[g]), (st["xs"].t, st["xs_done"]))):
                v = yield from acquire(vv[i])
                m, v_done = yield from self.project_rows("l1_v", wv, wkv_done, 0, src, done, v.t, v.free)
                vs.append((v, v_done))
            st["xs"].free = [m]
            return vs

        def l1_attention(g):
            st = begun[g]

            def mask_read(m):
                st["ky"].free = [m]
            st["ao"] = yield from self.narrow_attention(
                g, *st["qk"], l1_values(g), 1.0 / DH, ab, st["mask"], mask_read)

        def l1_end(g):
            st = begun.pop(g)
            banks, m = yield from self.out_projection(g, wo, wo_done, *st["ao"], wide, bv1)
            ys = yield from acquire(self.work)
            ys_t = ys.t[:].rearrange("p (b d) -> p b d", b=GB)
            xg = self.x_tok[:, g * GB:(g + 1) * GB, :]
            y0 = p.pool.do("l1_y", lambda e: e.tensor_tensor(
                ys_t, xg, ob[:].unsqueeze(1).to_broadcast([P, GB, D]), ALU.add), [self.x_done[g], bias, *ys.free])
            yield
            for i in range(2):
                yd = p.dve.do("l1_y", lambda e, i=i, banks=banks: e.tensor_tensor(
                    ys_t[:, 2 * i:2 * i + 2, :], ys_t[:, 2 * i:2 * i + 2, :],
                    banks[i].t.rearrange("p (b d) -> p b d", b=2), ALU.add), [y0, m])
                banks[i].free = [yd]
            xb = self.add_bias_rows(g, b2, [y0, st["tr"]])

            def y_read(op):
                ys.free = [op]
            hs = yield from acquire(wide)
            h_done = yield from self.norm_transposed(g, lambda b: ys_t[:, b, :], yd, pw, None, True, 1e-6, hs, nb, y_read)
            banks, m = yield from self.mlp(hs, h_done, w1, w1_done, b1, w2, w2_done, ACT.Gelu_apprx_tanh, mb)
            self.x_done[g] = self.add_to_x(g, banks, [m, m], [xb])

        sts, weights = [{"b": b} for b in range(B)], l1_weights()
        for step in range(B + 3):
            for off, f in ((0, l0_project), (1, l0_scores), (3, l0_out), (2, l0_values)):
                if 0 <= step - off < B:
                    f(sts[step - off])
            if step % GB == GB - 1 and step // GB + 2 < G:
                load_group(step // GB + 2)
            if step > 0:
                next(weights, None)
        run(weights)
        wq_done, wkv_done, wo_done, w1_done, w2_done = (done_of[n] for n in ("wq", "wkv", "wo", "w1", "w2"))
        l0_scope.close()
        self.close_phase()
        self.share_banks(scores=(0, 1), tr=(2, 3), acc=(4, 5), side=(6, 7))
        nb, mb, ab = self.norm_bufs(scope), self.mlp_bufs(scope), self.narrow_bufs(scope, 2, 2, L1_STEPS[2] - L1_STEPS[1] + 1)
        wide = self.split_ring("wide", 2, [DC, T], scope)
        qT = self.ring("qT", 1, [P, DC, GB, S], F32, scope)
        kT = self.ring("kT", 2, [P, DC, GB, 2, S], F32, scope)
        vv = [self.ring(f"vv{i}", 1, [P, GB, D], F32, scope) for i in range(2)]
        mask_i = self.ring("mask_i", 1, [1, GB, S], I32, scope)
        keys = self.ring("mask_keys", 1, [1, GB, S], F32R, scope)
        ctx_of = lambda g: self.ctxT[:, :, :, g * T:(g + 1) * T]
        begun = {}
        run(l1_begin(0))
        for g in range(G):
            side = [l1_end(g - 1)] if g > 0 else []
            side += [l1_begin(g + 1)] if g + 1 < G else []
            interleave(l1_attention(g), chain(*side), L1_RATE[g])
        run(l1_end(G - 1))

    def phase_l2_attention(self, scope):
        self.phase = "l2a_"
        p, a = self.p, self.a
        sb = lambda n, s, dt=F32: self.sb(n, s, dt, scope)
        hT = [self.split_ring(f"l2_hT{g}", 1, [DC, T], scope).slots[0] for g in range(G)]
        W = {k: self.ring("l2_" + k, 2, [P, 2, DC, HG * K2], F32R, scope) for k in ("wq", "wk", "wv")}
        W["wo"] = self.ring("l2_wo", 2, [P, 2, HG, D], F32R, scope)
        staging = self.ring("l2_staging", 3, [P, DC * HG * K2], F32, scope)
        V = self.ring("l2_V", 2, [P, GB, HG * K2], F32, scope)
        QT = self.ring("l2_qT", 2, [P, T], F32, scope)
        KT = self.ring("l2_kT", 2, [P, GB, S + 2], F32, scope)
        PR = self.ring("l2_prob", 2, [P, GB, S + 2], F32, scope)
        PT = self.ring("l2_probT", 1, [P, T], F32, scope)
        AO = self.split_ring("l2_ao", 1, [T], scope)
        MX = self.ring("l2_mx", 2, [P, 4, GB], F32, scope)
        pb = sb("l2_pb", [P, B, H2])
        pbT = self.ring("l2_pbT", 1, [H2, GB, S], F32, scope)
        BW = sb("l2_bw", [H2, D])
        dv = sb("l2_dv", [P, H2])
        dsel = sb("l2_dsel", [P, H2, H2])
        nb = {"stats": self.ring("st2_", 1, [P, GB, 6], F32, scope), "mv": self.ring("mv2_", 1, [P, GB, 2], F32, scope),
              "rstd": self.ring("rs2_", 1, [P, 5, GB], F32, scope)}
        self.share_banks(scores=(0, 1), tr=(2, 3), acc=(4, 5), misc=(6, 7))
        proj = self.misc
        scale = float(K2) ** -0.5
        cols = {}
        for i in ("1", "2"):
            for n in (f"ln{i}_scale", f"ln{i}_offset", f"bq{i}", f"bk{i}", f"bv{i}", f"bias_k{i}", f"bias_v{i}"):
                cols[n] = self.cols("L2_xattn_" + n)
            cols["bo" + i], cols_done = self.load_bcast("l2_bias", "l2_bo" + i, a["L2_xattn_bo" + i], scope)

        wslots = {}

        def load_weights(at, hg):
            n = str(at + 1)
            wslots[at, hg] = got = {}
            for k in ("wv", "wk", "wq", "wo"):
                w, s = W[k].take(), (yield from acquire(staging))
                if k == "wo":
                    src = a["L2_xattn_wo" + n][hg * HG * K2:(hg + 1) * HG * K2, :].rearrange("(c p) n -> p c n", p=P)
                    st = s.t[:].rearrange("p (c n) -> p c n", c=HG)
                else:
                    src = a[f"L2_xattn_{k}{n}"].rearrange("(c p) n -> p c n", p=P)[:, :, hg * HG * K2:(hg + 1) * HG * K2]
                    st = s.t[:].rearrange("p (c n) -> p c n", c=DC)
                ld = self.load(f"l2_staging{staging.slots.index(s)}", st, src, s.free)
                half = st.shape[1] // 2
                for c in (slice(0, half), slice(half, 2 * half)):
                    yield
                    done = self.split_on(p.pool, "l2_weights", w.t[:, 0, c], w.t[:, 1, c], st[:, c], [ld, *w.free])
                s.free = [done]
                got[k] = (w, done)

        def normalise(at, g):
            n = str(at + 1)
            bufs = dict(nb, xn=staging, ntmp=staging)

            def add_bias(read):
                self.x_done[g] = self.add_bias_rows(g, cols["bo" + n], [read, cols_done])
            hT_done[at, g] = yield from self.norm_transposed(
                g, lambda b: self.x_tok[:, g * GB + b, :], self.x_done[g], cols["ln" + n + "_scale"],
                cols["ln" + n + "_offset"], False, 1e-5, hT[g], bufs, add_bias)

        hT_done = {}
        weights_ahead, norms_ahead = [], []

        def advance(chains, n):
            for _ in range(n):
                while chains and next(chains[0], run) is run:
                    chains.pop(0)
        items = [(at, hg, g, h) for at in range(2) for hg in range(H2 // HG) for g in range(G) for h in range(HG)]
        N = len(items)
        st = [dict() for _ in items]
        vslot = {}
        acc_now = {}
        bw_done = {}

        def bias_rows(at, hg):
            n = str(at + 1)
            w, wd = wslots[at, hg]["wo"]
            if hg == 0:
                d = p.dve.do("l2_dv", lambda e: e.tensor_tensor(dv[:], cols["bias_v" + n], cols["bv" + n], ALU.subtract),
                             [cols_done])
                z = p.dve.do("l2_dv", lambda e: e.memset(dsel[:], 0.0), bw_free["dsel"])
                for h in range(H2):
                    d = p.dve.do("l2_dv", lambda e, h=h: e.tensor_copy(dsel[:, h, h:h + 1], dv[:, h:h + 1]), [d, z])
                bw_free["dv"] = d
            bk = self.misc.take()

            def mm(e):
                for i in range(HG):
                    for s in (0, 1):
                        ins = e.matmul(bk.t[0:H2, 0:D], dsel[:, hg * HG + i, :], f32(w.t[:, s, i, :]),
                                       start=i == 0 and s == 0, stop=i == HG - 1 and s == 1)
                return ins
            m = p.pe.do("l2_bw", mm, [wd, bw_free["dv"], *bk.free])
            bw_free["dsel"] = [m]
            if hg == 0:
                b = p.dve.do("l2_bw", lambda e: e.tensor_copy(BW[:], bk.t[0:H2, 0:D]), [m, *bw_free["bw"]])
            else:
                b = p.dve.do("l2_bw", lambda e: e.tensor_tensor(BW[:], BW[:], bk.t[0:H2, 0:D], ALU.add), [m, bw_done[at]])
            bk.free = [b]
            bw_done[at] = b
        bw_free = {"dsel": list(self.fence), "bw": list(self.fence)}

        def project(n, what):
            if what == "v":
                tgt, b = n - n % HG + HG, n % HG
                if tgt >= N:
                    return
                at, hg, g, _ = items[tgt]
                if b == 0:
                    vslot[tgt] = [V.take(), None]
                v = vslot[tgt][0]
                while "wv" not in wslots[at, hg]:
                    advance(weights_ahead, 1)
                w, wd = wslots[at, hg]["wv"]
                bk = proj.take()

                def mm(e):
                    for c in range(DC):
                        t0 = g * T + b * S
                        i = matmul_split(e, bk.t, [self.ctxT[:, s, c, t0:t0 + S] for s in (0, 1)],
                                         [w.t[:, s, c, :] for s in (0, 1)], c == 0, c == DC - 1)
                    return i
                m = p.pe.do("l2_v", mm, [wd, *bk.free])
                ev = p.dve.do("l2_v", lambda e: e.tensor_copy(v.t[:, b, :], bk.t), [m, *v.free])
                bk.free = [ev]
                vslot[tgt][1] = ev
                if b == GB - 1 and g == G - 1:
                    w.free = [m]
                return
            at, hg, g, h = items[n]
            nm = str(at + 1)
            while len(wslots[at, hg]) < 4:
                advance(weights_ahead, 1)
            while (at, g) not in hT_done:
                advance(norms_ahead, 1)
            if what == "q":
                w, wd = wslots[at, hg]["wq"]
                bk, q = proj.take(), QT.take()

                def mm(e):
                    for c in range(DC):
                        i = matmul_split(e, bk.t, [w.t[:, s, c, h * K2:(h + 1) * K2] for s in (0, 1)],
                                         [hT[g].t[:, s, c, :] for s in (0, 1)], c == 0, c == DC - 1)
                    return i
                m = p.pe.do("l2_q", mm, [wd, hT_done[at, g], *bk.free])
                hd = hg * HG + h
                st[n]["q_done"] = p.act.do("l2_q", lambda e: e.activation(
                    q.t[:], bk.t, ACT.Identity, bias=cols["bq" + nm][:, hd:hd + 1]), [m, *q.free])
                bk.free = [st[n]["q_done"]]
                st[n]["q"] = q
                if hg == H2 // HG - 1 and h == HG - 1:
                    hT[g].free = [m]
            else:
                w, wd = wslots[at, hg]["wk"]
                bk, k = proj.take(), KT.take()

                def mm(e):
                    for c in range(DC):
                        i = matmul_split(e, bk.t, [w.t[:, s, c, h * K2:(h + 1) * K2] for s in (0, 1)],
                                         [self.ctxT[:, s, c, g * T:(g + 1) * T] for s in (0, 1)], c == 0, c == DC - 1)
                    return i
                m = p.pe.do("l2_k", mm, [wd, *bk.free])
                hd = hg * HG + h
                st[n]["k_done"] = p.act.do("l2_k", lambda e: e.activation(
                    k.t[:, :, 0:S], bk.t.rearrange("p (b t) -> p b t", b=GB), ACT.Identity,
                    bias=cols["bk" + nm][:, hd:hd + 1]), [m, *k.free])
                bk.free = [st[n]["k_done"]]
                st[n]["bk_done"] = p.pool.do("l2_bias_k", lambda e: e.tensor_copy(
                    k.t[:, :, S:S + 2], cols["bias_k" + nm][:, hd:hd + 1].unsqueeze(2).to_broadcast([P, GB, 2])), k.free)
                st[n]["k"] = k
            if h == HG - 1 and g == G - 1:
                w.free = [m]

        def scores(n):
            s = st[n]
            q, k = s["q"], s["k"]
            banks = [self.scores.take() for _ in range(2)]
            pr, mx = PR.take(), MX.take()
            for i, bk in enumerate(banks):
                def mm(e, i=i, bk=bk):
                    for b in (2 * i, 2 * i + 1):
                        ins = e.matmul(bk.t[:, (b % 2) * (S + 2):(b % 2 + 1) * (S + 2)], q.t[:, b * S:(b + 1) * S],
                                       k.t[:, b, :], start=True, stop=True)
                    return ins
                m = p.pe.do("l2_scores", mm, [s["q_done"], s["k_done"], s["bk_done"], *bk.free])
                r = p.dve.do("l2_max", lambda e, i=i, bk=bk: e.tensor_reduce(
                    mx.t[:, 0, 2 * i:2 * i + 2], bk.t[:, 0:2 * (S + 2)].rearrange("p (b t) -> p b t", b=2)[:, :, 0:S + 1],
                    AX.X, ALU.max), [m, *mx.free])
            q.free = k.free = [m]
            r = p.dve.do("l2_max", lambda e: e.tensor_scalar(mx.t[:, 1, :], mx.t[:, 0, :], -scale, None, ALU.mult), [r])
            for b in range(GB):
                ex = p.act.do("l2_exp", lambda e, b=b: e.activation(
                    pr.t[:, b, 0:S + 1], banks[b // 2].t[:, (b % 2) * (S + 2):(b % 2) * (S + 2) + S + 1], ACT.Exp,
                    bias=mx.t[:, 1, b:b + 1], scale=scale, accum_out=mx.t[:, 2, b:b + 1]), [r, *pr.free])
                banks[b // 2].free = [ex]
            s.update(prob=pr, exp=ex, mx=mx)

        def normalise_rows(n):
            s = st[n]
            pr, mx = s["prob"], s["mx"]
            rc = p.dve.do("l2_recip", lambda e: e.reciprocal(mx.t[:, 3, :], mx.t[:, 2, :]), [s["exp"]])
            nm = p.pool.do("l2_norm", lambda e: e.tensor_tensor(
                pr.t[:, :, 0:S + 1], pr.t[:, :, 0:S + 1], mx.t[:, 3, :].unsqueeze(2).to_broadcast([P, GB, S + 1]), ALU.mult),
                [rc])
            at, hg, g, h = items[n]
            hd = hg * HG + h
            pbc = p.pool.do("l2_pb", lambda e: e.tensor_copy(
                pb[:, g * GB:(g + 1) * GB, hd:hd + 1], pr.t[:, :, S:S + 1]), [nm, *pb_free[g]])
            mx.free = [nm]
            s.update(prob_done=nm, pb_done=pbc)
        pb_free = [list(self.fence) for _ in range(G)]

        def transposes(n):
            s = st[n]
            bk, pt, pr = tr_ring.take(), PT.take(), s["prob"]

            def tr(e):
                for b in range(GB):
                    i = e.transpose(bk.t[:, b * S:(b + 1) * S], pr.t[:, b, 0:S], self.ident[:])
                return i
            t = p.pe.do("l2_tr", tr, [s["prob_done"], *bk.free])
            pr.free = [t, s["pb_done"]]
            ev = p.dve.do("l2_probT", lambda e: e.tensor_copy(pt.t[:], bk.t), [t, *pt.free])
            bk.free = [ev]
            s.update(probT=pt, probT_done=ev)
        tr_ring, pv_ring = Ring(self.tr.slots[0:1]), Ring(self.tr.slots[1:2])

        def values(n):
            at, hg, g, h = items[n]
            s = st[n]
            bk, ao, pt = pv_ring.take(), AO.take(), s["probT"]
            v, vd = vslot[n - h]

            def mm(e):
                for b in range(GB):
                    i = e.matmul(bk.t[:, b * S:(b + 1) * S], v.t[:, b, h * K2:(h + 1) * K2], pt.t[:, b * S:(b + 1) * S],
                                 start=True, stop=True)
                return i
            m = p.pe.do("l2_values", mm, [s["probT_done"], vd, *bk.free])
            pt.free = [m]
            if h == HG - 1:
                v.free = [m]
            hd = hg * HG + h
            done = self.split_psum_bias("l2_ao", ao.t[:, 0, :], ao.t[:, 1, :], bk.t, cols["bv" + str(at + 1)][:, hd:hd + 1],
                                        [m, *ao.free])
            bk.free = [done]
            s.update(ao=ao, ao_done=done)

        def output(n):
            at, hg, g, h = items[n]
            s = st[n]
            ao = s["ao"]
            w, wd = wslots[at, hg]["wo"]
            if h == 0:
                acc_now[0] = [self.acc.take() for _ in range(2)]
                if g == 0:
                    bias_rows(at, hg)
            banks = acc_now[0]
            last = hg == H2 // HG - 1
            if last and h == HG - 1:
                bk, pt = self.misc.take(), pbT.take()

                def tr(e):
                    for b in range(GB):
                        i = e.transpose(bk.t[0:H2, b * S:(b + 1) * S], pb[:, g * GB + b, :], self.ident[:])
                    return i
                t = p.pe.do("l2_pbT", tr, [s["pb_done"], *bk.free])
                pb_free[g] = [t]
                ev = p.act.do("l2_pbT", lambda e: e.activation(
                    pt.t[:].rearrange("h b t -> h (b t)"), bk.t[0:H2, :], ACT.Copy), [t, *pt.free])
                bk.free = [ev]

            def mm(e):
                for b in range(GB):
                    i = matmul_split(e, banks[b // 2].t[:, (b % 2) * D:(b % 2 + 1) * D],
                                     [ao.t[:, x, b * S:(b + 1) * S] for x in (0, 1)], [w.t[:, x, h, :] for x in (0, 1)],
                                     h == 0 and b % 2 == 0, h == HG - 1 and not last, check=False)
                return i
            m = p.pe.do("l2_out", mm, [s["ao_done"], wd, *banks[0].free, *banks[1].free])
            ao.free = [m]
            if g == G - 1 and h == HG - 1:
                w.free = [m]
            if last and h == HG - 1:
                def mm(e):
                    for b in range(GB):
                        i = e.matmul(banks[b // 2].t[:, (b % 2) * D:(b % 2 + 1) * D], pt.t[:, b, :], BW[:],
                                     start=False, stop=True, skip_group_check=True)
                    return i
                m = p.pe.do("l2_out_bias", mm, [ev, bw_done[at]])
                pt.free = [m]
                bw_free["bw"] = [m]
            if h == HG - 1:
                self.x_done[g] = self.add_to_x(g, banks, [m, m], [self.x_done[g]])
                if last and at == 0:
                    norms_ahead.append(normalise(1, g))
            nxt = (at, hg + 1) if not last else (at + 1, 0)
            if g == 1 and h == 0 and nxt[0] < 2 and nxt not in wslots:
                wslots[nxt] = {}
                weights_ahead.append(load_weights(*nxt))
            st[n] = None

        interleave(load_weights(0, 0), normalise(0, 0), 1.5)
        norms_ahead += [normalise(0, g) for g in range(1, G)]
        for n in range(-HG, -2):
            project(n, "v")
        for step in range(N + 3):
            if 1 <= step <= N:
                scores(step - 1)
            if step < N:
                project(step, "q")
            if 1 <= step <= N:
                normalise_rows(step - 1)
            if 2 <= step <= N + 1:
                values(step - 2)
            advance(weights_ahead, 1)
            advance(norms_ahead, 4 if step < 12 else 2)
            if step < N:
                project(step, "k")
            project(step - 2, "v")
            if 2 <= step <= N + 1:
                output(step - 2)
            if 1 <= step <= N:
                transposes(step - 1)

    def phase_l2_mlp(self, scope):
        self.phase = "l2m_"
        p, a = self.p, self.a
        self.stage_cols = 1024
        self.staging = self.ring("staging_m", 2, [P, self.stage_cols], F32, scope)
        cols = {n: self.cols("L2_xattn_" + n)
                for n in ("ln_mlp_scale", "ln_mlp_offset", "b_fc1")}
        b2, cd = self.load_bcast("l2m_bias", "l2m_b2", a["L2_xattn_b_fc2"], scope)
        w1, w1_done = run(self.load_weight("l2_w1", a["L2_xattn_w_fc1"], scope, p.pool))
        nb, mb = self.norm_bufs(scope), self.mlp_bufs(scope)
        hT = self.split_ring("l2m_hT", 2, [DC, T], scope)
        self.share_banks(tr=(2, 3), side=(4, 5, 0, 1), misc=(6, 7))
        ready = {}

        def norm(g):
            def add_bias(read):
                self.x_done[g] = self.add_bias_rows(g, b2, [read, cd])
            hs = yield from acquire(hT)
            ready[g] = (hs, (yield from self.norm_transposed(
                g, lambda b: self.x_tok[:, g * GB + b, :], self.x_done[g], cols["ln_mlp_scale"],
                cols["ln_mlp_offset"], False, 1e-5, hs, nb, add_bias)))

        def mlp(g):
            banks, m = yield from self.mlp(*ready[g], w1, w1_done, cols["b_fc1"], w2, w2_done, ACT.Gelu, mb)
            self.x_done[g] = self.add_to_x(g, banks, [m, m], [self.x_done[g]])
        run(norm(0))
        w2, w2_done = run(self.load_weight("l2_w2", a["L2_xattn_w_fc2"], scope, p.dve))
        for g in range(G):
            interleave(mlp(g), norm(g + 1) if g + 1 < G else iter(()), 0.5)

    def phase_l3(self, scope):
        self.phase = "l3_"
        p, a = self.p, self.a
        sb = lambda n, s, dt=F32: self.sb(n, s, dt, scope)
        self.stage_cols = 1024
        self.share_banks(scores=(0, 1), tr=(2, 3), acc=(4, 5), side=(6, 7))
        cols = {n: self.cols("L3_xattn_" + n)
                for n in ("ln1_s", "ln1_b", "ln2_s", "ln2_b", "ln3_s", "ln3_b", "b_qkv", "b_q", "b_kv", "b1")}
        rows = {n: self.load_bcast("l3_bias", "l3_" + n, a["L3_xattn_" + n], scope)[0] for n in ("b_ao", "b_co", "b2")}
        mask1 = sb("mask1", [P, 2, S])
        cd = self.load("l3_bias", mask1[:, 0, :], a["mask_1x1xSxS2_fc1"][0, 0], self.fence)
        MS = self.ring("mask2_", 2, [P, 2, GB, S], F32, scope)
        nb, mb, ab = self.norm_bufs(scope), self.mlp_bufs(scope), self.narrow_bufs(scope, 1, L3_STEPS[1] + 1, L3_STEPS[2] - L3_STEPS[1] + 1)
        self.staging = self.work
        wide = self.split_ring("l3_wide", 2, [DC, T], scope)
        qT = self.ring("l3_qT", 1, [P, DC, GB, S], F32, scope)
        kT = self.ring("l3_kT", 2, [P, DC, GB, 1, S], F32, scope)
        vv = self.ring("l3_v", 1, [P, GB, D], F32, scope)
        W = {}

        def weights(names, q):
            for n in names:
                W[n] = yield from self.load_weight("l3_" + n, a["L3_xattn_" + n], scope, q)
        run(weights(["w_qkv"], p.pool))
        m1 = p.dve.do("mask_prep", lambda e: e.tensor_scalar(
            mask1[:, 1, :], mask1[:, 0, :], -1.0, 40000.0, ALU.add, ALU.mult), [cd])
        scale = float(DH) ** -0.5
        begun, after = {}, {}
        tokens = lambda g: (lambda b: self.x_tok[:, g * GB + b, :])
        ctx_of = lambda g: self.ctxT[:, :, :, g * T:(g + 1) * T]

        def normalised(g, i, bias):
            def add_bias(read):
                self.x_done[g] = self.add_bias_rows(g, rows[bias], [read, cd])
            hs = yield from acquire(wide)
            return hs, (yield from self.norm_transposed(
                g, tokens(g), self.x_done[g], cols[f"ln{i}_s"], cols[f"ln{i}_b"], False, 1e-5, hs, nb, add_bias))

        def begin(g):
            hs, hd = yield from normalised(g, 1, "b_ao")
            k = yield from acquire(kT)
            _, kd = yield from self.project_cols("l3_k", *W["w_qkv"], D, hs.t, hd, cols["b_qkv"][:, 2:4],
                                                 lambda j: k.t[:, j, :, 0, :], k.free)
            q = yield from acquire(qT)
            _, qd = yield from self.project_cols("l3_q", *W["w_qkv"], 0, hs.t, hd, cols["b_qkv"][:, 0:2],
                                                 lambda j: q.t[:, j], q.free)
            qm = yield from self.mask_queries(0, q, qd, ab)
            begun[g] = hs, hd, (q, qd, k, kd, qm)

        def attention1(g):
            hs, hd, qk = begun.pop(g)

            def project_v():
                v = yield from acquire(vv)
                m, vd = yield from self.project_rows("l3_v", *W["w_qkv"], 2 * D, hs.t, hd, v.t, v.free)
                hs.free = [m]
                return [(v, vd)]
            mask = {"mul": lambda b: mask1[:, 0, :], "add": lambda b: mask1[:, 1, :], "ready": m1}
            after[g] = yield from self.narrow_attention(g, *qk, project_v(), scale, ab, mask)

        def middle(g):
            ms = yield from acquire(MS)
            ml = self.load(f"mask2_{MS.slots.index(ms)}", ms.t[:, 0], a["mask_Bx1xSxS2_ff1"][g * GB:(g + 1) * GB, 0]
                           .rearrange("b s t -> s b t"), ms.free)
            banks, m = yield from self.out_projection(g, *W["w_ao"], *after.pop(g), wide, cols["b_qkv"][:, 4:6])
            self.x_done[g] = self.add_to_x(g, banks, [m, m], [self.x_done[g]])
            yield
            m2 = p.pool.do("mask_prep", lambda e: e.tensor_scalar(
                ms.t[:, 1], ms.t[:, 0], -1.0, 40000.0, ALU.add, ALU.mult), [ml])
            hs, hd = yield from normalised(g, 2, "b_co")
            k = yield from acquire(kT)
            _, kd = yield from self.project_cols("l3_k", *W["w_kv"], 0, ctx_of(g), self.ctxT_done[g], cols["b_kv"][:, 0:2],
                                                 lambda j: k.t[:, j, :, 0, :], k.free)
            q = yield from acquire(qT)
            m, qd = yield from self.project_cols("l3_q", *W["w_q"], 0, hs.t, hd, cols["b_q"], lambda j: q.t[:, j], q.free)
            hs.free = [m]
            qm = yield from self.mask_queries(0, q, qd, ab)
            begun[g] = ms, m2, (q, qd, k, kd, qm)

        def attention2(g):
            ms, m2, qk = begun.pop(g)

            def project_v():
                v = yield from acquire(vv)
                _, vd = yield from self.project_rows("l3_v", *W["w_kv"], D, ctx_of(g), self.ctxT_done[g], v.t, v.free)
                return [(v, vd)]
            mask = {"mul": lambda b: ms.t[:, 0, b, :], "add": lambda b: ms.t[:, 1, b, :], "ready": m2}
            after[g] = yield from self.narrow_attention(g, *qk, project_v(), scale, ab, mask)
            ms.free = [after[g][1]]

        def end(g):
            banks, m = yield from self.out_projection(g, *W["w_co"], *after.pop(g), wide, cols["b_kv"][:, 2:4])
            self.x_done[g] = self.add_to_x(g, banks, [m, m], [self.x_done[g]])
            yield
            hs, hd = yield from normalised(g, 3, "b2")
            banks, m = yield from self.mlp(hs, hd, *W["w1"], cols["b1"], *W["w2"], ACT.Gelu_apprx_tanh, mb)
            self.x_done[g] = self.add_to_x(g, banks, [m, m], [self.x_done[g]])

        run(begin(0))
        turns = [(attention1(0), weights(["w_ao", "w_q", "w_kv", "w_co", "w1", "w2"], p.dve), begin(1)),
                 (attention1(1), middle(0)), (attention2(0), middle(1)), (attention2(1), end(0), begin(2)),
                 (attention1(2), end(1), begin(3)), (attention1(3), middle(2)), (attention2(2), middle(3)),
                 (attention2(3), end(2))]
        for (main, *side), rate in zip(turns, L3_RATE):
            interleave(main, chain(*side), rate)
        run(end(3))


def xattn_stack_kernel(nc, args, out):
    with ExitStack() as ctx:
        Kernel(nc, ctx, args, out).build()


def kernel(**inputs):
    import numpy as np
    from concourse import bacc, mybir
    from concourse.bass_utils import run_bass_kernel_spmd

    arrays = {n: v for n, v in inputs.items() if not n.startswith("L0_xattn_W")}
    packed = dict(inputs)
    kv_b = inputs["L1_xattn_kv_b"].reshape(-1, 2)
    packed["L1_kv_b_k"], packed["L1_kv_b_v"] = kv_b[:, 0], kv_b[:, 1]
    arrays = {n: v for n, v in arrays.items() if n not in COLUMNS and n != "L1_xattn_kv_b"}
    arrays["columns"] = np.concatenate([np.reshape(packed[n], (-1, P)).T for n in COLUMNS], axis=1)
    arrays.update({f"L0_W{c}T": np.transpose(inputs[f"L0_xattn_W{c}"]) for c in "qkv"})
    nc = bacc.Bacc("TRN2", target_bir_lowering=False, num_devices=1)
    feed, args = {}, {}
    for name, v in arrays.items():
        v = np.ascontiguousarray(v)
        feed["in_" + name] = v
        args[name] = nc.dram_tensor("in_" + name, v.shape, mybir.dt.from_np(v.dtype), kind="ExternalInput").ap()
    out = nc.dram_tensor("out_0", inputs["x"].shape, mybir.dt.float32, kind="ExternalOutput").ap()
    xattn_stack_kernel(nc, args, out)
    r = run_bass_kernel_spmd(nc, [feed], core_ids=[0])
    return r.results[0]["out_0"]
```
